# Optimizing a Trainium2 kernel written in Bass

```python
import numpy as np
import jax
import jax.numpy as jnp

def _softmax(x, axis=-1):
    return jax.nn.softmax(x, axis=axis)

def _gelu(x):
    return jax.nn.gelu(x, approximate=True)

def _silu(x):
    return jax.nn.silu(x)

def _sigmoid(x):
    return jax.nn.sigmoid(x)

def _layernorm(x, axis=-1, eps=1e-05):
    m = jnp.mean(x, axis=axis, keepdims=True)
    v = jnp.var(x, axis=axis, keepdims=True)
    return (x - m) / jnp.sqrt(v + eps)

def _scatter_add(tgt, idx, src, axis=0):
    return tgt.at[idx].add(src)

def _segment_sum(src, seg, n):
    return jax.ops.segment_sum(src, seg, n)
kernel_name = 'mk_gnn_preln_d2_gnn_r8_f61d4e'

def setup_inputs(seed: int=0):
    np.random.seed(seed)
    _w = jnp.asarray

    def _rec_inputs():
        import jax
        import jax.numpy as jnp
        _gk = jax.random.key(seed)
        x = -0.000202 + 1 * jax.random.normal(jax.random.fold_in(_gk, 1), (12500, 64), jnp.float32)
        _s = jax.random.randint(jax.random.fold_in(_gk, 2), (100000,), 0, 12500, jnp.int32)
        _d = jax.random.randint(jax.random.fold_in(_gk, 3), (100000,), 0, 12500, jnp.int32)
        _loop = jnp.arange(12500, dtype=jnp.int32)
        src = jnp.concatenate([_s, _d, _loop])
        dst = jnp.concatenate([_d, _s, _loop])
        _o = jnp.argsort(dst, stable=True)
        src = src[_o]
        dst = dst[_o]
        edge_attr_64 = 0.000189758 + 1.00013 * jax.random.normal(jax.random.fold_in(_gk, 12), (212500, 64), jnp.float32)
        return (x, src, dst, edge_attr_64)
    x, src, dst, edge_attr_64 = _rec_inputs()

    def _L0_gnn_setup():
        import jax, jax.numpy as jnp
        import numpy as np
        N_NODES = 12500
        N_EDGES = 200000
        IN_CH = 64
        OUT_CH = 64
        key = jax.random.key(seed)
        ks = jax.random.split(key, 6)
        x = jax.random.normal(ks[0], (N_NODES, IN_CH), dtype=jnp.float32)
        edge_index = jax.random.randint(ks[1], (2, N_EDGES), 0, N_NODES, dtype=jnp.int64)
        W1 = jax.random.normal(ks[2], (2 * IN_CH, OUT_CH), dtype=jnp.float32) * (1.0 / np.sqrt(2 * IN_CH))
        b1 = jnp.zeros((OUT_CH,), dtype=jnp.float32)
        W2 = jax.random.normal(ks[3], (OUT_CH, OUT_CH), dtype=jnp.float32) * (1.0 / np.sqrt(OUT_CH))
        b2 = jnp.zeros((OUT_CH,), dtype=jnp.float32)
        return {'x': x, 'edge_index': edge_index, 'W1': W1, 'b1': b1, 'W2': W2, 'b2': b2}
    _L0_gnn_all = _L0_gnn_setup()
    _L0_gnn_in = {k: v for k, v in _L0_gnn_all.items() if k in ('W1', 'b1', 'W2', 'b2')}
    del _L0_gnn_all

    def _L1_gnn_setup():
        import jax, jax.numpy as jnp
        import numpy as np
        EPS = 1e-05

        def _bn(h, gamma, beta):
            mu = h.mean(axis=0)
            var = ((h - mu) ** 2).mean(axis=0)
            return (h - mu) * jax.lax.rsqrt(var + EPS) * gamma + beta

        def _mlp(h, W1, b1, g1, be1, W2, b2):
            h = h @ W1 + b1
            h = jax.nn.relu(_bn(h, g1, be1))
            return h @ W2 + b2
        key = jax.random.key(seed)
        ks = jax.random.split(key, 12)
        N, E = (6250, 100000)
        node_dim, edge_dim, hidden = (64, 64, 128)
        d_in1 = node_dim + edge_dim
        d_in2 = node_dim + hidden

        def lin(k, fi, fo):
            s = 1.0 / np.sqrt(fi)
            return jax.random.uniform(k, (fi, fo), jnp.float32, -s, s)
        inp = {'x': jax.random.normal(ks[0], (N, node_dim), jnp.float32), 'edge_index': jax.random.randint(ks[1], (2, E), 0, N, jnp.int32), 'edge_attr': jax.random.normal(ks[2], (E, edge_dim), jnp.float32), 'u': jax.random.normal(ks[3], (1, 16), jnp.float32), 'batch': jnp.zeros((N,), jnp.int32), 'W1a': lin(ks[4], d_in1, hidden), 'b1a': jnp.zeros((hidden,), jnp.float32), 'g1a': jnp.ones((hidden,), jnp.float32), 'be1a': jnp.zeros((hidden,), jnp.float32), 'W2a': lin(ks[5], hidden, hidden), 'b2a': jnp.zeros((hidden,), jnp.float32), 'W1b': lin(ks[6], d_in2, hidden), 'b1b': jnp.zeros((hidden,), jnp.float32), 'g1b': jnp.ones((hidden,), jnp.float32), 'be1b': jnp.zeros((hidden,), jnp.float32), 'W2b': lin(ks[7], hidden, node_dim), 'b2b': jnp.zeros((node_dim,), jnp.float32)}
        return inp
    _L1_gnn_all = _L1_gnn_setup()
    _L1_gnn_in = {k: v for k, v in _L1_gnn_all.items() if k in ('u', 'W1a', 'b1a', 'g1a', 'be1a', 'W2a', 'b2a', 'W1b', 'b1b', 'g1b', 'be1b', 'W2b', 'b2b')}
    del _L1_gnn_all
    return {'x': x, 'src': src, 'dst': dst, 'edge_attr_64': edge_attr_64, 'L0_gnn_W1': _L0_gnn_in['W1'], 'L0_gnn_b1': _L0_gnn_in['b1'], 'L0_gnn_W2': _L0_gnn_in['W2'], 'L0_gnn_b2': _L0_gnn_in['b2'], 'L1_gnn_u': _L1_gnn_in['u'], 'L1_gnn_W1a': _L1_gnn_in['W1a'], 'L1_gnn_b1a': _L1_gnn_in['b1a'], 'L1_gnn_g1a': _L1_gnn_in['g1a'], 'L1_gnn_be1a': _L1_gnn_in['be1a'], 'L1_gnn_W2a': _L1_gnn_in['W2a'], 'L1_gnn_b2a': _L1_gnn_in['b2a'], 'L1_gnn_W1b': _L1_gnn_in['W1b'], 'L1_gnn_b1b': _L1_gnn_in['b1b'], 'L1_gnn_g1b': _L1_gnn_in['g1b'], 'L1_gnn_be1b': _L1_gnn_in['be1b'], 'L1_gnn_W2b': _L1_gnn_in['W2b'], 'L1_gnn_b2b': _L1_gnn_in['b2b']}

def reference(x, src, dst, edge_attr_64, L0_gnn_W1, L0_gnn_b1, L0_gnn_W2, L0_gnn_b2, L1_gnn_u, L1_gnn_W1a, L1_gnn_b1a, L1_gnn_g1a, L1_gnn_be1a, L1_gnn_W2a, L1_gnn_b2a, L1_gnn_W1b, L1_gnn_b1b, L1_gnn_g1b, L1_gnn_be1b, L1_gnn_W2b, L1_gnn_b2b):
    import jax
    import jax.numpy as jnp

    def _L0_gnn_ref(x, edge_index, W1, b1, W2, b2):
        import jax, jax.numpy as jnp
        import numpy as np
        N_NODES = 12500
        N_EDGES = 200000
        IN_CH = 64
        OUT_CH = 64
        src = edge_index[0]
        dst = edge_index[1]
        x_i = x[dst]
        x_j = x[src]
        edge_features = jnp.concatenate([x_i, x_j - x_i], axis=-1)
        h = jax.nn.relu(edge_features @ W1 + b1)
        edge_messages = h @ W2 + b2
        out = jax.ops.segment_max(edge_messages, dst, num_segments=x.shape[0])
        return jnp.where(jnp.isfinite(out), out, jnp.zeros_like(out))

    def _L1_gnn_ref(x, edge_index, edge_attr, u, batch, W1a, b1a, g1a, be1a, W2a, b2a, W1b, b1b, g1b, be1b, W2b, b2b):
        import jax, jax.numpy as jnp
        import numpy as np
        EPS = 1e-05

        def _bn(h, gamma, beta):
            mu = h.mean(axis=0)
            var = ((h - mu) ** 2).mean(axis=0)
            return (h - mu) * jax.lax.rsqrt(var + EPS) * gamma + beta

        def _mlp(h, W1, b1, g1, be1, W2, b2):
            h = h @ W1 + b1
            h = jax.nn.relu(_bn(h, g1, be1))
            return h @ W2 + b2
        row, col = (edge_index[0], edge_index[1])
        out = jnp.concatenate([x[row], edge_attr], axis=1)
        out = _mlp(out, W1a, b1a, g1a, be1a, W2a, b2a)
        out = jax.ops.segment_sum(out, col, num_segments=x.shape[0])
        out = jnp.concatenate([x, out], axis=1)
        return _mlp(out, W1b, b1b, g1b, be1b, W2b, b2b)
    edge_index = jnp.stack([src, dst])
    batch0 = jnp.zeros((12500,), jnp.int32)
    h = jnp.maximum(_layernorm(x, axis=-1), 0.0)
    x = x + _L0_gnn_ref(h, edge_index, L0_gnn_W1, L0_gnn_b1, L0_gnn_W2, L0_gnn_b2)
    h = jnp.maximum(_layernorm(x, axis=-1), 0.0)
    x = x + _L1_gnn_ref(h, edge_index, edge_attr_64, L1_gnn_u, batch0, L1_gnn_W1a, L1_gnn_b1a, L1_gnn_g1a, L1_gnn_be1a, L1_gnn_W2a, L1_gnn_b2a, L1_gnn_W1b, L1_gnn_b1b, L1_gnn_g1b, L1_gnn_be1b, L1_gnn_W2b, L1_gnn_b2b)
    return x

_drawn_inputs = setup_inputs


def setup_inputs(seed=0):
    import zlib

    import numpy as np

    out = dict(_drawn_inputs(seed))
    spreads = {'L0_gnn_b1': (0.0, 0.1),
     'L0_gnn_b2': (0.0, 0.1),
     'L1_gnn_b1a': (0.0, 0.8),
     'L1_gnn_g1a': (1.0, 0.2),
     'L1_gnn_be1a': (0.0, 0.288),
     'L1_gnn_b2a': (0.0, 0.1),
     'L1_gnn_b1b': (0.0, 0.8),
     'L1_gnn_g1b': (1.0, 0.2),
     'L1_gnn_be1b': (0.0, 0.1),
     'L1_gnn_b2b': (0.0, 0.1)}
    factors = {}
    for name, (base, spread) in spreads.items():
        noise = np.random.default_rng([zlib.crc32(name.encode()), seed]).standard_normal(out[name].shape)
        drawn = base * np.exp(spread * noise) if base else spread * noise
        out[name] = jnp.asarray(drawn.astype(out[name].dtype))
    for name, factor in factors.items():
        out[name] = (out[name] * factor).astype(out[name].dtype)
    return out
```

```python
from contextlib import ExitStack

import concourse.bass as bass
from concourse import mybir

P = 128
ALU = mybir.AluOpType
ACT = mybir.ActivationFunctionType
AX = mybir.AxisListType
F32 = mybir.dt.float32
BF16 = mybir.dt.bfloat16
I32 = mybir.dt.int32

BIG = 1.0e38
EPS = 1e-5


def at_least(eng, semaphore, value):
    if isinstance(value, int) and value <= 0:
        return
    eng.wait_ge(semaphore, value)


def at_least_apart(eng, semaphore, value, passed):
    at_least(eng, semaphore, value)
    if not isinstance(value, int):
        eng.sem_inc(passed, 1)


class Chain:

    def __init__(self, eng, semaphore, per_step=0):
        self.eng, self.semaphore, self.per_step = eng, semaphore, per_step
        self.base, self.n = 0, 0

    def start(self, step):
        self.base, self.n = step * self.per_step, 0

    def inc(self, ins):
        self.n += 1
        ins.then_inc(self.semaphore, 1)

    def wait(self):
        at_least(self.eng, self.semaphore, self.base + self.n)

    def link(self, ins):
        self.inc(ins)
        self.wait()

    def end(self):
        assert self.n == self.per_step


def pipeline(eng, steps, unroll, stages):
    rounds = steps // unroll
    assert rounds * unroll == steps and rounds >= 2
    last = max(lag for lag, _ in stages)
    assert last <= unroll

    def peeled(step):
        for lag, stage in stages:
            if 0 <= step - lag < steps:
                stage((step - lag) // unroll, (step - lag) % unroll)

    for step in range(unroll):
        peeled(step)
    if rounds > 2:
        with eng.Fori(1, rounds - 1) as r:
            for slot in range(unroll):
                for lag, stage in stages:
                    back = (slot - lag) // unroll
                    stage(r + back if back else r, (slot - lag) % unroll)
    for step in range(steps - unroll, steps + last):
        peeled(step)


def gnn_kernel(nc, x, src, dst, edge_attr, W1, b1, W2, b2, W1a, b1a, g1a, be1a, W2a, b2a,
               W1b, b1b, g1b, be1b, W2b, b2b, out):
    N, C = x.shape
    E = src.shape[0]
    HID = W1a.shape[1]
    assert C == 64 and HID == 128
    J = 4
    BLK = P * J
    CO = 2048
    NCO = -(-E // CO)
    EP = NCO * CO
    NBLK = EP // BLK
    HB = NBLK // 2
    MID = HB * BLK
    FINE = 32
    NI = 100
    NODE_P = N // NI
    NP = P * NI
    assert NODE_P * NI == N and NBLK % 8 == 0 and HB % 4 == 0
    FULL_CO = E // CO
    LAST_BLK = E // BLK
    TAIL = E - LAST_BLK * BLK
    assert LAST_BLK == NBLK - 1 and TAIL % J == 0 and TAIL > 0
    NB = 10
    NSTEP = NI // NB
    OUT_OF_RANGE = 1.0e6
    assert 3 * P < NBLK <= 4 * P

    def dram(name, shape, dt=F32):
        return nc.dram_tensor(name, shape, dt, kind="Internal").ap()

    fine_rows = dram("fine_rows", (EP // FINE, FINE))
    fine_first = dram("fine_first", (NCO, CO // FINE))
    same_max = dram("same_max", (EP,), BF16)
    same_sum = dram("same_sum", (EP,), BF16)
    starts = dram("starts", (NP + P,))
    recv_table = dram("recv_table", (NP, C))
    send_table = dram("send_table", (NP, C))
    recv_edges = dram("recv_edges", (EP, C))
    max_edges = dram("max_edges", (EP, C))
    norm_table = dram("norm_table", (NP, C))
    hid_edges = dram("hid_edges", (NBLK, P, BLK))
    sum_edges = dram("sum_edges", (EP, HID))

    stack = ExitStack()
    with stack:
        def tensor(scope, name, shape, dt=F32):
            return scope.enter_context(nc.sbuf_tensor(name, shape, dt))

        def banks(scope, name, shape, dt=F32):
            return scope.enter_context(nc.psum_tensor(name, shape, dt))

        def sem(name):
            phase_sems.append(nc.alloc_semaphore(name))
            return phase_sems[-1]

        phase_sems = []

        def end_phase():
            nc.clear_and_free_semaphores(list(phase_sems))
            phase_sems.clear()
            nc.all_engine_barrier()

        nodes = tensor(stack, "nodes", [P, NI, C])
        norm_deg = tensor(stack, "norm_deg", [P, NI, C + 1])
        src_cols = tensor(stack, "src_cols", [P, NBLK, J], I32)
        ident = tensor(stack, "ident", [P, P])
        end_idx = tensor(stack, "end_idx", [P, NI], I32)
        end_row = tensor(stack, "end_row", [P, NI], I32)
        has_edge = tensor(stack, "has_edge", [P, NI])
        spans_mid = tensor(stack, "spans_mid", [P, NI])
        mids = tensor(stack, "mids", [P, 2], I32)
        sel2 = tensor(stack, "sel2", [2, P], BF16)

        def norm_step(chain, k, stats, small, var_made, dev_made, made, result):
            dve = chain.eng
            chain.start(k)
            for i in range(NB):
                chain.inc(nc.vector.bn_stats(stats[:, i, :], nodes[:, bass.ds(k * NB + i, 1), :].rearrange("p a c -> p (a c)")))
            chain.wait()
            total, gap, var, dev, mean, inv, square, both = (small[:, q, :] for q in range(8))
            chain.inc(nc.vector.tensor_tensor(total, stats[:, :, 1], stats[:, :, 4], ALU.add))
            chain.inc(nc.vector.tensor_tensor(gap, stats[:, :, 1], stats[:, :, 4], ALU.subtract))
            chain.link(nc.vector.tensor_tensor(both, stats[:, :, 2], stats[:, :, 5], ALU.add))
            chain.inc(nc.vector.scalar_tensor_tensor(out=square, in0=gap, scalar=0.25, in1=gap, op0=ALU.mult, op1=ALU.mult))
            chain.link(nc.vector.tensor_scalar(both, both, 1.0 / C, EPS, ALU.mult, ALU.add))
            nc.vector.tensor_tensor(var, both, square, ALU.add).then_inc(var_made, 1)
            chain.inc(nc.vector.tensor_scalar(mean, total, 0.5, None, ALU.mult))
            at_least(dve, dev_made, k + 1)
            chain.link(nc.vector.reciprocal(inv, dev))
            chain.end()
            for i in range(NB):
                nc.vector.tensor_scalar(result(i), nodes[:, bass.ds(k * NB + i, 1), :].rearrange("p a c -> p (a c)"),
                                        mean[:, i:i + 1], inv[:, i:i + 1], ALU.subtract, ALU.mult).then_inc(made, 1)

        NORM_LINKS = NB + 7

        def affine_of_norm(chain, root_ready, root_made, stats, sums, gain, shift, g, be):
            chain.link(nc.vector.bn_aggr(sums[:, 0:2], stats))
            nc.vector.tensor_scalar(sums[:, 2:3], sums[:, 1:2], EPS, None, ALU.add).then_inc(root_ready, 1)
            chain.eng.wait_ge(root_made, 1)
            chain.link(nc.vector.reciprocal(sums[:, 4:5], sums[:, 3:4]))
            chain.link(nc.vector.tensor_tensor(gain, g, sums[:, 4:5], ALU.mult))
            chain.link(nc.vector.tensor_tensor(sums[:, 5:6], sums[:, 0:1], gain, ALU.mult))
            chain.link(nc.vector.tensor_tensor(shift, be, sums[:, 5:6], ALU.subtract))

        with ExitStack() as s1:
            edge_dst = tensor(s1, "edge_dst", [NCO, CO], I32)
            edge_dst_f = tensor(s1, "edge_dst_f", [NCO, CO])
            prev_last = tensor(s1, "prev_last", [NCO, 1], I32)
            prev_last_f = tensor(s1, "prev_last_f", [NCO, 1])
            m01 = tensor(s1, "m01", [NCO, CO], BF16)
            mbig = tensor(s1, "mbig", [NCO, CO], BF16)
            firsts = tensor(s1, "firsts", [NCO, CO // FINE])
            co_row = tensor(s1, "co_row", [1, NCO])
            co_all = tensor(s1, "co_all", [P, NCO])
            ones_row = tensor(s1, "ones_row", [1, P])
            node_i = tensor(s1, "node_i", [P, NI], I32)
            node_f = tensor(s1, "node_f", [P, NI])
            src_rows = tensor(s1, "src_rows", [P, 4, BLK], I32)
            src_rows_f = tensor(s1, "src_rows_f", [P, 4, BLK])
            floor_tile = tensor(s1, "floor_tile", [P, CO])
            cmp = tensor(s1, "cmp", [P, NB, NCO])
            count = tensor(s1, "count", [P, 2, NB])
            inner = tensor(s1, "inner", [P, NB])
            coarse_f = tensor(s1, "coarse_f", [P, NI])
            idx_b = tensor(s1, "idx_b", [P, 2, NB], I32)
            idx_c = tensor(s1, "idx_c", [P, 2, NB], I32)
            rows_b = tensor(s1, "rows_b", [P, 2, NB, CO // FINE])
            rows_c = tensor(s1, "rows_c", [P, 2, NB, FINE])
            fine_f = tensor(s1, "fine_f", [P, NI])
            start_f = tensor(s1, "start_f", [P, NI])
            start2 = tensor(s1, "start2", [P, NI + 1])
            degree, skip, last_edge, spans = (tensor(s1, n, [P, NI]) for n in ("degree", "skip", "last_edge", "spans"))
            second = tensor(s1, "second", [P, NI])
            mids_f = tensor(s1, "mids_f", [P, 2])
            start_idx = tensor(s1, "start_idx", [P, NI], I32)
            mid_row = tensor(s1, "mid_row", [P, C])
            e_const = tensor(s1, "e_const", [1, P])
            w_ab = tensor(s1, "w_ab", [P, 2 * C])
            b1_all = tensor(s1, "b1_all", [P, C])
            recv_sb = tensor(s1, "recv_sb", [P, NI, C])
            send_sb = tensor(s1, "send_sb", [P, NI, C])
            stats = tensor(s1, "stats", [P, NB, 6])
            small = tensor(s1, "small", [P, 8, NB])
            normed = tensor(s1, "normed", [P, 2, NB, C])
            normed_t = tensor(s1, "normed_t", [P, 2, NB // 2, P])
            ps_t = banks(s1, "ps_t", [P, 8, P])
            ps_ab = banks(s1, "ps_ab", [P, 2, 8, P])
            ps_src = banks(s1, "ps_src", [P, J, P])
            ps_co = banks(s1, "ps_co", [P, 512])

            consts = sem("consts")
            cleared = sem("cleared")
            dst_in, src_in, x_in, w_in, mid_in = (sem(n) for n in ("dst_in", "src_in", "x_in", "w_in", "mid_in"))
            masks_made, masks_out = sem("masks_made"), sem("masks_out")
            dst_f_made, fine_out = sem("dst_f_made"), sem("fine_out")
            co_turned, co_copied, co_spread, co_ready = (sem(n) for n in ("co_turned", "co_copied", "co_spread", "co_ready"))
            src_f_made, src_turned, src_made = (sem(n) for n in ("src_f_made", "src_turned", "src_made"))
            coarse_done, rows_b_in, fine_done, rows_c_in = (sem("coarse_done"), [sem(f"rows_b_in{i}") for i in range(2)],
                                                            sem("fine_done"), [sem(f"rows_c_in{i}") for i in range(2)])
            start_made = sem("start_made")
            starts_out, starts_in = sem("starts_out"), sem("starts_in")
            floor_made, floor_out = sem("floor_made"), sem("floor_out")
            idx_made = sem("idx_made")
            scattered, mid_gathered, mid_out = sem("scattered"), sem("mid_gathered"), sem("mid_out")
            w_made = sem("w_made")
            var_made, dev_made, normed_made, normed_turned, normed_copied, ab_made = (
                sem(n) for n in ("var_made", "dev_made", "normed_made", "normed_turned", "normed_copied", "ab_made"))
            recv_made, send_made, tables_out = sem("recv_made"), sem("send_made"), sem("tables_out")

            pool_passed, dve_passed = sem("pool_passed1"), sem("dve_passed1")
            block = s1.enter_context(nc.Block())

            @block.sync
            def _(sp):
                dst_v = dst[0:FULL_CO * CO].rearrange("(p c) -> p c", c=CO)
                cut = FULL_CO // 16 * 16
                sp.wait_ge(cleared, 4)
                sp.dma_start(edge_dst[0:cut, :], dst_v[0:cut, :]).then_inc(dst_in, 16)
                sp.dma_start(edge_dst[cut:FULL_CO, :], dst_v[cut:FULL_CO, :]).then_inc(dst_in, 16)
                sp.dma_start(edge_dst[FULL_CO:NCO, 0:E - FULL_CO * CO],
                             dst[FULL_CO * CO:E].rearrange("(p c) -> p c", p=1)).then_inc(dst_in, 16)
                with nc.allow_non_contiguous_dma(reason="one element per coarse group"):
                    sp.dma_start(prev_last[1:NCO, :], dst_v[:, CO - 1:CO]).then_inc(dst_in, 16)
                sp.dma_start(mids[:, :], dst[MID - 1:MID + 1].partition_broadcast(P)).then_inc(mid_in, 16)
                for g in range(4):
                    rows = min(P, LAST_BLK - g * P)
                    sp.dma_start(src_rows[0:rows, g, :],
                                 src[g * P * BLK:(g * P + rows) * BLK].rearrange("(p c) -> p c", c=BLK)).then_inc(src_in, 16)
                sp.dma_start(src_rows[LAST_BLK - 3 * P:NBLK - 3 * P, 3, 0:TAIL],
                             src[LAST_BLK * BLK:E].rearrange("(p c) -> p c", p=1)).then_inc(src_in, 16)
                x_v = x.rearrange("(p i) c -> p i c", i=NI)
                sp.dma_start(nodes[0:112, :, :], x_v[0:112, :, :]).then_inc(x_in, 16)
                sp.dma_start(nodes[112:NODE_P, :, :], x_v[112:NODE_P, :, :]).then_inc(x_in, 16)
                for h in range(2):
                    sp.dma_start(w_ab[h * C:(h + 1) * C, 0:C], W1[0:C, :]).then_inc(w_in, 16)
                    sp.dma_start(w_ab[h * C:(h + 1) * C, C:2 * C], W1[C:2 * C, :]).then_inc(w_in, 16)
                sp.dma_start(b1_all[:, :], b1.partition_broadcast(P)).then_inc(w_in, 16)
                sp.wait_ge(floor_made, 1)
                piece = P * CO
                floor_v = recv_edges.rearrange("(n p r) c -> p n (r c)", p=P, r=CO // C)
                per = EP * C // piece // 4
                for q in range(4):
                    sp.dma_start(floor_v[:, q * per:(q + 1) * per, :],
                                 floor_tile[:, :].unsqueeze(1).broadcast_to([P, per, CO])).then_inc(floor_out, 16)
                sp.wait_ge(dst_f_made, 2)
                sp.dma_start(fine_rows.rearrange("(p g) f -> p (g f)", p=NCO), edge_dst_f[:, :]).then_inc(fine_out, 16)
                sp.dma_start(fine_first, firsts[:, :]).then_inc(fine_out, 16)
                sp.wait_ge(masks_made, 2)
                sp.dma_start(same_sum.rearrange("(p c) -> p c", c=CO), m01[:, :]).then_inc(masks_out, 16)
                sp.dma_start(same_max.rearrange("(p c) -> p c", c=CO), mbig[:, :]).then_inc(masks_out, 16)
                sp.wait_ge(recv_made, NSTEP)
                sp.dma_start(recv_table.rearrange("(p i) c -> p (i c)", i=NI), recv_sb[:, :, :].rearrange("p i c -> p (i c)")).then_inc(tables_out, 16)
                sp.wait_ge(send_made, NSTEP)
                sp.dma_start(send_table.rearrange("(p i) c -> p (i c)", i=NI), send_sb[:, :, :].rearrange("p i c -> p (i c)")).then_inc(tables_out, 16)
                sp.wait_ge(start_made, NSTEP + 1)
                sp.dma_start(starts[0:NP].rearrange("(p i) -> p i", i=NI), start_f[:, :]).then_inc(starts_out, 16)
                sp.dma_start(starts[NP:NP + P].rearrange("(p i) -> p i", p=1), e_const[:, :]).then_inc(starts_out, 16)
                sp.wait_ge(starts_out, 32)
                with nc.allow_non_contiguous_dma(reason="one element per partition"):
                    sp.dma_start(start2[:, NI:NI + 1], starts[NI:NI + NP].rearrange("(p i) -> p i", i=NI)[:, 0:1]).then_inc(starts_in, 16)
                sp.wait_ge(mid_gathered, 16)
                sp.wait_ge(scattered, 16 * NI)
                sp.dma_start(recv_edges[1:2, :], mid_row[0:1, :]).then_inc(mid_out, 16)
                sp.wait_ge(mid_out, 16)
                sp.wait_ge(masks_out, 32)
                sp.wait_ge(tables_out, 32)

            @block.gpsimd
            def _(pool):
                nc.gpsimd.memset(floor_tile[:, :], -BIG).then_inc(floor_made, 1)
                nc.gpsimd.memset(ident[:, :], 0.0).then_inc(consts, 1)
                nc.gpsimd.memset(sel2[:, :], 1.0).then_inc(consts, 1)
                nc.gpsimd.iota(node_i[:, :], [[1, NI]], base=0, channel_multiplier=NI).then_inc(consts, 1)
                pool.wait_ge(consts, 3)
                nc.gpsimd.affine_select(out=ident[:, :], in_=ident[:, :], compare_op=ALU.not_equal, fill=1.0, base=0,
                                        pattern=[[-1, P]], channel_multiplier=1).then_inc(consts, 1)
                nc.gpsimd.affine_select(out=sel2[:, :], in_=sel2[:, :], compare_op=ALU.is_ge, fill=0.0, base=0,
                                        pattern=[[1, P]], channel_multiplier=-C).then_inc(consts, 1)
                pool.wait_ge(consts, 5)
                nc.gpsimd.affine_select(out=sel2[:, :], in_=sel2[:, :], compare_op=ALU.is_ge, fill=0.0, base=C - 1,
                                        pattern=[[-1, P]], channel_multiplier=C).then_inc(consts, 1)
                pool.wait_ge(fine_out, 32)

                def fetch(table, width, ready, idx, rows, got):
                    def stage(r, s):
                        at_least_apart(pool, ready, r * 2 + s + 1, pool_passed)
                        for i in range(NB):
                            pool.indirect_dma_start(out=rows[:, s, i, :], out_offset=None, in_=table,
                                                    in_offset=bass.IndirectOffsetOnAxis(ap=idx[:, s, i:i + 1], axis=0)
                                                    ).then_inc(got[s], 16)
                    return stage

                pipeline(pool, NSTEP, 2, [
                    (0, fetch(fine_first, CO // FINE, coarse_done, idx_b, rows_b, rows_b_in)),
                    (1, fetch(fine_rows, FINE, fine_done, idx_c, rows_c, rows_c_in)),
                ])
                pool.wait_ge(idx_made, 1)
                pool.wait_ge(recv_made, NSTEP)
                pool.wait_ge(floor_out, 64)
                for i in range(NI):
                    pool.indirect_dma_start(out=recv_edges, out_offset=bass.IndirectOffsetOnAxis(ap=start_idx[:, i:i + 1], axis=0),
                                            in_=recv_sb[:, i, :], in_offset=None,
                                            bounds_check=EP - 1, oob_is_err=False).then_inc(scattered, 16)
                pool.wait_ge(tables_out, 32)
                pool.wait_ge(mid_in, 16)
                pool.indirect_dma_start(out=mid_row[:, :], out_offset=None, in_=recv_table,
                                        in_offset=bass.IndirectOffsetOnAxis(ap=mids[:, 1:2], axis=0)).then_inc(mid_gathered, 16)

            @block.tensor
            def _(pe):
                pe.wait_ge(consts, 4)
                pe.wait_ge(dst_f_made, 2)
                nc.tensor.transpose(ps_co[0:1, 0:NCO], firsts[:, 0:1], ident[0:NCO, 0:NCO]).then_inc(co_turned, 1)
                pe.wait_ge(co_copied, 2)
                nc.tensor.matmul(ps_co[:, 256:256 + NCO], ones_row[:, :], co_row[:, :], start=True, stop=True).then_inc(co_spread, 1)
                pe.wait_ge(w_made, 1)

                def turn(r, s):
                    k = r * 2 + s
                    at_least(pe, normed_made, NB * (k + 1))
                    at_least(pe, normed_copied, k)
                    for q in range(NB // 2):
                        mm = nc.tensor.transpose(ps_t[:, q, :], normed[:, s, 2 * q:2 * q + 2, :].rearrange("p a c -> p (a c)"), ident[:, :])
                    mm.then_inc(normed_turned, 1)

                def product(r, s):
                    k = r * 2 + s
                    at_least(pe, normed_copied, k + 1)
                    at_least(pe, recv_made, k)
                    at_least(pe, send_made, k)
                    for i in range(NB):
                        h = (i % 2) * C
                        mm = nc.tensor.matmul(ps_ab[:, i % 2, i // 2, :], normed_t[h:h + C, s, i // 2, :], w_ab[h:h + C, :], start=True, stop=True)
                    mm.then_inc(ab_made, 1)

                pipeline(pe, NSTEP, 2, [(0, turn), (1, product)])
                for g in range(4):
                    rows = min(P, NBLK - g * P)
                    pe.wait_ge(src_f_made, g + 1)
                    at_least(pe, src_made, g)
                    for j in range(J):
                        mm = nc.tensor.transpose(ps_src[:, j, 0:rows], src_rows_f[0:rows, g, j::J], ident[0:rows, 0:rows])
                    mm.then_inc(src_turned, 1)

            @block.scalar
            def _(act):
                def deviation(r, s):
                    at_least(act, var_made, r * 2 + s + 1)
                    nc.scalar.activation(small[:, 3, :], small[:, 2, :], ACT.Sqrt).then_inc(dev_made, 1)

                def copy_turned(r, s):
                    k = r * 2 + s
                    at_least(act, normed_turned, k + 1)
                    at_least(act, ab_made, k - 1)
                    nc.scalar.activation(normed_t[:, s, :, :], ps_t[:, 0:NB // 2, :], ACT.Relu).then_inc(normed_copied, 1)

                def copy_send(r, s):
                    at_least(act, ab_made, r * 2 + s + 1)
                    nc.scalar.copy(send_sb[:, bass.ds((r * 2 + s) * NB, NB), :].rearrange("p (q h) c -> p q h c", h=2),
                                   ps_ab[:, :, 0:NB // 2, C:2 * C].rearrange("p h q c -> p q h c")).then_inc(send_made, 1)

                pipeline(act, NSTEP, 2, [(0, deviation), (0, copy_turned), (1, copy_send)])

            @block.vector
            def _(dve):
                once = Chain(dve, sem("dve_once"))
                nc.vector.memset(prev_last[:, :], -1).then_inc(cleared, 1)
                nc.vector.memset(edge_dst[96:NCO, :], 1000000).then_inc(cleared, 1)
                nc.vector.memset(nodes[96:P, :, :], 0.0).then_inc(cleared, 1)
                nc.vector.memset(src_rows[:, 3, :], 0).then_inc(cleared, 1)
                nc.vector.memset(ones_row[:, :], 1.0).then_inc(co_copied, 1)
                nc.vector.memset(e_const[:, :], float(E)).then_inc(start_made, 1)
                dve.wait_ge(dst_in, 64)
                nc.vector.tensor_copy(edge_dst_f[:, :], edge_dst[:, :]).then_inc(dst_f_made, 1)
                dve.wait_ge(dst_f_made, 1)
                nc.vector.tensor_copy(firsts[:, :], edge_dst_f[:, ::FINE]).then_inc(dst_f_made, 1)
                once.inc(nc.vector.tensor_copy(prev_last_f[:, :], prev_last[:, :]))
                once.link(nc.vector.tensor_tensor(m01[:, 1:CO], edge_dst_f[:, 1:CO], edge_dst_f[:, 0:CO - 1], ALU.is_equal))
                nc.vector.tensor_tensor(m01[:, 0:1], edge_dst_f[:, 0:1], prev_last_f[:, :], ALU.is_equal).then_inc(masks_made, 1)
                dve.wait_ge(co_turned, 1)
                nc.vector.tensor_copy(co_row[:, :], ps_co[0:1, 0:NCO]).then_inc(co_copied, 1)
                dve.wait_ge(masks_made, 1)
                nc.vector.tensor_scalar(mbig[:, :], m01[:, :], 2 * BIG, -BIG, ALU.mult, ALU.add).then_inc(masks_made, 1)
                dve.wait_ge(co_spread, 1)
                once.inc(nc.vector.tensor_copy(co_all[:, :], ps_co[:, 256:256 + NCO]))
                dve.wait_ge(consts, 3)
                once.link(nc.vector.tensor_copy(node_f[:, :], node_i[:, :]))
                dve.wait_ge(w_in, 16 * 5)
                nc.vector.tensor_tensor(w_ab[:, 0:C], w_ab[:, 0:C], w_ab[:, C:2 * C], ALU.subtract).then_inc(w_made, 1)
                dve.wait_ge(x_in, 32)

                coarse_chain = Chain(dve, sem("coarse_chain"), 3)
                fine_chain = Chain(dve, sem("fine_chain"), 4)
                edge_chain = Chain(dve, sem("edge_chain"), 2)
                norm_chain = Chain(dve, sem("norm_chain"), NORM_LINKS)

                def count_smaller(chain, k, s, rows, width):
                    target = node_f[:, bass.ds(k * NB, NB)].unsqueeze(2).broadcast_to([P, NB, width])
                    chain.link(nc.vector.tensor_tensor(cmp[:, :, 0:width], rows, target, ALU.is_lt))
                    chain.link(nc.vector.tensor_reduce(count[:, s, :], cmp[:, :, 0:width], AX.X, ALU.add))

                def coarse(r, s):
                    k = r * 2 + s
                    coarse_chain.start(k)
                    count_smaller(coarse_chain, k, s, co_all[:, :].unsqueeze(1).broadcast_to([P, NB, NCO]), NCO)
                    keep = coarse_f[:, bass.ds(k * NB, NB)]
                    coarse_chain.link(nc.vector.tensor_scalar(keep, count[:, s, :], -1.0, 0.0, ALU.add, ALU.max))
                    coarse_chain.end()
                    at_least(dve, rows_b_in[s], 16 * NB * r)
                    nc.vector.tensor_scalar(idx_b[:, s, :], keep, 0.0, None, ALU.add).then_inc(coarse_done, 1)

                def fine(r, s):
                    k = r * 2 + s
                    at_least(dve, rows_b_in[s], 16 * NB * (r + 1))
                    fine_chain.start(k)
                    count_smaller(fine_chain, k, s, rows_b[:, s, :, :], CO // FINE)
                    fine_chain.link(nc.vector.tensor_scalar(inner[:, :], count[:, s, :], -1.0, 0.0, ALU.add, ALU.max))
                    keep = fine_f[:, bass.ds(k * NB, NB)]
                    fine_chain.link(nc.vector.scalar_tensor_tensor(
                        out=keep, in0=coarse_f[:, bass.ds(k * NB, NB)], scalar=float(CO // FINE), in1=inner[:, :],
                        op0=ALU.mult, op1=ALU.add))
                    fine_chain.end()
                    at_least(dve, rows_c_in[s], 16 * NB * r)
                    nc.vector.tensor_scalar(idx_c[:, s, :], keep, 0.0, None, ALU.add).then_inc(fine_done, 1)

                def edge(r, s):
                    k = r * 2 + s
                    at_least(dve, rows_c_in[s], 16 * NB * (r + 1))
                    edge_chain.start(k)
                    count_smaller(edge_chain, k, s, rows_c[:, s, :, :], FINE)
                    edge_chain.end()
                    nc.vector.scalar_tensor_tensor(out=start_f[:, bass.ds(k * NB, NB)], in0=fine_f[:, bass.ds(k * NB, NB)],
                                                   scalar=float(FINE), in1=count[:, s, :], op0=ALU.mult, op1=ALU.add).then_inc(start_made, 1)

                def norm(r, s):
                    k = r * 2 + s
                    at_least_apart(dve, normed_turned, k - 1, dve_passed)
                    norm_step(norm_chain, k, stats, small, var_made, dev_made, normed_made, lambda i: normed[:, s, i, :])

                def add_bias(r, s):
                    k = r * 2 + s
                    at_least(dve, send_made, k + 1)
                    nc.vector.tensor_tensor(recv_sb[:, bass.ds(k * NB, NB), :].rearrange("p (q h) c -> p q h c", h=2),
                                            ps_ab[:, :, 0:NB // 2, 0:C].rearrange("p h q c -> p q h c"),
                                            b1_all[:, :].unsqueeze(1).unsqueeze(1).broadcast_to([P, NB // 2, 2, C]), ALU.add).then_inc(recv_made, 1)

                pipeline(dve, NSTEP, 2, [(0, coarse), (0, norm), (1, fine), (2, edge), (1, add_bias)])

                def to_row(result, edges, add):
                    once.link(nc.vector.tensor_scalar(second[:, :], edges, MID - 0.5, float(1 - 2 * MID), ALU.is_gt, ALU.mult))
                    if add is not None:
                        once.link(nc.vector.tensor_tensor(second[:, :], second[:, :], add[:, :], ALU.add))
                    once.link(nc.vector.scalar_tensor_tensor(out=result[:, :], in0=edges, scalar=2.0, in1=second[:, :],
                                                             op0=ALU.mult, op1=ALU.add))

                dve.wait_ge(start_made, NSTEP + 1)
                once.inc(nc.vector.tensor_copy(start2[:, 0:NI], start_f[:, :]))
                dve.wait_ge(starts_in, 16)
                once.wait()
                once.link(nc.vector.tensor_tensor(degree[:, :], start2[:, 1:NI + 1], start2[:, 0:NI], ALU.subtract))
                once.link(nc.vector.tensor_scalar(has_edge[:, :], degree[:, :], 0.5, None, ALU.is_gt))
                once.link(nc.vector.tensor_scalar(skip[:, :], has_edge[:, :], -OUT_OF_RANGE, OUT_OF_RANGE, ALU.mult, ALU.add))
                to_row(skip, start2[:, 0:NI], skip)
                nc.vector.tensor_copy(start_idx[:, :], skip[:, :]).then_inc(idx_made, 1)
                nc.vector.tensor_copy(norm_deg[:, :, C], degree[:, :])
                once.link(nc.vector.tensor_scalar(last_edge[:, :], start2[:, 1:NI + 1], -1.0, 0.0, ALU.add, ALU.max))
                nc.vector.tensor_copy(end_idx[:, :], last_edge[:, :])
                to_row(last_edge, last_edge[:, :], None)
                nc.vector.tensor_copy(end_row[:, :], last_edge[:, :])
                dve.wait_ge(mid_in, 16)
                once.link(nc.vector.tensor_copy(mids_f[:, :], mids[:, :]))
                once.link(nc.vector.tensor_scalar(spans[:, :], node_f[:, :], mids_f[:, 0:1], None, ALU.is_equal))
                once.link(nc.vector.scalar_tensor_tensor(out=spans[:, :], in0=node_f[:, :], scalar=mids_f[:, 1:2],
                                                         in1=spans[:, :], op0=ALU.is_equal, op1=ALU.mult))
                nc.vector.tensor_scalar(spans_mid[:, :], spans[:, :], BIG, -BIG, ALU.mult, ALU.add)
                dve.wait_ge(src_in, 16 * 5)
                for g in range(4):
                    nc.vector.tensor_copy(src_rows_f[:, g, :], src_rows[:, g, :]).then_inc(src_f_made, 1)
                for g in range(4):
                    rows = min(P, NBLK - g * P)
                    dve.wait_ge(src_turned, g + 1)
                    nc.vector.tensor_copy(src_cols[:, g * P:g * P + rows, :],
                                          ps_src[:, :, 0:rows].rearrange("p j b -> p b j")).then_inc(src_made, 1)

        end_phase()

        with ExitStack() as s2:
            U = 4
            recv_in = tensor(s2, "recv_in", [P, U, J, 2 * C])
            mask_in = tensor(s2, "mask_in", [2, U, BLK], BF16)
            send_in = tensor(s2, "send_in", [P, U, J, 2, C])
            send_idx = tensor(s2, "send_idx", [P, 2, 2, 2 * J], I32)
            mask = tensor(s2, "mask", [P, 2, BLK])
            filled = tensor(s2, "filled", [P, 2, BLK])
            joined = tensor(s2, "joined", [P, 2, BLK])
            hidden = tensor(s2, "hidden", [P, 2, BLK])
            maxima = tensor(s2, "maxima", [P, 2, BLK])
            max_rows = tensor(s2, "max_rows", [P, U, J * 2 * C])
            w2_twice = tensor(s2, "w2_twice", [P, P])
            ps_recv = [banks(s2, f"ps_recv{b}", [P, BLK]) for b in range(2)]
            ps_send = [banks(s2, f"ps_send{b}", [P, BLK]) for b in range(2)]
            ps_mask = banks(s2, "ps_mask", [P, BLK])
            ps_msg = banks(s2, "ps_msg", [P, BLK])
            ps_back = [banks(s2, f"ps_back{b}", [P, J, P]) for b in range(2)]

            loaded = [sem(f"loaded{i}") for i in range(U)]
            gathered = [sem(f"gathered{i}") for i in range(U)]
            stored = [sem(f"stored{i}") for i in range(U)]
            (idx_copied, recv_turned, mask_spread, mask_copied, send_turned, fill_done, join_done, hidden_done, msg_done, max_done,
             back_turned, rows_made, w2_clear, w2_in) = (
                sem(n) for n in ("idx_copied", "recv_turned", "mask_spread", "mask_copied", "send_turned", "fill_done", "join_done",
                                     "hidden_done", "msg_done", "max_done", "back_turned", "rows_made", "w2_clear", "w2_in"))
            fill_start = sem("fill_start")
            pool_passed, dve_passed = sem("pool_passed2"), sem("dve_passed2")
            block = s2.enter_context(nc.Block())

            @block.sync
            def _(sp):
                recv_v = recv_edges.rearrange("(k p j t) c -> p k (j t c)", p=P, j=J, t=2)
                max_v = max_edges.rearrange("(k p j t) c -> p k (j t c)", p=P, j=J, t=2)
                mask_v = same_max.rearrange("(t k c) -> t k c", t=2, k=HB)
                sp.wait_ge(w2_clear, 1)
                for h in range(2):
                    sp.dma_start(w2_twice[h * C:(h + 1) * C, h * C:(h + 1) * C], W2).then_inc(w2_in, 16)

                def load(r, s):
                    k = r * U + s
                    at_least(sp, recv_turned, k - U + 1)
                    sp.dma_start(recv_in[:, s, :, :].rearrange("p j c -> p (j c)"), recv_v[:, bass.ds(k, 1), :].rearrange("p a f -> p (a f)")).then_inc(loaded[s], 16)
                    at_least(sp, mask_spread, k - U + 1)
                    sp.dma_start(mask_in[:, s, :], mask_v[:, bass.ds(k, 1), :].rearrange("t a c -> t (a c)")).then_inc(loaded[s], 16)

                def store(r, s):
                    k = r * U + s
                    at_least(sp, rows_made, k + 1)
                    sp.dma_start(max_v[:, bass.ds(k, 1), :].rearrange("p a f -> p (a f)"), max_rows[:, s, :]).then_inc(stored[s], 16)

                pipeline(sp, HB, U, [(0, load), (3, store)])
                for s in range(U):
                    sp.wait_ge(stored[s], 16 * (HB // U))

            @block.gpsimd
            def _(pool):
                cols = src_cols[:, :, :].rearrange("p (t k) j -> p t (k j)", t=2)
                nc.gpsimd.memset(w2_twice[:, :], 0.0).then_inc(w2_clear, 1)

                def gather(r, s):
                    k = r * U + s
                    if s % 2 == 0:
                        at_least(pool, gathered[s], 16 * 2 * J * r)
                        at_least(pool, gathered[s + 1], 16 * 2 * J * r)
                        nc.gpsimd.tensor_copy(send_idx[:, s // 2, :, :], cols[:, :, bass.ds(k * J, 2 * J)]).then_inc(idx_copied, 1)
                        at_least(pool, idx_copied, r * (U // 2) + s // 2 + 1)
                    at_least_apart(pool, send_turned, k - U + 1, pool_passed)
                    for t in range(2):
                        for j in range(J):
                            col = (s % 2) * J + j
                            pool.indirect_dma_start(out=send_in[:, s, j, t, :], out_offset=None, in_=send_table,
                                                    in_offset=bass.IndirectOffsetOnAxis(ap=send_idx[:, s // 2, t, col:col + 1], axis=0)
                                                    ).then_inc(gathered[s], 16)

                pipeline(pool, HB, U, [(0, gather)])

            @block.tensor
            def _(pe):
                def message(r, s):
                    k = r * U + s
                    at_least(pe, hidden_done, k + 1)
                    at_least(pe, max_done, k)
                    nc.tensor.matmul(ps_msg[:, :], w2_twice[:, :], hidden[:, s % 2, :], start=True, stop=True).then_inc(msg_done, 1)

                def turn_back(r, s):
                    k = r * U + s
                    at_least(pe, max_done, k + 1)
                    at_least(pe, rows_made, k - 1)
                    for j in range(J):
                        mm = nc.tensor.transpose(ps_back[s % 2][:, j, :], maxima[:, s % 2, j::J], ident[:, :])
                    mm.then_inc(back_turned, 1)

                def turn_in(r, s):
                    k = r * U + s
                    at_least(pe, loaded[s], 32 * (r + 1))
                    at_least(pe, fill_done, k - 1)
                    for j in range(J):
                        mm = nc.tensor.transpose(ps_recv[s % 2][:, j::J], recv_in[:, s, j, :], ident[:, :])
                    mm.then_inc(recv_turned, 1)
                    at_least(pe, mask_copied, k)
                    nc.tensor.matmul(ps_mask[:, :], sel2[:, :], mask_in[:, s, :], start=True, stop=True).then_inc(mask_spread, 1)
                    at_least(pe, gathered[s], 16 * 2 * J * (r + 1))
                    at_least(pe, join_done, k - 1)
                    for j in range(J):
                        mm = nc.tensor.transpose(ps_send[s % 2][:, j::J], send_in[:, s, j, :, :].rearrange("p t c -> p (t c)"), ident[:, :])
                    mm.then_inc(send_turned, 1)

                pe.wait_ge(w2_in, 32)
                pipeline(pe, HB, U, [(1, message), (2, turn_back), (0, turn_in)])

            @block.scalar
            def _(act):
                def copy_mask(r, s):
                    k = r * U + s
                    at_least(act, mask_spread, k + 1)
                    at_least(act, max_done, k - 1)
                    nc.scalar.copy(mask[:, s % 2, :], ps_mask[:, :]).then_inc(mask_copied, 1)

                def rows_out(r, s):
                    k = r * U + s
                    at_least(act, back_turned, k + 1)
                    at_least(act, stored[s], 16 * r)
                    nc.scalar.copy(max_rows[:, s, :], ps_back[s % 2][:, :, :].rearrange("p j q -> p (j q)")).then_inc(rows_made, 1)

                def relu(r, s):
                    k = r * U + s
                    at_least(act, join_done, k + 1)
                    at_least(act, msg_done, k - 1)
                    nc.scalar.activation(hidden[:, s % 2, :], joined[:, s % 2, :], ACT.Relu).then_inc(hidden_done, 1)

                pipeline(act, HB, U, [(0, copy_mask), (2, rows_out), (0, relu)])

            @block.vector
            def _(dve):
                nc.vector.memset(filled[:, 1, BLK - 1:BLK], -BIG).then_inc(fill_start, 1)
                nc.vector.memset(maxima[:, 1, BLK - 1:BLK], -BIG).then_inc(fill_start, 1)
                dve.wait_ge(fill_start, 2)

                def maximum(r, s):
                    k = r * U + s
                    at_least(dve, msg_done, k + 1)
                    at_least(dve, back_turned, k - 1)
                    at_least(dve, max_done, k)
                    nc.vector.tensor_tensor_scan(maxima[:, s % 2, :], mask[:, s % 2, :], ps_msg[:, :],
                                                 maxima[:, 1 - s % 2, BLK - 1:BLK], ALU.min, ALU.max).then_inc(max_done, 1)

                def fill(r, s):
                    k = r * U + s
                    at_least(dve, recv_turned, k + 1)
                    at_least(dve, mask_copied, k + 1)
                    at_least(dve, fill_done, k)
                    nc.vector.tensor_tensor_scan(filled[:, s % 2, :], mask[:, s % 2, :], ps_recv[s % 2][:, :],
                                                 filled[:, 1 - s % 2, BLK - 1:BLK], ALU.min, ALU.max).then_inc(fill_done, 1)

                def join(r, s):
                    k = r * U + s
                    at_least(dve, send_turned, k + 1)
                    at_least(dve, fill_done, k + 1)
                    at_least(dve, hidden_done, k - 1)
                    nc.vector.tensor_tensor(joined[:, s % 2, :], filled[:, s % 2, :], ps_send[s % 2][:, :], ALU.add).then_inc(join_done, 1)

                pipeline(dve, HB, U, [(1, maximum), (0, fill), (0, join)])

        end_phase()

        with ExitStack() as s3:
            max_in = tensor(s3, "max_in", [P, 2, NB, C])
            node_idx = tensor(s3, "node_idx", [P, 2, NB], I32)
            mid_max = tensor(s3, "mid_max", [P, C])
            b2_all = tensor(s3, "b2_all", [P, C])
            with_mid = tensor(s3, "with_mid", [P, NB, C])
            stats = tensor(s3, "stats3", [P, NB, 6])
            small = tensor(s3, "small3", [P, 8, NB])
            normed = tensor(s3, "normed3", [P, 2, NB, C])
            table_rows = tensor(s3, "table_rows", [P, 2, NB, C])
            max_got = [sem(f"max_got{i}") for i in range(2)]
            table_out = [sem(f"table_out{i}") for i in range(2)]
            idx_copied, mid_in, max_used, var_made, dev_made, normed_made, relu_made, kept = (
                sem(n) for n in ("idx_copied3", "mid_in3", "max_used", "var_made3", "dev_made3", "normed_made3", "relu_made3", "kept"))
            pool_passed, dve_passed = sem("pool_passed3"), sem("dve_passed3")
            block = s3.enter_context(nc.Block())

            @block.sync
            def _(sp):
                table_v = norm_table.rearrange("(p i) c -> p i c", i=NI)
                sp.dma_start(mid_max[:, :], max_edges[2 * (MID - 1):2 * MID - 1, :].rearrange("a c -> (a c)").partition_broadcast(P)).then_inc(mid_in, 16)
                sp.dma_start(b2_all[:, :], b2.partition_broadcast(P)).then_inc(mid_in, 16)

                def store(r, s):
                    k = r * 2 + s
                    at_least(sp, relu_made, k + 1)
                    sp.dma_start(table_v[:, bass.ds(k * NB, NB), :], table_rows[:, s, :, :]).then_inc(table_out[s], 16)

                pipeline(sp, NSTEP, 2, [(0, store)])
                for s in range(2):
                    sp.wait_ge(table_out[s], 16 * (NSTEP // 2))

            @block.gpsimd
            def _(pool):
                def gather(r, s):
                    k = r * 2 + s
                    at_least(pool, max_got[s], 16 * NB * r)
                    nc.gpsimd.tensor_copy(node_idx[:, s, :], end_row[:, bass.ds(k * NB, NB)]).then_inc(idx_copied, 1)
                    at_least(pool, idx_copied, k + 1)
                    at_least_apart(pool, max_used, k - 1, pool_passed)
                    for i in range(NB):
                        pool.indirect_dma_start(out=max_in[:, s, i, :], out_offset=None, in_=max_edges,
                                                in_offset=bass.IndirectOffsetOnAxis(ap=node_idx[:, s, i:i + 1], axis=0)).then_inc(max_got[s], 16)

                pipeline(pool, NSTEP, 2, [(0, gather)])

            @block.scalar
            def _(act):
                def step(r, s):
                    k = r * 2 + s
                    at_least(act, var_made, k + 1)
                    nc.scalar.activation(small[:, 3, :], small[:, 2, :], ACT.Sqrt).then_inc(dev_made, 1)
                    at_least(act, normed_made, NB * (k + 1))
                    at_least(act, table_out[s], 16 * r)
                    nc.scalar.activation(table_rows[:, s, :, :], normed[:, s, :, :], ACT.Relu).then_inc(relu_made, 1)
                    nc.scalar.activation(norm_deg[:, bass.ds(k * NB, NB), 0:C], normed[:, s, :, :], ACT.Relu).then_inc(kept, 1)

                pipeline(act, NSTEP, 2, [(0, step)])

            @block.vector
            def _(dve):
                dve.wait_ge(mid_in, 32)
                join_chain = Chain(dve, sem("join_chain"), 4)
                norm_chain = Chain(dve, sem("norm_chain3"), NORM_LINKS)

                def step(r, s):
                    k = r * 2 + s
                    cols = bass.ds(k * NB, NB)
                    at_least(dve, max_got[s], 16 * NB * (r + 1))
                    join_chain.start(k)
                    join_chain.link(nc.vector.tensor_tensor(with_mid[:, :, :], mid_max[:, :].unsqueeze(1).broadcast_to([P, NB, C]),
                                                            spans_mid[:, cols].unsqueeze(2).broadcast_to([P, NB, C]), ALU.add))
                    nc.vector.tensor_tensor(with_mid[:, :, :], max_in[:, s, :, :], with_mid[:, :, :], ALU.max).then_inc(max_used, 1)
                    at_least(dve, max_used, k + 1)
                    join_chain.link(nc.vector.tensor_tensor(with_mid[:, :, :], with_mid[:, :, :],
                                                            b2_all[:, :].unsqueeze(1).broadcast_to([P, NB, C]), ALU.add))
                    join_chain.link(nc.vector.tensor_tensor(with_mid[:, :, :], with_mid[:, :, :],
                                                            has_edge[:, cols].unsqueeze(2).broadcast_to([P, NB, C]), ALU.mult))
                    join_chain.link(nc.vector.tensor_tensor(nodes[:, cols, :], nodes[:, cols, :], with_mid[:, :, :], ALU.add))
                    join_chain.end()
                    at_least_apart(dve, kept, k - 1, dve_passed)
                    norm_step(norm_chain, k, stats, small, var_made, dev_made, normed_made, lambda i: normed[:, s, i, :])

                pipeline(dve, NSTEP, 2, [(0, step)])

        end_phase()

        keep = stack.enter_context(ExitStack())
        gain = tensor(keep, "gain", [P, 2])
        shift = tensor(keep, "shift", [P, 2])
        with ExitStack() as s4:
            U = 8
            edge_in = tensor(s4, "edge_in", [P, U, J, C])
            pairs = tensor(s4, "pairs", [P, U, J, 2 * C])
            send_idx = tensor(s4, "send_idx4", [P, 2, U // 2 * J], I32)
            pairs_t = tensor(s4, "pairs_t", [P, 2, BLK])
            hid = tensor(s4, "hid", [P, U, BLK])
            stats = tensor(s4, "stats4", [P, NBLK, 6])
            w1a = tensor(s4, "w1a", [P, HID])
            vec = tensor(s4, "vec4", [P, 3])
            sums = tensor(s4, "sums4", [P, 6])
            ps_pairs = [banks(s4, f"ps_pairs{b}", [P, BLK]) for b in range(2)]
            ps_hid = [banks(s4, f"ps_hid{b}", [P, BLK]) for b in range(2)]
            loaded = [sem(f"loaded4_{i}") for i in range(U)]
            gathered = [sem(f"gathered4_{i}") for i in range(U)]
            stored = [sem(f"stored4_{i}") for i in range(U)]
            idx_copied, w_in, turned, copied, multiplied, hid_made, stats_made, root_ready, root_made = (
                sem(n + "4") for n in ("idx_copied", "w_in", "turned", "copied", "multiplied", "hid_made", "stats_made", "root_ready", "root_made"))
            edge_copied = sem("edge_copied")
            pool_passed, dve_passed = sem("pool_passed4"), sem("dve_passed4")
            block = s4.enter_context(nc.Block())

            @block.sync
            def _(sp):
                attr_v = edge_attr[0:LAST_BLK * BLK, :].rearrange("(k p j) c -> p k (j c)", p=P, j=J)
                hid_v = hid_edges.rearrange("k p c -> p k c")
                sp.dma_start(w1a[:, :], W1a).then_inc(w_in, 16)
                with nc.allow_non_contiguous_dma(reason="one element per partition"):
                    for n, v in enumerate((b1a, g1a, be1a)):
                        sp.dma_start(vec[:, n:n + 1], v.rearrange("(p a) -> p a", a=1)).then_inc(w_in, 16)

                def load(r, s):
                    k = r * U + s
                    at_least(sp, edge_copied, k - U + 1)
                    if isinstance(k, int) and k == LAST_BLK:
                        sp.dma_start(edge_in[0:TAIL // J, s, :, :].rearrange("p j c -> p (j c)"), edge_attr[LAST_BLK * BLK:E, :].rearrange("(p j) c -> p (j c)", j=J)).then_inc(loaded[s], 16)
                    else:
                        sp.dma_start(edge_in[:, s, :, :].rearrange("p j c -> p (j c)"), attr_v[:, bass.ds(k, 1), :].rearrange("p a f -> p (a f)")).then_inc(loaded[s], 16)

                def store(r, s):
                    k = r * U + s
                    at_least(sp, hid_made, k + 1)
                    sp.dma_start(hid_v[:, bass.ds(k, 1), :].rearrange("p a f -> p (a f)"), hid[:, s, :]).then_inc(stored[s], 16)

                pipeline(sp, NBLK, U, [(0, load), (5, store)])
                for s in range(U):
                    sp.wait_ge(stored[s], 16 * (NBLK // U))

            @block.gpsimd
            def _(pool):
                cols = src_cols[:, :, :].rearrange("p k j -> p (k j)")
                H = U // 2

                def gather(r, s):
                    k = r * U + s
                    if s % H == 0:
                        for q in range(s, s + H):
                            at_least(pool, gathered[q], 16 * J * r)
                        nc.gpsimd.tensor_copy(send_idx[:, s // H, :], cols[:, bass.ds(k * J, H * J)]).then_inc(idx_copied, 1)
                        at_least(pool, idx_copied, r * 2 + s // H + 1)
                    at_least_apart(pool, turned, k - U + 1, pool_passed)
                    for j in range(J):
                        col = (s % H) * J + j
                        pool.indirect_dma_start(out=pairs[:, s, j, 0:C], out_offset=None, in_=norm_table,
                                                in_offset=bass.IndirectOffsetOnAxis(ap=send_idx[:, s // H, col:col + 1], axis=0)
                                                ).then_inc(gathered[s], 16)

                pipeline(pool, NBLK, U, [(0, gather)])

            @block.tensor
            def _(pe):
                def turn(r, s):
                    k = r * U + s
                    at_least(pe, edge_copied, k + 1)
                    at_least(pe, gathered[s], 16 * J * (r + 1))
                    at_least(pe, copied, k - 1)
                    for j in range(J):
                        mm = nc.tensor.transpose(ps_pairs[s % 2][:, j::J], pairs[:, s, j, :], ident[:, :])
                    mm.then_inc(turned, 1)

                def product(r, s):
                    k = r * U + s
                    at_least(pe, copied, k + 1)
                    at_least(pe, hid_made, k - 1)
                    nc.tensor.matmul(ps_hid[s % 2][:, :], w1a[:, :], pairs_t[:, s % 2, :], start=True, stop=True).then_inc(multiplied, 1)

                pe.wait_ge(w_in, 64)
                pipeline(pe, NBLK, U, [(0, turn), (1, product)])

            @block.scalar
            def _(act):
                def copy(r, s):
                    k = r * U + s
                    at_least(act, turned, k + 1)
                    at_least(act, multiplied, k - 1)
                    nc.scalar.copy(pairs_t[:, s % 2, :], ps_pairs[s % 2][:, :]).then_inc(copied, 1)

                def copy_edge(r, s):
                    k = r * U + s
                    at_least(act, loaded[s], 16 * (r + 1))
                    at_least(act, turned, k - U + 1)
                    nc.scalar.copy(pairs[:, s, :, C:2 * C], edge_in[:, s, :, :]).then_inc(edge_copied, 1)

                pipeline(act, NBLK, U, [(0, copy_edge), (1, copy)])
                act.wait_ge(root_ready, 1)
                nc.scalar.activation(sums[:, 3:4], sums[:, 2:3], ACT.Sqrt).then_inc(root_made, 1)

            @block.vector
            def _(dve):
                def finish(r, s):
                    k = r * U + s
                    at_least(dve, multiplied, k + 1)
                    at_least(dve, stored[s], 16 * r)
                    nc.vector.tensor_scalar(hid[:, s, :], ps_hid[s % 2][:, :], vec[:, 0:1], None, ALU.add).then_inc(hid_made, 1)
                    at_least_apart(dve, hid_made, k + 1, dve_passed)
                    valid = TAIL if isinstance(k, int) and k == LAST_BLK else BLK
                    nc.vector.bn_stats(stats[:, bass.ds(k, 1), :].rearrange("p a q -> p (a q)"), hid[:, s, 0:valid]).then_inc(stats_made, 1)

                dve.wait_ge(w_in, 64)
                pipeline(dve, NBLK, U, [(0, finish)])
                dve.wait_ge(stats_made, NBLK)
                affine_of_norm(Chain(dve, sem("affine4")), root_ready, root_made, stats[:, :, :].rearrange("p k q -> p (k q)"),
                               sums, gain[:, 0:1], shift[:, 0:1], vec[:, 1:2], vec[:, 2:3])

        end_phase()

        with ExitStack() as s5:
            U = 4
            hid = tensor(s5, "hid5", [P, U, BLK])
            mask_in = tensor(s5, "mask_in5", [1, U, BLK], BF16)
            ones5 = tensor(s5, "ones5", [1, P], BF16)
            act_out = tensor(s5, "act_out", [P, 2, BLK])
            total = tensor(s5, "total", [P, 2, BLK])
            rows = tensor(s5, "rows5", [P, U, J * HID])
            ps_mask = [banks(s5, f"ps_mask5_{b}", [P, BLK]) for b in range(2)]
            ps_back = [banks(s5, f"ps_back5_{b}", [P, J * P]) for b in range(2)]
            loaded = [sem(f"loaded5_{i}") for i in range(U)]
            stored = [sem(f"stored5_{i}") for i in range(U)]
            begun, mask_spread, relu_done, sum_done, back_turned, rows_made = (
                sem(n + "5") for n in ("begun", "mask_spread", "relu_done", "sum_done", "back_turned", "rows_made"))
            pool_passed, dve_passed = sem("pool_passed5"), sem("dve_passed5")
            block = s5.enter_context(nc.Block())

            @block.sync
            def _(sp):
                hid_v = hid_edges.rearrange("k p c -> p k c")
                mask_v = same_sum.rearrange("(a k c) -> a k c", a=1, k=NBLK)
                sum_v = sum_edges.rearrange("(k p j) c -> p k (j c)", p=P, j=J)

                def load(r, s):
                    k = r * U + s
                    at_least(sp, relu_done, k - U + 1)
                    sp.dma_start(hid[:, s, :], hid_v[:, bass.ds(k, 1), :].rearrange("p a f -> p (a f)")).then_inc(loaded[s], 16)
                    at_least(sp, mask_spread, k - U + 1)
                    sp.dma_start(mask_in[:, s, :], mask_v[:, bass.ds(k, 1), :].rearrange("t a c -> t (a c)")).then_inc(loaded[s], 16)

                def store(r, s):
                    k = r * U + s
                    at_least(sp, rows_made, k + 1)
                    sp.dma_start(sum_v[:, bass.ds(k, 1), :].rearrange("p a f -> p (a f)"), rows[:, s, :]).then_inc(stored[s], 16)

                pipeline(sp, NBLK, U, [(0, load), (3, store)])
                for s in range(U):
                    sp.wait_ge(stored[s], 16 * (NBLK // U))

            @block.tensor
            def _(pe):
                def spread(r, s):
                    k = r * U + s
                    at_least(pe, loaded[s], 32 * (r + 1))
                    at_least(pe, sum_done, k - 1)
                    nc.tensor.matmul(ps_mask[s % 2][:, :], ones5[:, :], mask_in[:, s, :], start=True, stop=True).then_inc(mask_spread, 1)

                def turn_back(r, s):
                    k = r * U + s
                    at_least(pe, sum_done, k + 1)
                    at_least(pe, rows_made, k - 1)
                    for j in range(J):
                        mm = nc.tensor.transpose(ps_back[s % 2][:, j * P:(j + 1) * P], total[:, s % 2, j::J], ident[:, :])
                    mm.then_inc(back_turned, 1)

                pe.wait_ge(begun, 2)
                pipeline(pe, NBLK, U, [(0, spread), (1, turn_back)])

            @block.scalar
            def _(act):
                def relu(r, s):
                    k = r * U + s
                    at_least(act, loaded[s], 32 * (r + 1))
                    at_least(act, sum_done, k - 1)
                    nc.scalar.activation(act_out[:, s % 2, :], hid[:, s, :], ACT.Relu, bias=shift[:, 0:1], scale=gain[:, 0:1]).then_inc(relu_done, 1)

                def rows_out(r, s):
                    k = r * U + s
                    at_least(act, back_turned, k + 1)
                    at_least(act, stored[s], 16 * r)
                    nc.scalar.copy(rows[:, s, :], ps_back[s % 2][:, :]).then_inc(rows_made, 1)

                pipeline(act, NBLK, U, [(0, relu), (1, rows_out)])

            @block.vector
            def _(dve):
                nc.vector.memset(total[:, 1, BLK - 1:BLK], 0.0).then_inc(begun, 1)
                nc.vector.memset(ones5[:, :], 1.0).then_inc(begun, 1)
                dve.wait_ge(begun, 2)

                def running_sum(r, s):
                    k = r * U + s
                    at_least(dve, mask_spread, k + 1)
                    at_least(dve, relu_done, k + 1)
                    at_least(dve, back_turned, k - 1)
                    at_least(dve, sum_done, k)
                    nc.vector.tensor_tensor_scan(total[:, s % 2, :], ps_mask[s % 2][:, :], act_out[:, s % 2, :],
                                                 total[:, 1 - s % 2, BLK - 1:BLK], ALU.mult, ALU.add).then_inc(sum_done, 1)

                pipeline(dve, NBLK, U, [(0, running_sum)])

        end_phase()

        with ExitStack() as s6:
            NC = 5
            STEPS = NI // NC
            sum_in = tensor(s6, "sum_in", [P, 2, NC, HID])
            node_idx = tensor(s6, "node_idx6", [P, 2, NC], I32)
            sum_kept = tensor(s6, "sum_kept", [P, 2, NC, HID])
            norm_in = tensor(s6, "norm_in", [P, 2, NC, C + 1])
            sum_t = tensor(s6, "sum_t", [P, 2, NC * P])
            norm_t = tensor(s6, "norm_t", [C + 1, 2, NC * P])
            hid2 = tensor(s6, "hid2", [P, NI * P])
            stats = tensor(s6, "stats6", [P, 2 * STEPS, 6])
            vec = tensor(s6, "vec6", [P, 3])
            b2b_all = tensor(s6, "b2b_all", [P, C])
            w2a = tensor(s6, "w2a", [P, HID])
            w2a_t = tensor(s6, "w2a_t", [P, HID])
            w1b_low = tensor(s6, "w1b_low", [P, HID])
            w1b_top = tensor(s6, "w1b_top", [C + 1, HID])
            b2a_col = tensor(s6, "b2a_col", [P, C + 1])
            w_sum = tensor(s6, "w_sum", [P, HID])
            w_norm = tensor(s6, "w_norm", [C + 1, HID])
            w2b = tensor(s6, "w2b", [P, C])
            sums = tensor(s6, "sums6", [P, 6])
            active = tensor(s6, "active", [P, 2, NC, P])
            partial = tensor(s6, "partial", [P, 2, NC, C])
            result = tensor(s6, "result", [P, 2, NC, C])
            ps_sum = banks(s6, "ps_sum", [P, 8, P])
            ps_norm = banks(s6, "ps_norm", [P, 8, P])
            ps_hid = banks(s6, "ps_hid6", [P, 8 * P])
            ps_out = [banks(s6, f"ps_out{b}", [P, 8, C]) for b in range(2)]
            sum_got = [sem(f"sum_got{i}") for i in range(2)]
            out_done = [sem(f"out_done{i}") for i in range(2)]
            (cleared, w_in, w_turned, w_copied, w_multiplied, w_ready, idx_copied, sum_scaled, norm_copied, both_turned, sum_copied,
             norm_t_copied, multiplied, hid_made, stats_made, root_ready, root_made, affine_ready, relu_done, out_multiplied,
             partial_made, result_made) = (
                sem(n + "6") for n in ("cleared", "w_in", "w_turned", "w_copied", "w_multiplied", "w_ready", "idx_copied", "sum_scaled",
                                           "norm_copied", "both_turned", "sum_copied", "norm_t_copied", "multiplied", "hid_made",
                                           "stats_made", "root_ready", "root_made", "affine_ready", "relu_done", "out_multiplied",
                                           "partial_made", "result_made"))
            pool_passed, dve_passed = sem("pool_passed6"), sem("dve_passed6")
            block = s6.enter_context(nc.Block())

            @block.sync
            def _(sp):
                sp.dma_start(w2a[:, :], W2a).then_inc(w_in, 16)
                sp.dma_start(w1b_low[:, :], W1b[C:C + HID, :]).then_inc(w_in, 16)
                sp.dma_start(w2b[:, :], W2b).then_inc(w_in, 16)
                sp.dma_start(b2b_all[:, :], b2b.partition_broadcast(P)).then_inc(w_in, 16)
                with nc.allow_non_contiguous_dma(reason="one element per partition"):
                    for n, v in enumerate((b1b, g1b, be1b)):
                        sp.dma_start(vec[:, n:n + 1], v.rearrange("(p a) -> p a", a=1)).then_inc(w_in, 16)
                    sp.wait_ge(cleared, 2)
                    sp.dma_start(w1b_top[0:C, :], W1b[0:C, :]).then_inc(w_in, 16)
                    sp.dma_start(b2a_col[:, C:C + 1], b2a.rearrange("(p a) -> p a", a=1)).then_inc(w_in, 16)
                out_v = out.rearrange("(p i) c -> p i c", i=NI)

                def store(r, s):
                    k = r * 2 + s
                    at_least(sp, result_made, k + 1)
                    sp.dma_start(out_v[:, bass.ds(k * NC, NC), :], result[0:NODE_P, s, :, :]).then_inc(out_done[s], 16)

                pipeline(sp, STEPS, 2, [(0, store)])
                for s in range(2):
                    sp.wait_ge(out_done[s], 16 * (STEPS // 2))

            @block.gpsimd
            def _(pool):
                nc.gpsimd.memset(w1b_top[:, :], 0.0).then_inc(cleared, 1)
                nc.gpsimd.memset(b2a_col[:, :], 0.0).then_inc(cleared, 1)

                def gather(r, s):
                    k = r * 2 + s
                    at_least(pool, sum_got[s], 16 * NC * r)
                    nc.gpsimd.tensor_copy(node_idx[:, s, :], end_idx[:, bass.ds(k * NC, NC)]).then_inc(idx_copied, 1)
                    at_least(pool, idx_copied, k + 1)
                    at_least_apart(pool, sum_scaled, k - 1, pool_passed)
                    for i in range(NC):
                        pool.indirect_dma_start(out=sum_in[:, s, i, :], out_offset=None, in_=sum_edges,
                                                in_offset=bass.IndirectOffsetOnAxis(ap=node_idx[:, s, i:i + 1], axis=0)).then_inc(sum_got[s], 16)

                pipeline(pool, STEPS, 2, [(0, gather)])

            @block.tensor
            def _(pe):
                pe.wait_ge(w_in, 16 * 9)
                nc.tensor.transpose(ps_sum[:, 0, :], w2a[:, :], ident[:, :]).then_inc(w_turned, 1)
                pe.wait_ge(w_copied, 1)
                nc.tensor.matmul(ps_hid[:, 0:HID], w2a_t[:, :], w1b_low[:, :], start=True, stop=True).then_inc(w_multiplied, 1)
                nc.tensor.matmul(ps_norm[0:C + 1, 0, :], b2a_col[:, :], w1b_low[:, :], start=True, stop=True).then_inc(w_multiplied, 1)
                pe.wait_ge(w_ready, 2)

                def turn(r, s):
                    k = r * 2 + s
                    at_least(pe, sum_scaled, k + 1)
                    at_least(pe, sum_copied, k)
                    for i in range(NC):
                        nc.tensor.transpose(ps_sum[:, i, :], sum_kept[:, s, i, :], ident[:, :])
                    at_least(pe, norm_copied, k + 1)
                    at_least(pe, norm_t_copied, k)
                    for i in range(NC):
                        mm = nc.tensor.transpose(ps_norm[0:C + 1, i, :], norm_in[:, s, i, :], ident[:, :])
                    mm.then_inc(both_turned, 1)

                def product(r, s):
                    k = r * 2 + s
                    at_least(pe, sum_copied, k + 1)
                    at_least(pe, norm_t_copied, k + 1)
                    at_least(pe, hid_made, k)
                    for a, b in ((0, 512), (512, NC * P)):
                        nc.tensor.matmul(ps_hid[:, a:b], w_sum[:, :], sum_t[:, s, a:b], start=True, stop=False)
                        mm = nc.tensor.matmul(ps_hid[:, a:b], w_norm[:, :], norm_t[:, s, a:b], start=False, stop=True)
                    mm.then_inc(multiplied, 1)

                pipeline(pe, STEPS, 2, [(1, product), (0, turn)])

                def last_product(r, s):
                    k = r * 2 + s
                    at_least(pe, relu_done, k + 1)
                    at_least(pe, partial_made, k - 1)
                    for i in range(NC):
                        mm = nc.tensor.matmul(ps_out[s][:, i, :], active[:, s, i, :], w2b[:, :], start=True, stop=True)
                    mm.then_inc(out_multiplied, 1)

                pipeline(pe, STEPS, 2, [(0, last_product)])

            @block.scalar
            def _(act):
                act.wait_ge(w_turned, 1)
                nc.scalar.copy(w2a_t[:, :], ps_sum[:, 0, :]).then_inc(w_copied, 1)
                act.wait_ge(w_multiplied, 2)
                nc.scalar.copy(w_sum[:, :], ps_hid[:, 0:HID]).then_inc(w_ready, 1)

                def copy_norm(r, s):
                    k = r * 2 + s
                    at_least(act, both_turned, k - 1)
                    nc.scalar.copy(norm_in[:, s, :, :], norm_deg[:, bass.ds(k * NC, NC), :]).then_inc(norm_copied, 1)

                def copy_sum(r, s):
                    k = r * 2 + s
                    at_least(act, both_turned, k + 1)
                    at_least(act, multiplied, k - 1)
                    nc.scalar.copy(sum_t[:, s, :], ps_sum[:, 0:NC, :].rearrange("p i q -> p (i q)")).then_inc(sum_copied, 1)

                pipeline(act, STEPS, 2, [(0, copy_norm), (1, copy_sum)])
                act.wait_ge(root_ready, 1)
                nc.scalar.activation(sums[:, 3:4], sums[:, 2:3], ACT.Sqrt).then_inc(root_made, 1)
                act.wait_ge(affine_ready, 1)

                def relu(r, s):
                    k = r * 2 + s
                    at_least(act, out_multiplied, k - 1)
                    nc.scalar.activation(active[:, s, :, :].rearrange("p i q -> p (i q)"), hid2[:, bass.ds(k * NC * P, NC * P)], ACT.Relu,
                                         bias=shift[:, 1:2], scale=gain[:, 1:2]).then_inc(relu_done, 1)

                pipeline(act, STEPS, 2, [(0, relu)])

            @block.vector
            def _(dve):
                dve.wait_ge(w_multiplied, 2)
                nc.vector.tensor_tensor(w_norm[:, :], ps_norm[0:C + 1, 0, :], w1b_top[:, :], ALU.add).then_inc(w_ready, 1)

                def scale(r, s):
                    k = r * 2 + s
                    at_least(dve, sum_got[s], 16 * NC * (r + 1))
                    at_least(dve, both_turned, k - 1)
                    nc.vector.tensor_tensor(sum_kept[:, s, :, :], sum_in[:, s, :, :],
                                            has_edge[:, bass.ds(k * NC, NC)].unsqueeze(2).broadcast_to([P, NC, HID]), ALU.mult).then_inc(sum_scaled, 1)

                def copy_norm_t(r, s):
                    k = r * 2 + s
                    at_least(dve, both_turned, k + 1)
                    at_least(dve, multiplied, k - 1)
                    nc.vector.tensor_copy(norm_t[:, s, :], ps_norm[0:C + 1, 0:NC, :].rearrange("p i q -> p (i q)")).then_inc(norm_t_copied, 1)

                def finish(r, s):
                    k = r * 2 + s
                    at_least(dve, multiplied, k + 1)
                    part = hid2[:, bass.ds(k * NC * P, NC * P)]
                    nc.vector.tensor_scalar(part, ps_hid[:, 0:NC * P], vec[:, 0:1], None, ALU.add).then_inc(hid_made, 1)
                    at_least_apart(dve, hid_made, k + 1, dve_passed)
                    cols = part.rearrange("p (i q) -> p i q", q=P)[:, :, 0:NODE_P]
                    nc.vector.bn_stats(stats[:, bass.ds(2 * k, 1), :].rearrange("p a q -> p (a q)"), cols[:, 0:2, :]).then_inc(stats_made, 1)
                    nc.vector.bn_stats(stats[:, bass.ds(2 * k + 1, 1), :].rearrange("p a q -> p (a q)"), cols[:, 2:NC, :]).then_inc(stats_made, 1)

                pipeline(dve, STEPS, 2, [(0, scale), (1, copy_norm_t), (2, finish)])
                dve.wait_ge(stats_made, 2 * STEPS)
                affine_of_norm(Chain(dve, sem("affine6")), root_ready, root_made, stats[:, :, :].rearrange("p k q -> p (k q)"),
                               sums, gain[:, 1:2], shift[:, 1:2], vec[:, 1:2], vec[:, 2:3])
                nc.vector.memset(sums[:, 5:6], 0.0).then_inc(affine_ready, 1)

                def partial_step(r, s):
                    k = r * 2 + s
                    at_least(dve, out_multiplied, k + 1)
                    nc.vector.tensor_tensor(partial[:, s, :, :], ps_out[s][:, 0:NC, :], nodes[:, bass.ds(k * NC, NC), :], ALU.add).then_inc(partial_made, 1)
                    at_least(dve, partial_made, k + 1)
                    at_least(dve, out_done[s], 16 * r)
                    nc.vector.tensor_tensor(result[:, s, :, :], partial[:, s, :, :],
                                            b2b_all[:, :].unsqueeze(1).broadcast_to([P, NC, C]), ALU.add).then_inc(result_made, 1)

                pipeline(dve, STEPS, 2, [(0, partial_step)])


_INS = ["x", "src", "dst", "edge_attr_64", "L0_gnn_W1", "L0_gnn_b1", "L0_gnn_W2", "L0_gnn_b2", "L1_gnn_W1a", "L1_gnn_b1a",
        "L1_gnn_g1a", "L1_gnn_be1a", "L1_gnn_W2a", "L1_gnn_b2a", "L1_gnn_W1b", "L1_gnn_b1b", "L1_gnn_g1b", "L1_gnn_be1b",
        "L1_gnn_W2b", "L1_gnn_b2b"]


_OUTS = [((12500, 64), "float32")]


def kernel(**inputs):
    import numpy as _np
    import concourse.bacc as _bacc
    from concourse import mybir as _mybir
    from concourse.bass_utils import run_bass_kernel_spmd as _run

    nc = _bacc.Bacc("TRN2", target_bir_lowering=False, num_devices=1)
    arrays, args = {}, []
    for name in _INS:
        a = _np.ascontiguousarray(inputs[name])
        arrays[f"in_{name}_dram"] = a
        args.append(nc.dram_tensor(f"in_{name}_dram", a.shape, _mybir.dt.from_np(a.dtype), kind="ExternalInput").ap())
    for i, (shape, dtype) in enumerate(_OUTS):
        dt = _mybir.dt.from_np(_np.dtype(dtype))
        args.append(nc.dram_tensor(f"out_{i}_dram", shape, dt, kind="ExternalOutput").ap())
    gnn_kernel(nc, *args)
    r = _run(nc, [arrays], core_ids=[0])
    got = tuple(r.results[0][f"out_{i}_dram"] for i in range(len(_OUTS)))
    return got[0]
```

```python
from contextlib import ExitStack

import concourse.bass as bass
from concourse import mybir

P = 128
ALU = mybir.AluOpType
ACT = mybir.ActivationFunctionType
AX = mybir.AxisListType
F32 = mybir.dt.float32
BF16 = mybir.dt.bfloat16
I32 = mybir.dt.int32
I16 = mybir.dt.int16

BIG = 1.0e38
EPS = 1e-5


def at_least(eng, semaphore, value):
    if isinstance(value, int) and value <= 0:
        return
    eng.wait_ge(semaphore, value)


def at_least_apart(eng, semaphore, value, passed):
    at_least(eng, semaphore, value)
    if not isinstance(value, int):
        eng.sem_inc(passed, 1)


class Chain:

    def __init__(self, eng, semaphore, per_step=0):
        self.eng, self.semaphore, self.per_step = eng, semaphore, per_step
        self.base, self.n = 0, 0

    def start(self, step):
        self.base, self.n = step * self.per_step, 0

    def inc(self, ins):
        self.n += 1
        ins.then_inc(self.semaphore, 1)

    def wait(self):
        at_least(self.eng, self.semaphore, self.base + self.n)

    def link(self, ins):
        self.inc(ins)
        self.wait()

    def end(self):
        assert self.n == self.per_step


def pipeline(eng, steps, unroll, stages):
    rounds = steps // unroll
    assert rounds * unroll == steps and rounds >= 2
    last = max(lag for lag, _ in stages)
    assert last <= unroll

    def peeled(step):
        for lag, stage in stages:
            if 0 <= step - lag < steps:
                stage((step - lag) // unroll, (step - lag) % unroll)

    for step in range(unroll):
        peeled(step)
    if rounds > 2:
        with eng.Fori(1, rounds - 1) as r:
            for slot in range(unroll):
                for lag, stage in stages:
                    back = (slot - lag) // unroll
                    stage(r + back if back else r, (slot - lag) % unroll)
    for step in range(steps - unroll, steps + last):
        peeled(step)


def gnn_kernel(nc, x, src, dst, edge_attr, W1, b1, W2, b2, W1a, b1a, g1a, be1a, W2a, b2a,
               W1b, b1b, g1b, be1b, W2b, b2b, out):
    N, C = x.shape
    E = src.shape[0]
    HID = W1a.shape[1]
    assert C == 64 and HID == 128
    J = 4
    BLK = P * J
    CO = 2048
    NCO = -(-E // CO)
    EP = NCO * CO
    NBLK = EP // BLK
    HB = NBLK // 2
    MID = HB * BLK
    GRP = BLK
    NGRP = EP // GRP
    PAD_DST = 2 ** 15 - 1
    NI = 100
    NODE_P = N // NI
    NP = P * NI
    assert NODE_P * NI == N and NBLK % 8 == 0 and HB % 4 == 0
    FULL_CO = E // CO
    LAST_BLK = E // BLK
    TAIL = E - LAST_BLK * BLK
    assert LAST_BLK == NBLK - 1 and TAIL % J == 0 and TAIL > 0
    NB = 10
    NSTEP = NI // NB
    NS = 5
    SSTEP = NI // NS
    SLOTS = 4
    OUT_OF_RANGE = 1.0e6
    assert 3 * P < NBLK <= 4 * P and N < PAD_DST and NGRP <= 512

    def dram(name, shape, dt=F32):
        return nc.dram_tensor(name, shape, dt, kind="Internal").ap()

    dst_groups = dram("dst_groups", (NGRP, GRP), I16)
    same_max = dram("same_max", (EP,), BF16)
    same_sum = dram("same_sum", (EP,), BF16)
    recv_table = dram("recv_table", (NP, C))
    send_table = dram("send_table", (NP, C))
    recv_edges = dram("recv_edges", (EP, C))
    max_edges = dram("max_edges", (EP, C))
    norm_table = dram("norm_table", (NP, C))
    hid_edges = dram("hid_edges", (NBLK // 2, P, 2 * BLK))
    sum_edges = dram("sum_edges", (EP, HID))

    stack = ExitStack()
    with stack:
        def tensor(scope, name, shape, dt=F32):
            return scope.enter_context(nc.sbuf_tensor(name, shape, dt))

        def banks(scope, name, shape, dt=F32):
            return scope.enter_context(nc.psum_tensor(name, shape, dt))

        def sem(name):
            phase_sems.append(nc.alloc_semaphore(name))
            return phase_sems[-1]

        phase_sems = []

        def end_phase():
            nc.clear_and_free_semaphores(list(phase_sems))
            phase_sems.clear()
            nc.all_engine_barrier()

        nodes = tensor(stack, "nodes", [P, NI, C])
        norm_deg = tensor(stack, "norm_deg", [P, NI, C + 1])
        src_cols = tensor(stack, "src_cols", [P, NBLK, J], I32)
        ident = tensor(stack, "ident", [P, P])
        end_idx = tensor(stack, "end_idx", [P, NI], I32)
        end_row = tensor(stack, "end_row", [P, NI], I32)
        has_edge = tensor(stack, "has_edge", [P, NI])
        spans_mid = tensor(stack, "spans_mid", [P, NI])
        mids = tensor(stack, "mids", [P, 2], I32)
        sel2 = tensor(stack, "sel2", [2, P], BF16)

        def norm_step(chain, k, stats, small, var_made, dev_made, made, result):
            dve = chain.eng
            chain.start(k)
            for i in range(NB):
                chain.inc(nc.vector.bn_stats(stats[:, i, :], nodes[:, bass.ds(k * NB + i, 1), :].rearrange("p a c -> p (a c)")))
            chain.wait()
            total, gap, var, dev, mean, inv, square, both = (small[:, q, :] for q in range(8))
            chain.inc(nc.vector.tensor_tensor(total, stats[:, :, 1], stats[:, :, 4], ALU.add))
            chain.inc(nc.vector.tensor_tensor(gap, stats[:, :, 1], stats[:, :, 4], ALU.subtract))
            chain.link(nc.vector.tensor_tensor(both, stats[:, :, 2], stats[:, :, 5], ALU.add))
            chain.inc(nc.vector.scalar_tensor_tensor(out=square, in0=gap, scalar=0.25, in1=gap, op0=ALU.mult, op1=ALU.mult))
            chain.link(nc.vector.tensor_scalar(both, both, 1.0 / C, EPS, ALU.mult, ALU.add))
            nc.vector.tensor_tensor(var, both, square, ALU.add).then_inc(var_made, 1)
            chain.inc(nc.vector.tensor_scalar(mean, total, 0.5, None, ALU.mult))
            at_least(dve, dev_made, k + 1)
            chain.link(nc.vector.reciprocal(inv, dev))
            chain.end()
            for i in range(NB):
                nc.vector.tensor_scalar(result(i), nodes[:, bass.ds(k * NB + i, 1), :].rearrange("p a c -> p (a c)"),
                                        mean[:, i:i + 1], inv[:, i:i + 1], ALU.subtract, ALU.mult).then_inc(made, 1)

        NORM_LINKS = NB + 7

        def affine_of_norm(chain, root_ready, root_made, stats, sums, gain, shift, g, be):
            chain.link(nc.vector.bn_aggr(sums[:, 0:2], stats))
            nc.vector.tensor_scalar(sums[:, 2:3], sums[:, 1:2], EPS, None, ALU.add).then_inc(root_ready, 1)
            chain.eng.wait_ge(root_made, 1)
            chain.link(nc.vector.reciprocal(sums[:, 4:5], sums[:, 3:4]))
            chain.link(nc.vector.tensor_tensor(gain, g, sums[:, 4:5], ALU.mult))
            chain.link(nc.vector.tensor_tensor(sums[:, 5:6], sums[:, 0:1], gain, ALU.mult))
            chain.link(nc.vector.tensor_tensor(shift, be, sums[:, 5:6], ALU.subtract))

        with ExitStack() as s1:
            edge_dst = tensor(s1, "edge_dst", [NCO, CO], I32)
            edge_dst16 = tensor(s1, "edge_dst16", [NCO, CO], I16)
            prev_last = tensor(s1, "prev_last", [NCO, 1], I32)
            prev_last_f = tensor(s1, "prev_last_f", [NCO, 1])
            m01 = tensor(s1, "m01", [NCO, CO], BF16)
            mbig = tensor(s1, "mbig", [NCO, CO], BF16)
            firsts = tensor(s1, "firsts", [NCO, CO // GRP])
            first_row = tensor(s1, "first_row", [1, NGRP])
            first_all = tensor(s1, "first_all", [P, NGRP])
            ones_row = tensor(s1, "ones_row", [1, P])
            node_i = tensor(s1, "node_i", [P, NI], I32)
            node_f = tensor(s1, "node_f", [P, NI])
            src_rows = tensor(s1, "src_rows", [P, 4, BLK], I32)
            src_rows_f = tensor(s1, "src_rows_f", [P, 4, BLK])
            floor_tile = tensor(s1, "floor_tile", [P, CO])
            smaller = tensor(s1, "smaller", [P, NS, GRP], BF16)
            signs = tensor(s1, "signs", [P, NS, NGRP], BF16)
            node_m = tensor(s1, "node_m", [P, NI])
            sign_sum = tensor(s1, "sign_sum", [P, NI])
            clamped = tensor(s1, "clamped", [P, NS])
            count = tensor(s1, "count", [P, NS])
            group_f = tensor(s1, "group_f", [P, NI])
            group_idx = tensor(s1, "group_idx", [P, NI], I32)
            entries = tensor(s1, "entries", [P, SLOTS, NS, GRP], I16)
            start_f = tensor(s1, "start_f", [P, NI])
            start2 = tensor(s1, "start2", [P, NI + 1])
            degree, skip, last_edge, spans = (tensor(s1, n, [P, NI]) for n in ("degree", "skip", "last_edge", "spans"))
            second = tensor(s1, "second", [P, NI])
            mids_f = tensor(s1, "mids_f", [P, 2])
            start_idx = tensor(s1, "start_idx", [P, NI], I32)
            mid_row = tensor(s1, "mid_row", [P, C])
            w_ab = tensor(s1, "w_ab", [P, 2 * C])
            b1_all = tensor(s1, "b1_all", [P, C])
            recv_sb = tensor(s1, "recv_sb", [P, NI, C])
            send_sb = tensor(s1, "send_sb", [P, NI, C])
            stats = tensor(s1, "stats", [P, NB, 6])
            small = tensor(s1, "small", [P, 8, NB])
            normed = tensor(s1, "normed", [P, 2, NB, C])
            normed_t = tensor(s1, "normed_t", [P, 2, NB // 2, P])
            ps_t = banks(s1, "ps_t", [P, 8, P])
            ps_ab = banks(s1, "ps_ab", [P, 2, 8, P])
            ps_src = banks(s1, "ps_src", [P, J, P])
            ps_first = banks(s1, "ps_first", [P, 512])

            consts = sem("consts")
            dst_in, src_in, x_in, w_in, mid_in = (sem(n) for n in ("dst_in", "src_in", "x_in", "w_in", "mid_in"))
            masks_made, masks_out = sem("masks_made"), sem("masks_out")
            dst16_made, groups_out = sem("dst16_made"), sem("groups_out")
            firsts_made, firsts_turned, row_made, firsts_spread = (
                sem(n) for n in ("firsts_made", "firsts_turned", "row_made", "firsts_spread"))
            src_f_made, src_turned, src_made = (sem(n) for n in ("src_f_made", "src_turned", "src_made"))
            nodes_numbered, firsts_ready, signs_summed = sem("nodes_numbered"), sem("firsts_ready"), sem("signs_summed")
            group_found, entries_in = sem("group_found"), [sem(f"entries_in{i}") for i in range(SLOTS)]
            start_made = sem("start_made")
            last_padded, firsts_shifted = sem("last_padded"), sem("firsts_shifted")
            floor_made, floor_out = sem("floor_made"), [sem(f"floor_out{i}") for i in range(2)]
            idx_made = sem("idx_made")
            scattered, mid_gathered, mid_out = sem("scattered"), sem("mid_gathered"), sem("mid_out")
            w_made = sem("w_made")
            var_made, dev_made, normed_made, normed_turned, normed_copied, ab_made = (
                sem(n) for n in ("var_made", "dev_made", "normed_made", "normed_turned", "normed_copied", "ab_made"))
            recv_made, send_made, tables_out = sem("recv_made"), sem("send_made"), sem("tables_out")

            pool_passed, dve_passed = sem("pool_passed1"), sem("dve_passed1")
            FILLS = EP * C // (P * CO)
            dst_padded, nodes_padded, src_padded = sem("dst_padded"), sem("nodes_padded"), sem("src_padded")
            block = s1.enter_context(nc.Block())

            @block.sync
            def _(sp):
                dst_v = dst[0:FULL_CO * CO].rearrange("(p c) -> p c", c=CO)
                cut = FULL_CO // 16 * 16
                sp.wait_ge(dst_padded, 2)
                sp.dma_start(edge_dst[0:cut, :], dst_v[0:cut, :]).then_inc(dst_in, 16)
                sp.dma_start(edge_dst[cut:FULL_CO, :], dst_v[cut:FULL_CO, :]).then_inc(dst_in, 16)
                sp.dma_start(edge_dst[FULL_CO:NCO, 0:E - FULL_CO * CO],
                             dst[FULL_CO * CO:E].rearrange("(p c) -> p c", p=1)).then_inc(dst_in, 16)
                with nc.allow_non_contiguous_dma(reason="one element per partition"):
                    sp.dma_start(prev_last[1:NCO, :], dst_v[:, CO - 1:CO]).then_inc(dst_in, 16)
                sp.wait_ge(dst16_made, 1)
                sp.dma_start(dst_groups.rearrange("(p g) f -> p (g f)", p=NCO), edge_dst16[:, :]).then_inc(groups_out, 16)
                sp.wait_ge(floor_made, 1)
                floor_v = recv_edges.rearrange("(n p r) c -> p n (r c)", p=P, r=CO // C)

                def fill(r, s):
                    at_least(sp, floor_out[s], 16 * r)
                    sp.dma_start(floor_v[:, bass.ds(r * 2 + s, 1), :].rearrange("p n c -> p (n c)"), floor_tile[:, :]).then_inc(floor_out[s], 16)

                pipeline(sp, FILLS, 2, [(0, fill)])
                sp.wait_ge(masks_made, 2)
                sp.dma_start(same_sum.rearrange("(p c) -> p c", c=CO), m01[:, :]).then_inc(masks_out, 16)
                sp.dma_start(same_max.rearrange("(p c) -> p c", c=CO), mbig[:, :]).then_inc(masks_out, 16)
                sp.wait_ge(mid_gathered, 16)
                sp.wait_ge(scattered, 16 * NI)
                sp.dma_start(recv_edges[1:2, :], mid_row[0:1, :]).then_inc(mid_out, 16)
                sp.wait_ge(mid_out, 16)
                sp.wait_ge(masks_out, 32)

            @block.gpsimd
            def _(pool):
                nc.gpsimd.iota(node_i[:, :], [[1, NI]], base=0, channel_multiplier=NI).then_inc(nodes_numbered, 1)
                pool.wait_ge(nodes_numbered, 1)
                nc.gpsimd.memset(nodes[96:P, :, :], 0.0).then_inc(nodes_padded, 1)
                pool.wait_ge(nodes_padded, 1)
                nc.gpsimd.memset(src_rows[:, 3, :], 0).then_inc(src_padded, 1)
                nc.gpsimd.memset(ident[:, :], 0.0).then_inc(consts, 1)
                nc.gpsimd.memset(sel2[:, :], 1.0).then_inc(consts, 1)
                pool.wait_ge(consts, 2)
                nc.gpsimd.affine_select(out=ident[:, :], in_=ident[:, :], compare_op=ALU.not_equal, fill=1.0, base=0,
                                        pattern=[[-1, P]], channel_multiplier=1).then_inc(consts, 1)
                nc.gpsimd.affine_select(out=sel2[:, :], in_=sel2[:, :], compare_op=ALU.is_ge, fill=0.0, base=0,
                                        pattern=[[1, P]], channel_multiplier=-C).then_inc(consts, 1)
                pool.wait_ge(consts, 4)
                nc.gpsimd.affine_select(out=sel2[:, :], in_=sel2[:, :], compare_op=ALU.is_ge, fill=0.0, base=C - 1,
                                        pattern=[[-1, P]], channel_multiplier=C).then_inc(consts, 1)
                pool.wait_ge(groups_out, 16)

                for k in range(SSTEP):
                    pool.wait_ge(group_found, k + 1)
                    at_least(pool, start_made, k - SLOTS + 1)
                    for i in range(NS):
                        col = k * NS + i
                        pool.indirect_dma_start(out=entries[:, k % SLOTS, i, :], out_offset=None, in_=dst_groups,
                                                in_offset=bass.IndirectOffsetOnAxis(ap=group_idx[:, col:col + 1], axis=0)
                                                ).then_inc(entries_in[k % SLOTS], 16)
                pool.wait_ge(idx_made, 1)
                pool.wait_ge(recv_made, NSTEP)
                for s in range(2):
                    pool.wait_ge(floor_out[s], 16 * (FILLS // 2))
                for i in range(NI):
                    pool.indirect_dma_start(out=recv_edges, out_offset=bass.IndirectOffsetOnAxis(ap=start_idx[:, i:i + 1], axis=0),
                                            in_=recv_sb[:, i, :], in_offset=None,
                                            bounds_check=EP - 1, oob_is_err=False).then_inc(scattered, 16)
                pool.wait_ge(tables_out, 32)
                pool.wait_ge(mid_in, 16)
                pool.indirect_dma_start(out=mid_row[:, :], out_offset=None, in_=recv_table,
                                        in_offset=bass.IndirectOffsetOnAxis(ap=mids[:, 1:2], axis=0)).then_inc(mid_gathered, 16)

            @block.tensor
            def _(pe):
                pe.wait_ge(consts, 3)
                pe.wait_ge(firsts_made, 1)
                for g in range(CO // GRP):
                    mm = nc.tensor.transpose(ps_first[0:1, g * NCO:(g + 1) * NCO], firsts[:, g:g + 1], ident[0:NCO, 0:NCO])
                mm.then_inc(firsts_turned, 1)
                pe.wait_ge(row_made, 2)
                nc.tensor.matmul(ps_first[:, 0:NGRP], ones_row[:, :], first_row[:, :], start=True, stop=True).then_inc(firsts_spread, 1)
                pe.wait_ge(w_made, 1)

                def turn(r, s):
                    k = r * 2 + s
                    at_least(pe, normed_made, NB * (k + 1))
                    at_least(pe, normed_copied, k)
                    for q in range(NB // 2):
                        mm = nc.tensor.transpose(ps_t[:, q, :], normed[:, s, 2 * q:2 * q + 2, :].rearrange("p a c -> p (a c)"), ident[:, :])
                    mm.then_inc(normed_turned, 1)

                def product(r, s):
                    k = r * 2 + s
                    at_least(pe, normed_copied, k + 1)
                    at_least(pe, recv_made, k)
                    at_least(pe, send_made, k)
                    for i in range(NB):
                        h = (i % 2) * C
                        mm = nc.tensor.matmul(ps_ab[:, i % 2, i // 2, :], normed_t[h:h + C, s, i // 2, :], w_ab[h:h + C, :], start=True, stop=True)
                    mm.then_inc(ab_made, 1)

                pipeline(pe, NSTEP, 2, [(0, turn), (1, product)])
                pe.wait_ge(start_made, SSTEP)
                nc.tensor.matmul(ps_first[0:P - 1, 0:1], ident[:, 1:P], start_f[:, 0:1], start=True, stop=True).then_inc(firsts_shifted, 1)
                for g in range(4):
                    rows = min(P, NBLK - g * P)
                    pe.wait_ge(src_f_made, g + 1)
                    at_least(pe, src_made, g)
                    for j in range(J):
                        mm = nc.tensor.transpose(ps_src[:, j, 0:rows], src_rows_f[0:rows, g, j::J], ident[0:rows, 0:rows])
                    mm.then_inc(src_turned, 1)

            @block.scalar
            def _(act):
                act.dma_start(mids[:, :], dst[MID - 1:MID + 1].partition_broadcast(P)).then_inc(mid_in, 16)
                for h in range(2):
                    act.dma_start(w_ab[h * C:(h + 1) * C, 0:C], W1[0:C, :]).then_inc(w_in, 16)
                    act.dma_start(w_ab[h * C:(h + 1) * C, C:2 * C], W1[C:2 * C, :]).then_inc(w_in, 16)
                act.dma_start(b1_all[:, :], b1.partition_broadcast(P)).then_inc(w_in, 16)
                act.wait_ge(nodes_padded, 1)
                x_v = x.rearrange("(p i) c -> p i c", i=NI)
                act.dma_start(nodes[0:112, :, :], x_v[0:112, :, :]).then_inc(x_in, 16)
                act.dma_start(nodes[112:NODE_P, :, :], x_v[112:NODE_P, :, :]).then_inc(x_in, 16)
                act.wait_ge(src_padded, 1)
                for g in range(4):
                    rows = min(P, LAST_BLK - g * P)
                    act.dma_start(src_rows[0:rows, g, :],
                                  src[g * P * BLK:(g * P + rows) * BLK].rearrange("(p c) -> p c", c=BLK)).then_inc(src_in, 16)
                act.dma_start(src_rows[LAST_BLK - 3 * P:NBLK - 3 * P, 3, 0:TAIL],
                              src[LAST_BLK * BLK:E].rearrange("(p c) -> p c", p=1)).then_inc(src_in, 16)

                act.wait_ge(firsts_ready, 2)

                def sum_signs(r, s):
                    k = r * SLOTS + s
                    at_least(act, signs_summed, NS * k)
                    for i in range(NS):
                        col = bass.ds(k * NS + i, 1)
                        nc.scalar.activation(signs[:, i, :], first_all[:, :], ACT.Sign, bias=node_m[:, col], scale=-1.0,
                                             accum_out=sign_sum[:, col]).then_inc(signs_summed, 1)

                def deviation(r, s):
                    if s % 2:
                        return
                    at_least(act, var_made, r * 2 + s // 2 + 1)
                    nc.scalar.activation(small[:, 3, :], small[:, 2, :], ACT.Sqrt).then_inc(dev_made, 1)

                def copy_turned(r, s):
                    if s % 2:
                        return
                    k, s = r * 2 + s // 2, s // 2
                    at_least(act, normed_turned, k + 1)
                    at_least(act, ab_made, k - 1)
                    nc.scalar.activation(normed_t[:, s, :, :], ps_t[:, 0:NB // 2, :], ACT.Relu).then_inc(normed_copied, 1)

                def copy_send(r, s):
                    if s % 2:
                        return
                    k = r * 2 + s // 2
                    at_least(act, ab_made, k + 1)
                    nc.scalar.copy(send_sb[:, bass.ds(k * NB, NB), :].rearrange("p (q h) c -> p q h c", h=2),
                                   ps_ab[:, :, 0:NB // 2, C:2 * C].rearrange("p h q c -> p q h c")).then_inc(send_made, 1)

                pipeline(act, SSTEP, SLOTS, [(0, sum_signs), (2, deviation), (2, copy_turned), (4, copy_send)])
                for s in range(2):
                    act.wait_ge(floor_out[s], 16 * (FILLS // 2))
                act.wait_ge(recv_made, NSTEP)
                act.dma_start(recv_table.rearrange("(p i) c -> p (i c)", i=NI), recv_sb[:, :, :].rearrange("p i c -> p (i c)")).then_inc(tables_out, 16)
                act.wait_ge(send_made, NSTEP)
                act.dma_start(send_table.rearrange("(p i) c -> p (i c)", i=NI), send_sb[:, :, :].rearrange("p i c -> p (i c)")).then_inc(tables_out, 16)
                act.wait_ge(tables_out, 32)

            @block.vector
            def _(dve):
                once = Chain(dve, sem("dve_once"))
                nc.vector.memset(prev_last[:, :], -1).then_inc(dst_padded, 1)
                nc.vector.memset(edge_dst[96:NCO, E - FULL_CO * CO:CO], PAD_DST).then_inc(dst_padded, 1)
                nc.vector.memset(floor_tile[:, :], -BIG).then_inc(floor_made, 1)
                nc.vector.memset(ones_row[:, :], 1.0).then_inc(row_made, 1)
                nc.vector.memset(start2[96:P, NI:NI + 1], float(E)).then_inc(last_padded, 1)
                dve.wait_ge(nodes_numbered, 1)
                once.inc(nc.vector.tensor_copy(node_f[:, :], node_i[:, :]))
                nc.vector.tensor_scalar(node_m[:, :], node_i[:, :], 0.5, None, ALU.subtract).then_inc(firsts_ready, 1)
                dve.wait_ge(dst_in, 64)
                nc.vector.tensor_copy(firsts[:, :], edge_dst[:, ::GRP]).then_inc(firsts_made, 1)
                nc.vector.tensor_copy(edge_dst16[:, :], edge_dst[:, :]).then_inc(dst16_made, 1)
                once.link(nc.vector.tensor_copy(prev_last_f[:, :], prev_last[:, :]))
                dve.wait_ge(firsts_turned, 1)
                nc.vector.tensor_copy(first_row[:, :].rearrange("a (p g) -> a p g", p=NCO),
                                      ps_first[0:1, 0:NGRP].rearrange("a (g p) -> a p g", p=NCO)).then_inc(row_made, 1)
                dve.wait_ge(dst16_made, 1)
                once.link(nc.vector.tensor_tensor(m01[:, 1:CO], edge_dst16[:, 1:CO], edge_dst16[:, 0:CO - 1], ALU.is_equal))
                nc.vector.tensor_tensor(m01[:, 0:1], edge_dst16[:, 0:1], prev_last_f[:, :], ALU.is_equal).then_inc(masks_made, 1)
                dve.wait_ge(firsts_spread, 1)
                nc.vector.tensor_copy(first_all[:, :], ps_first[:, 0:NGRP]).then_inc(firsts_ready, 1)
                group_chain = Chain(dve, sem("group_chain"), 2)
                entry_chain = Chain(dve, sem("entry_chain"), NS)
                norm_chain = Chain(dve, sem("norm_chain"), NORM_LINKS)

                def find_group(r, s):
                    k = r * SLOTS + s
                    part = bass.ds(k * NS, NS)
                    at_least(dve, signs_summed, NS * (k + 1))
                    group_chain.start(k)
                    group_chain.link(nc.vector.tensor_scalar(clamped[:, :], sign_sum[:, part], 2.0 - NGRP, 0.5, ALU.max, ALU.mult))
                    nc.vector.tensor_scalar(group_idx[:, part], clamped[:, :], NGRP / 2 - 1.0, None, ALU.add).then_inc(group_found, 1)
                    group_chain.link(nc.vector.tensor_scalar(group_f[:, part], clamped[:, :], NGRP / 2 - 1.0, None, ALU.add))
                    group_chain.end()

                def find_start(r, s):
                    k = r * SLOTS + s
                    at_least(dve, entries_in[s], 16 * NS * (r + 1))
                    at_least(dve, start_made, k)
                    entry_chain.start(k)
                    for i in range(NS):
                        entry_chain.inc(nc.vector.tensor_scalar(smaller[:, i, :], entries[:, s, i, :], node_f[:, bass.ds(k * NS + i, 1)], 0.0,
                                                                ALU.is_lt, ALU.add, accum_out=count[:, i:i + 1]))
                    entry_chain.wait()
                    entry_chain.end()
                    nc.vector.scalar_tensor_tensor(out=start_f[:, bass.ds(k * NS, NS)], in0=group_f[:, bass.ds(k * NS, NS)],
                                                   scalar=float(GRP), in1=count[:, :], op0=ALU.mult, op1=ALU.add).then_inc(start_made, 1)

                def norm(r, s):
                    if s % 2:
                        return
                    k, s = r * 2 + s // 2, s // 2
                    at_least_apart(dve, normed_turned, k - 1, dve_passed)
                    norm_step(norm_chain, k, stats, small, var_made, dev_made, normed_made, lambda i: normed[:, s, i, :])

                def add_bias(r, s):
                    if s % 2:
                        return
                    k = r * 2 + s // 2
                    at_least(dve, send_made, k + 1)
                    nc.vector.tensor_tensor(recv_sb[:, bass.ds(k * NB, NB), :].rearrange("p (q h) c -> p q h c", h=2),
                                            ps_ab[:, :, 0:NB // 2, 0:C].rearrange("p h q c -> p q h c"),
                                            b1_all[:, :].unsqueeze(1).unsqueeze(1).broadcast_to([P, NB // 2, 2, C]), ALU.add).then_inc(recv_made, 1)

                dve.wait_ge(w_in, 16 * 5)
                nc.vector.tensor_tensor(w_ab[:, 0:C], w_ab[:, 0:C], w_ab[:, C:2 * C], ALU.subtract).then_inc(w_made, 1)
                dve.wait_ge(x_in, 32)
                pipeline(dve, SSTEP, SLOTS, [(0, find_group), (3, find_start), (1, norm), (4, add_bias)])
                dve.wait_ge(masks_made, 1)
                nc.vector.tensor_scalar(mbig[:, :], m01[:, :], 2 * BIG, -BIG, ALU.mult, ALU.add).then_inc(masks_made, 1)

                def to_row(result, edges, add):
                    once.link(nc.vector.tensor_scalar(second[:, :], edges, MID - 0.5, float(1 - 2 * MID), ALU.is_gt, ALU.mult))
                    if add is not None:
                        once.link(nc.vector.tensor_tensor(second[:, :], second[:, :], add[:, :], ALU.add))
                    once.link(nc.vector.scalar_tensor_tensor(out=result[:, :], in0=edges, scalar=2.0, in1=second[:, :],
                                                             op0=ALU.mult, op1=ALU.add))

                dve.wait_ge(start_made, SSTEP)
                once.inc(nc.vector.tensor_copy(start2[:, 0:NI], start_f[:, :]))
                dve.wait_ge(firsts_shifted, 1)
                dve.wait_ge(last_padded, 1)
                once.link(nc.vector.tensor_copy(start2[0:P - 1, NI:NI + 1], ps_first[0:P - 1, 0:1]))
                once.link(nc.vector.tensor_tensor(degree[:, :], start2[:, 1:NI + 1], start2[:, 0:NI], ALU.subtract))
                once.link(nc.vector.tensor_scalar(has_edge[:, :], degree[:, :], 0.5, None, ALU.is_gt))
                once.link(nc.vector.tensor_scalar(skip[:, :], has_edge[:, :], -OUT_OF_RANGE, OUT_OF_RANGE, ALU.mult, ALU.add))
                to_row(skip, start2[:, 0:NI], skip)
                nc.vector.tensor_copy(start_idx[:, :], skip[:, :]).then_inc(idx_made, 1)
                nc.vector.tensor_copy(norm_deg[:, :, C], degree[:, :])
                once.link(nc.vector.tensor_scalar(last_edge[:, :], start2[:, 1:NI + 1], -1.0, 0.0, ALU.add, ALU.max))
                nc.vector.tensor_copy(end_idx[:, :], last_edge[:, :])
                to_row(last_edge, last_edge[:, :], None)
                nc.vector.tensor_copy(end_row[:, :], last_edge[:, :])
                dve.wait_ge(mid_in, 16)
                once.link(nc.vector.tensor_copy(mids_f[:, :], mids[:, :]))
                once.link(nc.vector.tensor_scalar(spans[:, :], node_f[:, :], mids_f[:, 0:1], None, ALU.is_equal))
                once.link(nc.vector.scalar_tensor_tensor(out=spans[:, :], in0=node_f[:, :], scalar=mids_f[:, 1:2],
                                                         in1=spans[:, :], op0=ALU.is_equal, op1=ALU.mult))
                nc.vector.tensor_scalar(spans_mid[:, :], spans[:, :], BIG, -BIG, ALU.mult, ALU.add)
                dve.wait_ge(src_in, 16 * 5)
                for g in range(4):
                    nc.vector.tensor_copy(src_rows_f[:, g, :], src_rows[:, g, :]).then_inc(src_f_made, 1)
                for g in range(4):
                    rows = min(P, NBLK - g * P)
                    dve.wait_ge(src_turned, g + 1)
                    nc.vector.tensor_copy(src_cols[:, g * P:g * P + rows, :],
                                          ps_src[:, :, 0:rows].rearrange("p j b -> p b j")).then_inc(src_made, 1)

        end_phase()

        with ExitStack() as s2:
            U = 4
            recv_in = tensor(s2, "recv_in", [P, U, J, 2 * C])
            mask_in = tensor(s2, "mask_in", [2, U, BLK], BF16)
            send_in = tensor(s2, "send_in", [P, U, J, 2, C])
            send_idx = tensor(s2, "send_idx", [P, 2, 2, 2 * J], I32)
            mask = tensor(s2, "mask", [P, 2, BLK])
            filled = tensor(s2, "filled", [P, 2, BLK])
            joined = tensor(s2, "joined", [P, 2, BLK])
            hidden = tensor(s2, "hidden", [P, 2, BLK])
            maxima = tensor(s2, "maxima", [P, 2, BLK])
            max_rows = tensor(s2, "max_rows", [P, U, J * 2 * C])
            w2_twice = tensor(s2, "w2_twice", [P, P])
            ps_recv = [banks(s2, f"ps_recv{b}", [P, BLK]) for b in range(2)]
            ps_send = [banks(s2, f"ps_send{b}", [P, BLK]) for b in range(2)]
            ps_mask = banks(s2, "ps_mask", [P, BLK])
            ps_msg = banks(s2, "ps_msg", [P, BLK])
            ps_back = [banks(s2, f"ps_back{b}", [P, J, P]) for b in range(2)]

            loaded = [sem(f"loaded{i}") for i in range(U)]
            gathered = [sem(f"gathered{i}") for i in range(U)]
            stored = [sem(f"stored{i}") for i in range(U)]
            (idx_copied, recv_turned, mask_spread, mask_copied, send_turned, fill_done, join_done, hidden_done, msg_done, max_done,
             back_turned, rows_made, w2_clear, w2_in) = (
                sem(n) for n in ("idx_copied", "recv_turned", "mask_spread", "mask_copied", "send_turned", "fill_done", "join_done",
                                     "hidden_done", "msg_done", "max_done", "back_turned", "rows_made", "w2_clear", "w2_in"))
            fill_start = sem("fill_start")
            pool_passed, dve_passed = sem("pool_passed2"), sem("dve_passed2")
            block = s2.enter_context(nc.Block())

            @block.sync
            def _(sp):
                recv_v = recv_edges.rearrange("(k p j t) c -> p k (j t c)", p=P, j=J, t=2)
                max_v = max_edges.rearrange("(k p j t) c -> p k (j t c)", p=P, j=J, t=2)
                mask_v = same_max.rearrange("(t k c) -> t k c", t=2, k=HB)
                sp.wait_ge(w2_clear, 1)
                for h in range(2):
                    sp.dma_start(w2_twice[h * C:(h + 1) * C, h * C:(h + 1) * C], W2).then_inc(w2_in, 16)

                def load(r, s):
                    k = r * U + s
                    at_least(sp, recv_turned, k - U + 1)
                    sp.dma_start(recv_in[:, s, :, :].rearrange("p j c -> p (j c)"), recv_v[:, bass.ds(k, 1), :].rearrange("p a f -> p (a f)")).then_inc(loaded[s], 16)
                    at_least(sp, mask_spread, k - U + 1)
                    sp.dma_start(mask_in[:, s, :], mask_v[:, bass.ds(k, 1), :].rearrange("t a c -> t (a c)")).then_inc(loaded[s], 16)

                def store(r, s):
                    k = r * U + s
                    at_least(sp, rows_made, k + 1)
                    sp.dma_start(max_v[:, bass.ds(k, 1), :].rearrange("p a f -> p (a f)"), max_rows[:, s, :]).then_inc(stored[s], 16)

                pipeline(sp, HB, U, [(0, load), (3, store)])
                for s in range(U):
                    sp.wait_ge(stored[s], 16 * (HB // U))

            @block.gpsimd
            def _(pool):
                cols = src_cols[:, :, :].rearrange("p (t k) j -> p t (k j)", t=2)
                nc.gpsimd.memset(w2_twice[:, :], 0.0).then_inc(w2_clear, 1)

                def gather(r, s):
                    k = r * U + s
                    if s % 2 == 0:
                        at_least(pool, gathered[s], 16 * 2 * J * r)
                        at_least(pool, gathered[s + 1], 16 * 2 * J * r)
                        nc.gpsimd.tensor_copy(send_idx[:, s // 2, :, :], cols[:, :, bass.ds(k * J, 2 * J)]).then_inc(idx_copied, 1)
                        at_least(pool, idx_copied, r * (U // 2) + s // 2 + 1)
                    at_least_apart(pool, send_turned, k - U + 1, pool_passed)
                    for t in range(2):
                        for j in range(J):
                            col = (s % 2) * J + j
                            pool.indirect_dma_start(out=send_in[:, s, j, t, :], out_offset=None, in_=send_table,
                                                    in_offset=bass.IndirectOffsetOnAxis(ap=send_idx[:, s // 2, t, col:col + 1], axis=0)
                                                    ).then_inc(gathered[s], 16)

                pipeline(pool, HB, U, [(0, gather)])

            @block.tensor
            def _(pe):
                def message(r, s):
                    k = r * U + s
                    at_least(pe, hidden_done, k + 1)
                    at_least(pe, max_done, k)
                    nc.tensor.matmul(ps_msg[:, :], w2_twice[:, :], hidden[:, s % 2, :], start=True, stop=True).then_inc(msg_done, 1)

                def turn_back(r, s):
                    k = r * U + s
                    at_least(pe, max_done, k + 1)
                    at_least(pe, rows_made, k - 1)
                    for j in range(J):
                        mm = nc.tensor.transpose(ps_back[s % 2][:, j, :], maxima[:, s % 2, j::J], ident[:, :])
                    mm.then_inc(back_turned, 1)

                def turn_in(r, s):
                    k = r * U + s
                    at_least(pe, loaded[s], 32 * (r + 1))
                    at_least(pe, fill_done, k - 1)
                    for j in range(J):
                        mm = nc.tensor.transpose(ps_recv[s % 2][:, j::J], recv_in[:, s, j, :], ident[:, :])
                    mm.then_inc(recv_turned, 1)
                    at_least(pe, mask_copied, k)
                    nc.tensor.matmul(ps_mask[:, :], sel2[:, :], mask_in[:, s, :], start=True, stop=True).then_inc(mask_spread, 1)
                    at_least(pe, gathered[s], 16 * 2 * J * (r + 1))
                    at_least(pe, join_done, k - 1)
                    for j in range(J):
                        mm = nc.tensor.transpose(ps_send[s % 2][:, j::J], send_in[:, s, j, :, :].rearrange("p t c -> p (t c)"), ident[:, :])
                    mm.then_inc(send_turned, 1)

                pe.wait_ge(w2_in, 32)
                pipeline(pe, HB, U, [(1, message), (2, turn_back), (0, turn_in)])

            @block.scalar
            def _(act):
                def copy_mask(r, s):
                    k = r * U + s
                    at_least(act, mask_spread, k + 1)
                    at_least(act, max_done, k - 1)
                    nc.scalar.copy(mask[:, s % 2, :], ps_mask[:, :]).then_inc(mask_copied, 1)

                def rows_out(r, s):
                    k = r * U + s
                    at_least(act, back_turned, k + 1)
                    at_least(act, stored[s], 16 * r)
                    nc.scalar.copy(max_rows[:, s, :], ps_back[s % 2][:, :, :].rearrange("p j q -> p (j q)")).then_inc(rows_made, 1)

                def relu(r, s):
                    k = r * U + s
                    at_least(act, join_done, k + 1)
                    at_least(act, msg_done, k - 1)
                    nc.scalar.activation(hidden[:, s % 2, :], joined[:, s % 2, :], ACT.Relu).then_inc(hidden_done, 1)

                pipeline(act, HB, U, [(0, copy_mask), (2, rows_out), (0, relu)])

            @block.vector
            def _(dve):
                nc.vector.memset(filled[:, 1, BLK - 1:BLK], -BIG).then_inc(fill_start, 1)
                nc.vector.memset(maxima[:, 1, BLK - 1:BLK], -BIG).then_inc(fill_start, 1)
                dve.wait_ge(fill_start, 2)

                def maximum(r, s):
                    k = r * U + s
                    at_least(dve, msg_done, k + 1)
                    at_least(dve, back_turned, k - 1)
                    at_least(dve, max_done, k)
                    nc.vector.tensor_tensor_scan(maxima[:, s % 2, :], mask[:, s % 2, :], ps_msg[:, :],
                                                 maxima[:, 1 - s % 2, BLK - 1:BLK], ALU.min, ALU.max).then_inc(max_done, 1)

                def fill(r, s):
                    k = r * U + s
                    at_least(dve, recv_turned, k + 1)
                    at_least(dve, mask_copied, k + 1)
                    at_least(dve, fill_done, k)
                    nc.vector.tensor_tensor_scan(filled[:, s % 2, :], mask[:, s % 2, :], ps_recv[s % 2][:, :],
                                                 filled[:, 1 - s % 2, BLK - 1:BLK], ALU.min, ALU.max).then_inc(fill_done, 1)

                def join(r, s):
                    k = r * U + s
                    at_least(dve, send_turned, k + 1)
                    at_least(dve, fill_done, k + 1)
                    at_least(dve, hidden_done, k - 1)
                    nc.vector.tensor_tensor(joined[:, s % 2, :], filled[:, s % 2, :], ps_send[s % 2][:, :], ALU.add).then_inc(join_done, 1)

                pipeline(dve, HB, U, [(1, maximum), (0, fill), (0, join)])

        end_phase()

        with ExitStack() as s3:
            max_in = tensor(s3, "max_in", [P, 2, NB, C])
            node_idx = tensor(s3, "node_idx", [P, 2, NB], I32)
            mid_max = tensor(s3, "mid_max", [P, C])
            b2_all = tensor(s3, "b2_all", [P, C])
            with_mid = tensor(s3, "with_mid", [P, NB, C])
            stats = tensor(s3, "stats3", [P, NB, 6])
            small = tensor(s3, "small3", [P, 8, NB])
            normed = tensor(s3, "normed3", [P, 2, NB, C])
            table_rows = tensor(s3, "table_rows", [P, 2, NB, C])
            max_got = [sem(f"max_got{i}") for i in range(2)]
            table_out = [sem(f"table_out{i}") for i in range(2)]
            idx_copied, mid_in, max_used, var_made, dev_made, normed_made, relu_made, kept = (
                sem(n) for n in ("idx_copied3", "mid_in3", "max_used", "var_made3", "dev_made3", "normed_made3", "relu_made3", "kept"))
            pool_passed, dve_passed = sem("pool_passed3"), sem("dve_passed3")
            block = s3.enter_context(nc.Block())

            @block.sync
            def _(sp):
                table_v = norm_table.rearrange("(p i) c -> p i c", i=NI)
                sp.dma_start(mid_max[:, :], max_edges[2 * (MID - 1):2 * MID - 1, :].rearrange("a c -> (a c)").partition_broadcast(P)).then_inc(mid_in, 16)
                sp.dma_start(b2_all[:, :], b2.partition_broadcast(P)).then_inc(mid_in, 16)

                def store(r, s):
                    k = r * 2 + s
                    at_least(sp, relu_made, k + 1)
                    sp.dma_start(table_v[:, bass.ds(k * NB, NB), :], table_rows[:, s, :, :]).then_inc(table_out[s], 16)

                pipeline(sp, NSTEP, 2, [(0, store)])
                for s in range(2):
                    sp.wait_ge(table_out[s], 16 * (NSTEP // 2))

            @block.gpsimd
            def _(pool):
                def gather(r, s):
                    k = r * 2 + s
                    at_least(pool, max_got[s], 16 * NB * r)
                    nc.gpsimd.tensor_copy(node_idx[:, s, :], end_row[:, bass.ds(k * NB, NB)]).then_inc(idx_copied, 1)
                    at_least(pool, idx_copied, k + 1)
                    at_least_apart(pool, max_used, k - 1, pool_passed)
                    for i in range(NB):
                        pool.indirect_dma_start(out=max_in[:, s, i, :], out_offset=None, in_=max_edges,
                                                in_offset=bass.IndirectOffsetOnAxis(ap=node_idx[:, s, i:i + 1], axis=0)).then_inc(max_got[s], 16)

                pipeline(pool, NSTEP, 2, [(0, gather)])

            @block.scalar
            def _(act):
                def step(r, s):
                    k = r * 2 + s
                    at_least(act, var_made, k + 1)
                    nc.scalar.activation(small[:, 3, :], small[:, 2, :], ACT.Sqrt).then_inc(dev_made, 1)
                    at_least(act, normed_made, NB * (k + 1))
                    at_least(act, table_out[s], 16 * r)
                    nc.scalar.activation(table_rows[:, s, :, :], normed[:, s, :, :], ACT.Relu).then_inc(relu_made, 1)
                    nc.scalar.activation(norm_deg[:, bass.ds(k * NB, NB), 0:C], normed[:, s, :, :], ACT.Relu).then_inc(kept, 1)

                pipeline(act, NSTEP, 2, [(0, step)])

            @block.vector
            def _(dve):
                dve.wait_ge(mid_in, 32)
                join_chain = Chain(dve, sem("join_chain"), 4)
                norm_chain = Chain(dve, sem("norm_chain3"), NORM_LINKS)

                def step(r, s):
                    k = r * 2 + s
                    cols = bass.ds(k * NB, NB)
                    at_least(dve, max_got[s], 16 * NB * (r + 1))
                    join_chain.start(k)
                    join_chain.link(nc.vector.tensor_tensor(with_mid[:, :, :], mid_max[:, :].unsqueeze(1).broadcast_to([P, NB, C]),
                                                            spans_mid[:, cols].unsqueeze(2).broadcast_to([P, NB, C]), ALU.add))
                    nc.vector.tensor_tensor(with_mid[:, :, :], max_in[:, s, :, :], with_mid[:, :, :], ALU.max).then_inc(max_used, 1)
                    at_least(dve, max_used, k + 1)
                    join_chain.link(nc.vector.tensor_tensor(with_mid[:, :, :], with_mid[:, :, :],
                                                            b2_all[:, :].unsqueeze(1).broadcast_to([P, NB, C]), ALU.add))
                    join_chain.link(nc.vector.tensor_tensor(with_mid[:, :, :], with_mid[:, :, :],
                                                            has_edge[:, cols].unsqueeze(2).broadcast_to([P, NB, C]), ALU.mult))
                    join_chain.link(nc.vector.tensor_tensor(nodes[:, cols, :], nodes[:, cols, :], with_mid[:, :, :], ALU.add))
                    join_chain.end()
                    at_least_apart(dve, kept, k - 1, dve_passed)
                    norm_step(norm_chain, k, stats, small, var_made, dev_made, normed_made, lambda i: normed[:, s, i, :])

                pipeline(dve, NSTEP, 2, [(0, step)])

        end_phase()

        keep = stack.enter_context(ExitStack())
        gain = tensor(keep, "gain", [P, 2])
        shift = tensor(keep, "shift", [P, 2])
        with ExitStack() as s4:
            U = 8
            edge_in = tensor(s4, "edge_in", [P, U, J, C])
            pairs = tensor(s4, "pairs", [P, U, J, 2 * C])
            send_idx = tensor(s4, "send_idx4", [P, 2, U // 2 * J], I32)
            pairs_t = tensor(s4, "pairs_t", [P, 2, BLK])
            hid = tensor(s4, "hid", [P, U // 2, 2, BLK])
            stats = tensor(s4, "stats4", [P, NBLK, 6])
            w1a = tensor(s4, "w1a", [P, HID])
            vec = tensor(s4, "vec4", [P, 3])
            sums = tensor(s4, "sums4", [P, 6])
            ps_pairs = [banks(s4, f"ps_pairs{b}", [P, BLK]) for b in range(2)]
            ps_hid = [banks(s4, f"ps_hid{b}", [P, BLK]) for b in range(2)]
            loaded = [sem(f"loaded4_{i}") for i in range(U)]
            gathered = [sem(f"gathered4_{i}") for i in range(U)]
            stored = [sem(f"stored4_{i}") for i in range(U // 2)]
            idx_copied, w_in, turned, copied, multiplied, hid_made, stats_made, root_ready, root_made = (
                sem(n + "4") for n in ("idx_copied", "w_in", "turned", "copied", "multiplied", "hid_made", "stats_made", "root_ready", "root_made"))
            edge_copied = sem("edge_copied")
            pool_passed, dve_passed = sem("pool_passed4"), sem("dve_passed4")
            block = s4.enter_context(nc.Block())

            @block.sync
            def _(sp):
                attr_v = edge_attr[0:LAST_BLK * BLK, :].rearrange("(k p j) c -> p k (j c)", p=P, j=J)
                hid_v = hid_edges.rearrange("k p c -> p k c")
                sp.dma_start(w1a[:, :], W1a).then_inc(w_in, 16)
                with nc.allow_non_contiguous_dma(reason="one element per partition"):
                    for n, v in enumerate((b1a, g1a, be1a)):
                        sp.dma_start(vec[:, n:n + 1], v.rearrange("(p a) -> p a", a=1)).then_inc(w_in, 16)

                def load(r, s):
                    k = r * U + s
                    at_least(sp, edge_copied, k - U + 1)
                    if isinstance(k, int) and k == LAST_BLK:
                        sp.dma_start(edge_in[0:TAIL // J, s, :, :].rearrange("p j c -> p (j c)"), edge_attr[LAST_BLK * BLK:E, :].rearrange("(p j) c -> p (j c)", j=J)).then_inc(loaded[s], 16)
                    else:
                        sp.dma_start(edge_in[:, s, :, :].rearrange("p j c -> p (j c)"), attr_v[:, bass.ds(k, 1), :].rearrange("p a f -> p (a f)")).then_inc(loaded[s], 16)

                def store(r, s):
                    if s % 2 == 0:
                        return
                    at_least(sp, hid_made, r * U + s + 1)
                    sp.dma_start(hid_v[:, bass.ds(r * (U // 2) + s // 2, 1), :].rearrange("p a f -> p (a f)"),
                                 hid[:, s // 2, :, :].rearrange("p b q -> p (b q)")).then_inc(stored[s // 2], 16)

                pipeline(sp, NBLK, U, [(0, load), (5, store)])
                for q in range(U // 2):
                    sp.wait_ge(stored[q], 16 * (NBLK // U))

            @block.gpsimd
            def _(pool):
                cols = src_cols[:, :, :].rearrange("p k j -> p (k j)")
                H = U // 2

                def gather(r, s):
                    k = r * U + s
                    if s % H == 0:
                        for q in range(s, s + H):
                            at_least(pool, gathered[q], 16 * J * r)
                        nc.gpsimd.tensor_copy(send_idx[:, s // H, :], cols[:, bass.ds(k * J, H * J)]).then_inc(idx_copied, 1)
                        at_least(pool, idx_copied, r * 2 + s // H + 1)
                    at_least_apart(pool, turned, k - U + 1, pool_passed)
                    for j in range(J):
                        col = (s % H) * J + j
                        pool.indirect_dma_start(out=pairs[:, s, j, 0:C], out_offset=None, in_=norm_table,
                                                in_offset=bass.IndirectOffsetOnAxis(ap=send_idx[:, s // H, col:col + 1], axis=0)
                                                ).then_inc(gathered[s], 16)

                pipeline(pool, NBLK, U, [(0, gather)])

            @block.tensor
            def _(pe):
                def turn(r, s):
                    k = r * U + s
                    at_least(pe, edge_copied, k + 1)
                    at_least(pe, gathered[s], 16 * J * (r + 1))
                    at_least(pe, copied, k - 1)
                    for j in range(J):
                        mm = nc.tensor.transpose(ps_pairs[s % 2][:, j::J], pairs[:, s, j, :], ident[:, :])
                    mm.then_inc(turned, 1)

                def product(r, s):
                    k = r * U + s
                    at_least(pe, copied, k + 1)
                    at_least(pe, hid_made, k - 1)
                    nc.tensor.matmul(ps_hid[s % 2][:, :], w1a[:, :], pairs_t[:, s % 2, :], start=True, stop=True).then_inc(multiplied, 1)

                pe.wait_ge(w_in, 64)
                pipeline(pe, NBLK, U, [(0, turn), (1, product)])

            @block.scalar
            def _(act):
                def copy(r, s):
                    k = r * U + s
                    at_least(act, turned, k + 1)
                    at_least(act, multiplied, k - 1)
                    nc.scalar.copy(pairs_t[:, s % 2, :], ps_pairs[s % 2][:, :]).then_inc(copied, 1)

                def copy_edge(r, s):
                    k = r * U + s
                    at_least(act, loaded[s], 16 * (r + 1))
                    at_least(act, turned, k - U + 1)
                    nc.scalar.copy(pairs[:, s, :, C:2 * C], edge_in[:, s, :, :]).then_inc(edge_copied, 1)

                pipeline(act, NBLK, U, [(0, copy_edge), (1, copy)])
                act.wait_ge(root_ready, 1)
                nc.scalar.activation(sums[:, 3:4], sums[:, 2:3], ACT.Sqrt).then_inc(root_made, 1)

            @block.vector
            def _(dve):
                def finish(r, s):
                    k = r * U + s
                    at_least(dve, multiplied, k + 1)
                    at_least(dve, stored[s // 2], 16 * r)
                    part = hid[:, s // 2, s % 2, :]
                    nc.vector.tensor_scalar(part, ps_hid[s % 2][:, :], vec[:, 0:1], None, ALU.add).then_inc(hid_made, 1)
                    at_least_apart(dve, hid_made, k + 1, dve_passed)
                    valid = TAIL if isinstance(k, int) and k == LAST_BLK else BLK
                    nc.vector.bn_stats(stats[:, bass.ds(k, 1), :].rearrange("p a q -> p (a q)"), part[:, 0:valid]).then_inc(stats_made, 1)

                dve.wait_ge(w_in, 64)
                pipeline(dve, NBLK, U, [(0, finish)])
                dve.wait_ge(stats_made, NBLK)
                affine_of_norm(Chain(dve, sem("affine4")), root_ready, root_made, stats[:, :, :].rearrange("p k q -> p (k q)"),
                               sums, gain[:, 0:1], shift[:, 0:1], vec[:, 1:2], vec[:, 2:3])

        end_phase()

        with ExitStack() as s5:
            U = 8
            R = 4
            STEP = 2 * BLK
            JS = STEP // P
            STEPS = EP // STEP
            hid = tensor(s5, "hid5", [P, U, STEP])
            mask_in = tensor(s5, "mask_in5", [1, U, STEP], BF16)
            ones5 = tensor(s5, "ones5", [1, P], BF16)
            act_out = tensor(s5, "act_out", [P, 2, STEP])
            total = tensor(s5, "total", [P, 2, STEP])
            rows = tensor(s5, "rows5", [P, R, JS * HID])
            ps_mask = [banks(s5, f"ps_mask5_{b}", [P, STEP]) for b in range(2)]
            ps_back = [banks(s5, f"ps_back5_{b}", [P, JS * HID]) for b in range(2)]
            loaded = [sem(f"loaded5_{i}") for i in range(U)]
            stored = [sem(f"stored5_{i}") for i in range(R)]
            begun, mask_spread, relu_done, sum_done, back_turned, rows_made = (
                sem(n + "5") for n in ("begun", "mask_spread", "relu_done", "sum_done", "back_turned", "rows_made"))
            block = s5.enter_context(nc.Block())

            @block.sync
            def _(sp):
                hid_v = hid_edges.rearrange("k p c -> p k c")
                mask_v = same_sum.rearrange("(a k c) -> a k c", a=1, k=STEPS)
                sum_v = sum_edges.rearrange("(k p j) c -> p k (j c)", p=P, j=JS)

                def load(r, s):
                    k = r * U + s
                    at_least(sp, relu_done, k - U + 1)
                    sp.dma_start(hid[:, s, :], hid_v[:, bass.ds(k, 1), :].rearrange("p a f -> p (a f)")).then_inc(loaded[s], 16)
                    at_least(sp, mask_spread, k - U + 1)
                    sp.dma_start(mask_in[:, s, :], mask_v[:, bass.ds(k, 1), :].rearrange("t a c -> t (a c)")).then_inc(loaded[s], 16)

                def store(r, s):
                    k = r * U + s
                    at_least(sp, rows_made, k + 1)
                    sp.dma_start(sum_v[:, bass.ds(k, 1), :].rearrange("p a f -> p (a f)"), rows[:, s % R, :]).then_inc(stored[s % R], 16)

                pipeline(sp, STEPS, U, [(0, load), (U, store)])
                for s in range(R):
                    sp.wait_ge(stored[s], 16 * (STEPS // R))

            @block.tensor
            def _(pe):
                def spread(r, s):
                    k = r * U + s
                    at_least(pe, loaded[s], 32 * (r + 1))
                    at_least(pe, sum_done, k - 1)
                    for a in range(0, STEP, BLK):
                        mm = nc.tensor.matmul(ps_mask[s % 2][:, a:a + BLK], ones5[:, :], mask_in[:, s, a:a + BLK], start=True, stop=True)
                    mm.then_inc(mask_spread, 1)

                def turn_back(r, s):
                    k = r * U + s
                    at_least(pe, sum_done, k + 1)
                    at_least(pe, rows_made, k - 1)
                    for j in range(JS):
                        mm = nc.tensor.transpose(ps_back[s % 2][:, j * P:(j + 1) * P], total[:, s % 2, j::JS], ident[:, :])
                    mm.then_inc(back_turned, 1)

                pe.wait_ge(begun, 2)
                pipeline(pe, STEPS, U, [(0, spread), (1, turn_back)])

            @block.scalar
            def _(act):
                def relu(r, s):
                    k = r * U + s
                    at_least(act, loaded[s], 32 * (r + 1))
                    at_least(act, sum_done, k - 1)
                    nc.scalar.activation(act_out[:, s % 2, :], hid[:, s, :], ACT.Relu, bias=shift[:, 0:1], scale=gain[:, 0:1]).then_inc(relu_done, 1)

                def rows_out(r, s):
                    k = r * U + s
                    at_least(act, back_turned, k + 1)
                    at_least(act, stored[s % R], 16 * (r * (U // R) + s // R))
                    nc.scalar.copy(rows[:, s % R, :], ps_back[s % 2][:, :]).then_inc(rows_made, 1)

                pipeline(act, STEPS, U, [(0, relu), (1, rows_out)])

            @block.vector
            def _(dve):
                nc.vector.memset(total[:, 1, STEP - 1:STEP], 0.0).then_inc(begun, 1)
                nc.vector.memset(ones5[:, :], 1.0).then_inc(begun, 1)
                dve.wait_ge(begun, 2)

                def running_sum(r, s):
                    k = r * U + s
                    at_least(dve, mask_spread, k + 1)
                    at_least(dve, relu_done, k + 1)
                    at_least(dve, back_turned, k - 1)
                    at_least(dve, sum_done, k)
                    nc.vector.tensor_tensor_scan(total[:, s % 2, :], ps_mask[s % 2][:, :], act_out[:, s % 2, :],
                                                 total[:, 1 - s % 2, STEP - 1:STEP], ALU.mult, ALU.add).then_inc(sum_done, 1)

                pipeline(dve, STEPS, U, [(0, running_sum)])

        end_phase()

        with ExitStack() as s6:
            NC = 5
            STEPS = NI // NC
            sum_in = tensor(s6, "sum_in", [P, 2, NC, HID])
            node_idx = tensor(s6, "node_idx6", [P, 2, NC], I32)
            sum_kept = tensor(s6, "sum_kept", [P, 2, NC, HID])
            norm_in = tensor(s6, "norm_in", [P, 2, NC, C + 1])
            sum_t = tensor(s6, "sum_t", [P, 2, NC * P])
            norm_t = tensor(s6, "norm_t", [C + 1, 2, NC * P])
            hid2 = tensor(s6, "hid2", [P, NI * P])
            stats = tensor(s6, "stats6", [P, 2 * STEPS, 6])
            vec = tensor(s6, "vec6", [P, 3])
            b2b_all = tensor(s6, "b2b_all", [P, C])
            w2a = tensor(s6, "w2a", [P, HID])
            w2a_t = tensor(s6, "w2a_t", [P, HID])
            w1b_low = tensor(s6, "w1b_low", [P, HID])
            w1b_top = tensor(s6, "w1b_top", [C + 1, HID])
            b2a_col = tensor(s6, "b2a_col", [P, C + 1])
            w_sum = tensor(s6, "w_sum", [P, HID])
            w_norm = tensor(s6, "w_norm", [C + 1, HID])
            w2b = tensor(s6, "w2b", [P, C])
            sums = tensor(s6, "sums6", [P, 6])
            active = tensor(s6, "active", [P, 2, NC, P])
            partial = tensor(s6, "partial", [P, 2, NC, C])
            result = tensor(s6, "result", [P, 2, NC, C])
            ps_sum = banks(s6, "ps_sum", [P, 8, P])
            ps_norm = banks(s6, "ps_norm", [P, 8, P])
            ps_hid = banks(s6, "ps_hid6", [P, 8 * P])
            ps_out = [banks(s6, f"ps_out{b}", [P, 8, C]) for b in range(2)]
            sum_got = [sem(f"sum_got{i}") for i in range(2)]
            out_done = [sem(f"out_done{i}") for i in range(2)]
            (cleared, w_in, w_turned, w_copied, w_multiplied, w_ready, idx_copied, sum_scaled, norm_copied, both_turned, sum_copied,
             norm_t_copied, multiplied, hid_made, stats_made, root_ready, root_made, affine_ready, relu_done, out_multiplied,
             partial_made, result_made) = (
                sem(n + "6") for n in ("cleared", "w_in", "w_turned", "w_copied", "w_multiplied", "w_ready", "idx_copied", "sum_scaled",
                                           "norm_copied", "both_turned", "sum_copied", "norm_t_copied", "multiplied", "hid_made",
                                           "stats_made", "root_ready", "root_made", "affine_ready", "relu_done", "out_multiplied",
                                           "partial_made", "result_made"))
            pool_passed, dve_passed = sem("pool_passed6"), sem("dve_passed6")
            block = s6.enter_context(nc.Block())

            @block.sync
            def _(sp):
                sp.dma_start(w2a[:, :], W2a).then_inc(w_in, 16)
                sp.dma_start(w1b_low[:, :], W1b[C:C + HID, :]).then_inc(w_in, 16)
                sp.dma_start(w2b[:, :], W2b).then_inc(w_in, 16)
                sp.dma_start(b2b_all[:, :], b2b.partition_broadcast(P)).then_inc(w_in, 16)
                with nc.allow_non_contiguous_dma(reason="one element per partition"):
                    for n, v in enumerate((b1b, g1b, be1b)):
                        sp.dma_start(vec[:, n:n + 1], v.rearrange("(p a) -> p a", a=1)).then_inc(w_in, 16)
                    sp.wait_ge(cleared, 2)
                    sp.dma_start(w1b_top[0:C, :], W1b[0:C, :]).then_inc(w_in, 16)
                    sp.dma_start(b2a_col[:, C:C + 1], b2a.rearrange("(p a) -> p a", a=1)).then_inc(w_in, 16)
                out_v = out.rearrange("(p i) c -> p i c", i=NI)

                def store(r, s):
                    k = r * 2 + s
                    at_least(sp, result_made, k + 1)
                    sp.dma_start(out_v[:, bass.ds(k * NC, NC), :], result[0:NODE_P, s, :, :]).then_inc(out_done[s], 16)

                pipeline(sp, STEPS, 2, [(0, store)])
                for s in range(2):
                    sp.wait_ge(out_done[s], 16 * (STEPS // 2))

            @block.gpsimd
            def _(pool):
                nc.gpsimd.memset(w1b_top[:, :], 0.0).then_inc(cleared, 1)
                nc.gpsimd.memset(b2a_col[:, :], 0.0).then_inc(cleared, 1)

                def gather(r, s):
                    k = r * 2 + s
                    at_least(pool, sum_got[s], 16 * NC * r)
                    nc.gpsimd.tensor_copy(node_idx[:, s, :], end_idx[:, bass.ds(k * NC, NC)]).then_inc(idx_copied, 1)
                    at_least(pool, idx_copied, k + 1)
                    at_least_apart(pool, sum_scaled, k - 1, pool_passed)
                    for i in range(NC):
                        pool.indirect_dma_start(out=sum_in[:, s, i, :], out_offset=None, in_=sum_edges,
                                                in_offset=bass.IndirectOffsetOnAxis(ap=node_idx[:, s, i:i + 1], axis=0)).then_inc(sum_got[s], 16)

                pipeline(pool, STEPS, 2, [(0, gather)])

            @block.tensor
            def _(pe):
                pe.wait_ge(w_in, 16 * 9)
                nc.tensor.transpose(ps_sum[:, 0, :], w2a[:, :], ident[:, :]).then_inc(w_turned, 1)
                pe.wait_ge(w_copied, 1)
                nc.tensor.matmul(ps_hid[:, 0:HID], w2a_t[:, :], w1b_low[:, :], start=True, stop=True).then_inc(w_multiplied, 1)
                nc.tensor.matmul(ps_norm[0:C + 1, 0, :], b2a_col[:, :], w1b_low[:, :], start=True, stop=True).then_inc(w_multiplied, 1)
                pe.wait_ge(w_ready, 2)

                def turn(r, s):
                    k = r * 2 + s
                    at_least(pe, sum_scaled, k + 1)
                    at_least(pe, sum_copied, k)
                    for i in range(NC):
                        nc.tensor.transpose(ps_sum[:, i, :], sum_kept[:, s, i, :], ident[:, :])
                    at_least(pe, norm_copied, k + 1)
                    at_least(pe, norm_t_copied, k)
                    for i in range(NC):
                        mm = nc.tensor.transpose(ps_norm[0:C + 1, i, :], norm_in[:, s, i, :], ident[:, :])
                    mm.then_inc(both_turned, 1)

                def product(r, s):
                    k = r * 2 + s
                    at_least(pe, sum_copied, k + 1)
                    at_least(pe, norm_t_copied, k + 1)
                    at_least(pe, hid_made, k)
                    for a, b in ((0, 512), (512, NC * P)):
                        nc.tensor.matmul(ps_hid[:, a:b], w_sum[:, :], sum_t[:, s, a:b], start=True, stop=False)
                        mm = nc.tensor.matmul(ps_hid[:, a:b], w_norm[:, :], norm_t[:, s, a:b], start=False, stop=True)
                    mm.then_inc(multiplied, 1)

                pipeline(pe, STEPS, 2, [(1, product), (0, turn)])

                def last_product(r, s):
                    k = r * 2 + s
                    at_least(pe, relu_done, k + 1)
                    at_least(pe, partial_made, k - 1)
                    for i in range(NC):
                        mm = nc.tensor.matmul(ps_out[s][:, i, :], active[:, s, i, :], w2b[:, :], start=True, stop=True)
                    mm.then_inc(out_multiplied, 1)

                pipeline(pe, STEPS, 2, [(0, last_product)])

            @block.scalar
            def _(act):
                act.wait_ge(w_turned, 1)
                nc.scalar.copy(w2a_t[:, :], ps_sum[:, 0, :]).then_inc(w_copied, 1)
                act.wait_ge(w_multiplied, 2)
                nc.scalar.copy(w_sum[:, :], ps_hid[:, 0:HID]).then_inc(w_ready, 1)

                def copy_norm(r, s):
                    k = r * 2 + s
                    at_least(act, both_turned, k - 1)
                    nc.scalar.copy(norm_in[:, s, :, :], norm_deg[:, bass.ds(k * NC, NC), :]).then_inc(norm_copied, 1)

                def copy_sum(r, s):
                    k = r * 2 + s
                    at_least(act, both_turned, k + 1)
                    at_least(act, multiplied, k - 1)
                    nc.scalar.copy(sum_t[:, s, :], ps_sum[:, 0:NC, :].rearrange("p i q -> p (i q)")).then_inc(sum_copied, 1)

                pipeline(act, STEPS, 2, [(0, copy_norm), (1, copy_sum)])
                act.wait_ge(root_ready, 1)
                nc.scalar.activation(sums[:, 3:4], sums[:, 2:3], ACT.Sqrt).then_inc(root_made, 1)
                act.wait_ge(affine_ready, 1)

                def relu(r, s):
                    k = r * 2 + s
                    at_least(act, out_multiplied, k - 1)
                    nc.scalar.activation(active[:, s, :, :].rearrange("p i q -> p (i q)"), hid2[:, bass.ds(k * NC * P, NC * P)], ACT.Relu,
                                         bias=shift[:, 1:2], scale=gain[:, 1:2]).then_inc(relu_done, 1)

                pipeline(act, STEPS, 2, [(0, relu)])

            @block.vector
            def _(dve):
                dve.wait_ge(w_multiplied, 2)
                nc.vector.tensor_tensor(w_norm[:, :], ps_norm[0:C + 1, 0, :], w1b_top[:, :], ALU.add).then_inc(w_ready, 1)

                def scale(r, s):
                    k = r * 2 + s
                    at_least(dve, sum_got[s], 16 * NC * (r + 1))
                    at_least(dve, both_turned, k - 1)
                    nc.vector.tensor_tensor(sum_kept[:, s, :, :], sum_in[:, s, :, :],
                                            has_edge[:, bass.ds(k * NC, NC)].unsqueeze(2).broadcast_to([P, NC, HID]), ALU.mult).then_inc(sum_scaled, 1)

                def copy_norm_t(r, s):
                    k = r * 2 + s
                    at_least(dve, both_turned, k + 1)
                    at_least(dve, multiplied, k - 1)
                    nc.vector.tensor_copy(norm_t[:, s, :], ps_norm[0:C + 1, 0:NC, :].rearrange("p i q -> p (i q)")).then_inc(norm_t_copied, 1)

                def finish(r, s):
                    k = r * 2 + s
                    at_least(dve, multiplied, k + 1)
                    part = hid2[:, bass.ds(k * NC * P, NC * P)]
                    nc.vector.tensor_scalar(part, ps_hid[:, 0:NC * P], vec[:, 0:1], None, ALU.add).then_inc(hid_made, 1)
                    at_least_apart(dve, hid_made, k + 1, dve_passed)
                    cols = part.rearrange("p (i q) -> p i q", q=P)[:, :, 0:NODE_P]
                    nc.vector.bn_stats(stats[:, bass.ds(2 * k, 1), :].rearrange("p a q -> p (a q)"), cols[:, 0:2, :]).then_inc(stats_made, 1)
                    nc.vector.bn_stats(stats[:, bass.ds(2 * k + 1, 1), :].rearrange("p a q -> p (a q)"), cols[:, 2:NC, :]).then_inc(stats_made, 1)

                pipeline(dve, STEPS, 2, [(0, scale), (1, copy_norm_t), (2, finish)])
                dve.wait_ge(stats_made, 2 * STEPS)
                affine_of_norm(Chain(dve, sem("affine6")), root_ready, root_made, stats[:, :, :].rearrange("p k q -> p (k q)"),
                               sums, gain[:, 1:2], shift[:, 1:2], vec[:, 1:2], vec[:, 2:3])
                nc.vector.memset(sums[:, 5:6], 0.0).then_inc(affine_ready, 1)

                def partial_step(r, s):
                    k = r * 2 + s
                    at_least(dve, out_multiplied, k + 1)
                    nc.vector.tensor_tensor(partial[:, s, :, :], ps_out[s][:, 0:NC, :], nodes[:, bass.ds(k * NC, NC), :], ALU.add).then_inc(partial_made, 1)
                    at_least(dve, partial_made, k + 1)
                    at_least(dve, out_done[s], 16 * r)
                    nc.vector.tensor_tensor(result[:, s, :, :], partial[:, s, :, :],
                                            b2b_all[:, :].unsqueeze(1).broadcast_to([P, NC, C]), ALU.add).then_inc(result_made, 1)

                pipeline(dve, STEPS, 2, [(0, partial_step)])


_INS = ["x", "src", "dst", "edge_attr_64", "L0_gnn_W1", "L0_gnn_b1", "L0_gnn_W2", "L0_gnn_b2", "L1_gnn_W1a", "L1_gnn_b1a",
        "L1_gnn_g1a", "L1_gnn_be1a", "L1_gnn_W2a", "L1_gnn_b2a", "L1_gnn_W1b", "L1_gnn_b1b", "L1_gnn_g1b", "L1_gnn_be1b",
        "L1_gnn_W2b", "L1_gnn_b2b"]


_OUTS = [((12500, 64), "float32")]


def kernel(**inputs):
    import numpy as _np
    import concourse.bacc as _bacc
    from concourse import mybir as _mybir
    from concourse.bass_utils import run_bass_kernel_spmd as _run

    nc = _bacc.Bacc("TRN2", target_bir_lowering=False, num_devices=1)
    arrays, args = {}, []
    for name in _INS:
        a = _np.ascontiguousarray(inputs[name])
        arrays[f"in_{name}_dram"] = a
        args.append(nc.dram_tensor(f"in_{name}_dram", a.shape, _mybir.dt.from_np(a.dtype), kind="ExternalInput").ap())
    for i, (shape, dtype) in enumerate(_OUTS):
        dt = _mybir.dt.from_np(_np.dtype(dtype))
        args.append(nc.dram_tensor(f"out_{i}_dram", shape, dt, kind="ExternalOutput").ap())
    gnn_kernel(nc, *args)
    r = _run(nc, [arrays], core_ids=[0])
    got = tuple(r.results[0][f"out_{i}_dram"] for i in range(len(_OUTS)))
    return got[0]
```

```python
from contextlib import ExitStack

import concourse.bass as bass
from concourse import mybir

P = 128
ALU = mybir.AluOpType
ACT = mybir.ActivationFunctionType
AX = mybir.AxisListType
F32 = mybir.dt.float32
BF16 = mybir.dt.bfloat16
I32 = mybir.dt.int32
I16 = mybir.dt.int16

BIG = 1.0e38
EPS = 1e-5


def at_least(eng, semaphore, value):
    if isinstance(value, int) and value <= 0:
        return
    eng.wait_ge(semaphore, value)


def at_least_apart(eng, semaphore, value, passed):
    at_least(eng, semaphore, value)
    if not isinstance(value, int):
        eng.sem_inc(passed, 1)


class Chain:

    def __init__(self, eng, semaphore, per_step=0):
        self.eng, self.semaphore, self.per_step = eng, semaphore, per_step
        self.base, self.n = 0, 0

    def start(self, step):
        self.base, self.n = step * self.per_step, 0

    def inc(self, ins):
        self.n += 1
        ins.then_inc(self.semaphore, 1)

    def wait(self):
        at_least(self.eng, self.semaphore, self.base + self.n)

    def link(self, ins):
        self.inc(ins)
        self.wait()

    def end(self):
        assert self.n == self.per_step


def pipeline(eng, steps, unroll, stages):
    rounds = steps // unroll
    last = max(lag for lag, _ in stages)
    first = 2 if last else 1
    assert rounds * unroll == steps and rounds > first and last <= unroll

    def peeled(step):
        for lag, stage in stages:
            if 0 <= step - lag < steps:
                stage((step - lag) // unroll, (step - lag) % unroll)

    for step in range(first * unroll):
        peeled(step)
    if rounds > first + 1:
        with eng.Fori(first, rounds - 1) as r:
            for slot in range(unroll):
                for lag, stage in stages:
                    back = (slot - lag) // unroll
                    stage(r + back if back else r, (slot - lag) % unroll)
    for step in range(steps - unroll, steps + last):
        peeled(step)


def gnn_kernel(nc, x, src, dst, edge_attr, W1, b1, W2, b2, W1a, b1a, g1a, be1a, W2a, b2a,
               W1b, b1b, g1b, be1b, W2b, b2b, out):
    N, C = x.shape
    E = src.shape[0]
    HID = W1a.shape[1]
    assert C == 64 and HID == 128
    J = 4
    BLK = P * J
    STEP = 2 * BLK
    CO = 2048
    NCO = -(-E // CO)
    EP = NCO * CO
    NBLK = EP // BLK
    HB = NBLK // 2
    MID = HB * BLK
    STEP_BITS = STEP.bit_length() - 1
    assert STEP == 1 << STEP_BITS
    GRP = 256
    NGRP = EP // GRP
    PAD_DST = 2 ** 15 - 1
    NI = 100
    FULL_NI = N // P
    REST = N - FULL_NI * P
    NP = P * NI
    NODE_EVERY = 4
    NI_PAD = NBLK // NODE_EVERY
    assert NI <= NI_PAD
    assert FULL_NI < NI <= 128 and REST > 0 and NBLK % 8 == 0 and HB % 4 == 0
    FULL_CO = E // CO
    LAST_BLK = E // BLK
    TAIL = E - LAST_BLK * BLK
    assert LAST_BLK == NBLK - 1 and TAIL % J == 0 and TAIL > 0
    NB = 10
    NSTEP = NI // NB
    NS = 5
    SSTEP = NI // NS
    SLOTS = 4
    OUT_OF_RANGE = 1.0e6
    assert 3 * P < NBLK <= 4 * P and N < PAD_DST and NGRP <= 1024

    def dram(name, shape, dt=F32):
        return nc.dram_tensor(name, shape, dt, kind="Internal").ap()

    dst_groups = dram("dst_groups", (NGRP, GRP), I16)
    same_max = dram("same_max", (EP,), BF16)
    same_sum = dram("same_sum", (EP,), BF16)
    recv_table = dram("recv_table", (NP, C))
    send_table = dram("send_table", (NP, C))
    recv_edges = dram("recv_edges", (EP, C))
    max_edges = dram("max_edges", (EP, C))
    norm_table = dram("norm_table", (NP, C))
    hid_edges = dram("hid_edges", (NBLK // 2, P, 2 * BLK))
    sum_edges = hid_edges.rearrange("k p c -> (k p c)").rearrange("(e c) -> e c", c=HID)

    stack = ExitStack()
    with stack:
        def tensor(scope, name, shape, dt=F32):
            return scope.enter_context(nc.sbuf_tensor(name, shape, dt))

        def banks(scope, name, shape, dt=F32):
            return scope.enter_context(nc.psum_tensor(name, shape, dt))

        def sem(name):
            phase_sems.append(nc.alloc_semaphore(name))
            return phase_sems[-1]

        phase_sems = []

        def end_phase():
            nc.clear_and_free_semaphores(list(phase_sems))
            phase_sems.clear()
            nc.all_engine_barrier()

        nodes = tensor(stack, "nodes", [P, NI, C])
        ident = tensor(stack, "ident", [P, P])
        end_idx = tensor(stack, "end_idx", [P, NI], I32)
        end_row = tensor(stack, "end_row", [P, NI], I32)
        has_edge = tensor(stack, "has_edge", [P, NI])
        spans_mid = tensor(stack, "spans_mid", [P, NI])
        steps_needed = tensor(stack, "steps_needed", [1, NI], I32)
        mids = tensor(stack, "mids", [P, 2], I32)
        sel2 = tensor(stack, "sel2", [2, P], BF16)

        hid2 = tensor(stack, "hid2", [P, NI * P])
        recv_sb, send_sb = (hid2[:, h * NI * C:(h + 1) * NI * C].rearrange("p (i c) -> p i c", c=C) for h in range(2))
        node_sums = tensor(stack, "node_sums", [P, NI * HID])
        sum_in = node_sums[:, :].rearrange("p (i c) -> p i c", c=HID)
        norm_deg = node_sums[:, 0:NI_PAD * (C + 1)].rearrange("p (i c) -> p i c", c=C + 1)
        src_at = NI_PAD * (C + 1)
        src_cols = node_sums[:, src_at:src_at + NBLK * J].bitcast(I32).rearrange("p (k j) -> p k j", j=J)
        spare_at = src_at + NBLK * J
        assert NI * P >= 2 * NI * C and NI * HID >= spare_at + 4 * BLK + CO + NI

        def norm_step(chain, k, stats, small, var_made, dev_made, made, result):
            dve = chain.eng
            chain.start(k)
            for i in range(NB):
                chain.inc(nc.vector.bn_stats(stats[:, i, :], nodes[:, bass.ds(k * NB + i, 1), :].rearrange("p a c -> p (a c)")))
            chain.wait()
            total, gap, var, dev, mean, inv, square, both = (small[:, q, :] for q in range(8))
            chain.inc(nc.vector.tensor_tensor(total, stats[:, :, 1], stats[:, :, 4], ALU.add))
            chain.inc(nc.vector.tensor_tensor(gap, stats[:, :, 1], stats[:, :, 4], ALU.subtract))
            chain.link(nc.vector.tensor_tensor(both, stats[:, :, 2], stats[:, :, 5], ALU.add))
            chain.inc(nc.vector.scalar_tensor_tensor(out=square, in0=gap, scalar=0.25, in1=gap, op0=ALU.mult, op1=ALU.mult))
            chain.link(nc.vector.tensor_scalar(both, both, 1.0 / C, EPS, ALU.mult, ALU.add))
            nc.vector.tensor_tensor(var, both, square, ALU.add).then_inc(var_made, 1)
            chain.inc(nc.vector.tensor_scalar(mean, total, 0.5, None, ALU.mult))
            at_least(dve, dev_made, k + 1)
            chain.link(nc.vector.reciprocal(inv, dev))
            chain.end()
            for i in range(NB):
                nc.vector.tensor_scalar(result(i), nodes[:, bass.ds(k * NB + i, 1), :].rearrange("p a c -> p (a c)"),
                                        mean[:, i:i + 1], inv[:, i:i + 1], ALU.subtract, ALU.mult).then_inc(made, 1)

        NORM_LINKS = NB + 7

        def affine_of_norm(chain, root_ready, root_made, stats, sums, gain, shift, g, be):
            chain.link(nc.vector.bn_aggr(sums[:, 0:2], stats))
            nc.vector.tensor_scalar(sums[:, 2:3], sums[:, 1:2], EPS, None, ALU.add).then_inc(root_ready, 1)
            chain.eng.wait_ge(root_made, 1)
            chain.link(nc.vector.reciprocal(sums[:, 4:5], sums[:, 3:4]))
            chain.link(nc.vector.tensor_tensor(gain, g, sums[:, 4:5], ALU.mult))
            chain.link(nc.vector.tensor_tensor(sums[:, 5:6], sums[:, 0:1], gain, ALU.mult))
            chain.link(nc.vector.tensor_tensor(shift, be, sums[:, 5:6], ALU.subtract))

        with ExitStack() as s1:
            edge_dst = tensor(s1, "edge_dst", [NCO, CO], I32)
            edge_dst16 = tensor(s1, "edge_dst16", [NCO, CO], I16)
            prev_last = tensor(s1, "prev_last", [NCO, 1], I32)
            prev_last_f = tensor(s1, "prev_last_f", [NCO, 1])
            m01 = tensor(s1, "m01", [NCO, CO], BF16)
            mbig = tensor(s1, "mbig", [NCO, CO], BF16)
            firsts = tensor(s1, "firsts", [NCO, CO // GRP])
            first_row = tensor(s1, "first_row", [1, NGRP])
            first_all = tensor(s1, "first_all", [P, NGRP])
            ones_row = tensor(s1, "ones_row", [1, P])
            node_i = tensor(s1, "node_i", [P, NI], I32)
            node_f = tensor(s1, "node_f", [P, NI])
            src_rows = tensor(s1, "src_rows", [P, 4, BLK], I32)
            src_rows_f = node_sums[:, spare_at:spare_at + 4 * BLK].rearrange("p (g c) -> p g c", c=BLK)
            floor_tile = node_sums[:, spare_at + 4 * BLK:spare_at + 4 * BLK + CO]
            smaller = tensor(s1, "smaller", [P, NS, GRP], BF16)
            signs = tensor(s1, "signs", [P, NS, NGRP], BF16)
            node_m = node_sums[:, spare_at + 4 * BLK + CO:spare_at + 4 * BLK + CO + NI]
            sign_sum = tensor(s1, "sign_sum", [P, NI])
            clamped = tensor(s1, "clamped", [P, NS])
            count = tensor(s1, "count", [P, NS])
            group_f = tensor(s1, "group_f", [P, NI])
            group_idx = tensor(s1, "group_idx", [P, NI], I32)
            entries = tensor(s1, "entries", [P, SLOTS, NS, GRP], I16)
            start_f = tensor(s1, "start_f", [P, NI + 1])
            next_start = tensor(s1, "next_start", [P, NI])
            shift_one = tensor(s1, "shift_one", [P, P])
            shift_wrap = tensor(s1, "shift_wrap", [P, P])
            column_end = tensor(s1, "column_end", [1, NI])
            column_end_i = tensor(s1, "column_end_i", [1, NI], I32)
            end_piece, over_mid = tensor(s1, "end_piece", [1, NI]), tensor(s1, "over_mid", [1, NI])
            fills_needed = tensor(s1, "fills_needed", [1, NI // 2], I32)
            degree, skip, last_edge, spans = (tensor(s1, n, [P, NI]) for n in ("degree", "skip", "last_edge", "spans"))
            second = tensor(s1, "second", [P, NI])
            mids_f = tensor(s1, "mids_f", [P, 2])
            start_idx = tensor(s1, "start_idx", [P, NI], I32)
            mid_row = tensor(s1, "mid_row", [P, C])
            w_ab = tensor(s1, "w_ab", [P, 2 * C])
            b1_all = tensor(s1, "b1_all", [P, C])
            stats = tensor(s1, "stats", [P, NB, 6])
            small = tensor(s1, "small", [P, 8, NB])
            normed = tensor(s1, "normed", [P, 2, NB, C])
            normed_t = tensor(s1, "normed_t", [P, 2, NB // 2, P])
            ps_t = banks(s1, "ps_t", [P, 8, P])
            ps_ab = banks(s1, "ps_ab", [P, 2, 8, P])
            ps_first = banks(s1, "ps_first", [P, 2, 512])
            ps_shifted = ps_first[:, 0, 0:NI]
            ps_src = ps_first[:, 1, :].rearrange("p (j q) -> p j q", j=J)
            HALF_CO = CO // GRP // 2

            consts = sem("consts")
            dst_in, src_in, x_in, w_in, mid_in = (sem(n) for n in ("dst_in", "src_in", "x_in", "w_in", "mid_in"))
            masks_made, masks_out = sem("masks_made"), sem("masks_out")
            dst16_made, groups_out = sem("dst16_made"), sem("groups_out")
            firsts_made, firsts_turned, row_made, firsts_spread = (
                sem(n) for n in ("firsts_made", "firsts_turned", "row_made", "firsts_spread"))
            src_f_made, src_turned, src_made = (sem(n) for n in ("src_f_made", "src_turned", "src_made"))
            nodes_numbered, firsts_ready, signs_summed = sem("nodes_numbered"), sem("firsts_ready"), sem("signs_summed")
            group_found, entries_in = sem("group_found"), [sem(f"entries_in{i}") for i in range(SLOTS)]
            start_made = sem("start_made")
            last_padded, shifts, starts_shifted = sem("last_padded"), sem("shifts"), sem("starts_shifted")
            floor_made, floor_out = sem("floor_made"), [sem(f"floor_out{i}") for i in range(2)]
            idx_made = sem("idx_made")
            scattered, mid_gathered, mid_out = sem("scattered"), sem("mid_gathered"), sem("mid_out")
            w_made = sem("w_made")
            var_made, dev_made, normed_made, normed_turned, normed_copied, ab_made = (
                sem(n) for n in ("var_made", "dev_made", "normed_made", "normed_turned", "normed_copied", "ab_made"))
            recv_made, send_made, tables_out = sem("recv_made"), sem("send_made"), sem("tables_out")

            pool_passed, dve_passed = sem("pool_passed1"), sem("dve_passed1")
            FILLS = EP * C // (P * CO)
            PIECE_BITS = (P * CO // C).bit_length() - 1
            assert P * CO // C == 1 << PIECE_BITS and NI % 2 == 0
            filled, fill_known = sem("filled"), sem("fill_known")
            dst_padded, nodes_padded, src_padded = sem("dst_padded"), sem("nodes_padded"), sem("src_padded")
            block = s1.enter_context(nc.Block())

            @block.sync
            def _(sp):
                dst_v = dst[0:FULL_CO * CO].rearrange("(p c) -> p c", c=CO)
                cut = FULL_CO // 16 * 16
                sp.wait_ge(dst_padded, 2)
                sp.dma_start(edge_dst[0:cut, :], dst_v[0:cut, :]).then_inc(dst_in, 16)
                sp.dma_start(edge_dst[cut:FULL_CO, :], dst_v[cut:FULL_CO, :]).then_inc(dst_in, 16)
                sp.dma_start(edge_dst[FULL_CO:NCO, 0:E - FULL_CO * CO],
                             dst[FULL_CO * CO:E].rearrange("(p c) -> p c", p=1)).then_inc(dst_in, 16)
                with nc.allow_non_contiguous_dma(reason="one element per partition"):
                    sp.dma_start(prev_last[1:NCO, :], dst_v[:, CO - 1:CO]).then_inc(dst_in, 16)
                sp.wait_ge(dst16_made, 1)
                sp.dma_start(dst_groups.rearrange("(p g) f -> p (g f)", p=NCO), edge_dst16[:, :]).then_inc(groups_out, 16)
                sp.wait_ge(nodes_padded, 1)
                cut = FULL_NI // 2
                for a, b in ((0, cut), (cut, FULL_NI)):
                    sp.dma_start(nodes[:, a:b, :], x[a * P:b * P, :].rearrange("(i p) c -> p i c", p=P)).then_inc(x_in, 16)
                sp.dma_start(nodes[0:REST, FULL_NI, :], x[FULL_NI * P:N, :]).then_inc(x_in, 16)
                sp.wait_ge(floor_made, 1)
                floor_v = recv_edges.rearrange("(n p r) c -> p n (r c)", p=P, r=CO // C)

                def fill(r, s):
                    at_least(sp, floor_out[s], 16 * r)
                    if not (isinstance(r, int) and r == 0):
                        sp.sem_inc(filled, 1)
                    sp.dma_start(floor_v[:, bass.ds(r * 2 + s, 1), :].rearrange("p n c -> p (n c)"), floor_tile[:, :]).then_inc(floor_out[s], 16)

                pipeline(sp, FILLS, 2, [(0, fill)])
                for s in range(2):
                    sp.wait_ge(floor_out[s], 16 * (FILLS // 2))
                    sp.sem_inc(filled, 1)
                sp.wait_ge(masks_made, 2)
                sp.dma_start(same_sum.rearrange("(p c) -> p c", c=CO), m01[:, :]).then_inc(masks_out, 16)
                sp.dma_start(same_max.rearrange("(p c) -> p c", c=CO), mbig[:, :]).then_inc(masks_out, 16)
                sp.wait_ge(mid_gathered, 16)
                sp.wait_ge(scattered, 16 * NI)
                sp.dma_start(recv_edges[1:2, :], mid_row[0:1, :]).then_inc(mid_out, 16)
                sp.wait_ge(mid_out, 16)
                sp.wait_ge(masks_out, 32)

            @block.gpsimd
            def _(pool):
                nc.gpsimd.iota(node_i[:, :], [[P, NI]], base=0, channel_multiplier=1).then_inc(nodes_numbered, 1)
                nc.gpsimd.memset(nodes[:, FULL_NI:NI, :], 0.0).then_inc(nodes_padded, 1)
                nc.gpsimd.memset(src_rows[:, 3, :], 0).then_inc(src_padded, 1)
                nc.gpsimd.memset(ident[:, :], 0.0).then_inc(consts, 1)
                nc.gpsimd.memset(sel2[:, :], 1.0).then_inc(consts, 1)
                pool.wait_ge(consts, 2)
                nc.gpsimd.affine_select(out=ident[:, :], in_=ident[:, :], compare_op=ALU.not_equal, fill=1.0, base=0,
                                        pattern=[[-1, P]], channel_multiplier=1).then_inc(consts, 1)
                nc.gpsimd.affine_select(out=sel2[:, :], in_=sel2[:, :], compare_op=ALU.is_ge, fill=0.0, base=0,
                                        pattern=[[1, P]], channel_multiplier=-C).then_inc(consts, 1)
                pool.wait_ge(consts, 4)
                nc.gpsimd.affine_select(out=sel2[:, :], in_=sel2[:, :], compare_op=ALU.is_ge, fill=0.0, base=C - 1,
                                        pattern=[[-1, P]], channel_multiplier=C).then_inc(consts, 1)
                nc.gpsimd.memset(shift_one[:, :], 0.0).then_inc(shifts, 1)
                nc.gpsimd.memset(shift_wrap[:, :], 0.0).then_inc(shifts, 1)
                pool.wait_ge(shifts, 2)
                nc.gpsimd.affine_select(out=shift_one[:, :], in_=shift_one[:, :], compare_op=ALU.not_equal, fill=1.0, base=-1,
                                        pattern=[[-1, P]], channel_multiplier=1).then_inc(shifts, 1)
                nc.gpsimd.affine_select(out=shift_wrap[:, :], in_=shift_wrap[:, :], compare_op=ALU.not_equal, fill=1.0, base=P - 1,
                                        pattern=[[-1, P]], channel_multiplier=1).then_inc(shifts, 1)
                pool.wait_ge(groups_out, 16)

                for k in range(SSTEP):
                    pool.wait_ge(group_found, k + 1)
                    at_least(pool, start_made, k - SLOTS + 1)
                    for i in range(NS):
                        col = k * NS + i
                        pool.indirect_dma_start(out=entries[:, k % SLOTS, i, :], out_offset=None, in_=dst_groups,
                                                in_offset=bass.IndirectOffsetOnAxis(ap=group_idx[:, col:col + 1], axis=0)
                                                ).then_inc(entries_in[k % SLOTS], 16)
                pool.wait_ge(idx_made, 1)
                pool.wait_ge(fill_known, 1)
                pool.wait_ge(recv_made, NSTEP)
                for h in range(NI // 2):
                    needed = pool.value_load(fills_needed[0:1, h:h + 1], min_val=1, max_val=FILLS)
                    pool.wait_ge(filled, needed)
                    pool.sem_inc(pool_passed, 1)
                    for i in (h, h + NI // 2):
                        pool.indirect_dma_start(out=recv_edges, out_offset=bass.IndirectOffsetOnAxis(ap=start_idx[:, i:i + 1], axis=0),
                                                in_=recv_sb[:, i, :], in_offset=None,
                                                bounds_check=EP - 1, oob_is_err=False).then_inc(scattered, 16)
                pool.wait_ge(tables_out, 32)
                pool.wait_ge(mid_in, 16)
                pool.indirect_dma_start(out=mid_row[:, :], out_offset=None, in_=recv_table,
                                        in_offset=bass.IndirectOffsetOnAxis(ap=mids[:, 1:2], axis=0)).then_inc(mid_gathered, 16)

            @block.tensor
            def _(pe):
                pe.wait_ge(consts, 3)
                pe.wait_ge(firsts_made, 1)
                for g in range(CO // GRP):
                    h, at = g // HALF_CO, g % HALF_CO * NCO
                    mm = nc.tensor.transpose(ps_first[0:1, h, at:at + NCO], firsts[:, g:g + 1], ident[0:NCO, 0:NCO])
                mm.then_inc(firsts_turned, 1)
                pe.wait_ge(row_made, 2)
                for h in range(2):
                    mm = nc.tensor.matmul(ps_first[:, h, 0:NGRP // 2], ones_row[:, :], first_row[:, h * (NGRP // 2):(h + 1) * (NGRP // 2)],
                                          start=True, stop=True)
                mm.then_inc(firsts_spread, 1)
                pe.wait_ge(w_made, 1)

                def turn(r, s):
                    k = r * 2 + s
                    at_least(pe, normed_made, NB * (k + 1))
                    at_least(pe, normed_copied, k)
                    for q in range(NB // 2):
                        mm = nc.tensor.transpose(ps_t[:, q, :], normed[:, s, 2 * q:2 * q + 2, :].rearrange("p a c -> p (a c)"), ident[:, :])
                    mm.then_inc(normed_turned, 1)

                def product(r, s):
                    k = r * 2 + s
                    at_least(pe, normed_copied, k + 1)
                    at_least(pe, recv_made, k)
                    at_least(pe, send_made, k)
                    for i in range(NB):
                        h = (i % 2) * C
                        mm = nc.tensor.matmul(ps_ab[:, i % 2, i // 2, :], normed_t[h:h + C, s, i // 2, :], w_ab[h:h + C, :], start=True, stop=True)
                    mm.then_inc(ab_made, 1)

                pipeline(pe, NSTEP, 2, [(0, turn), (0, product)])
                pe.wait_ge(start_made, SSTEP)
                pe.wait_ge(last_padded, 1)
                pe.wait_ge(shifts, 4)
                nc.tensor.matmul(ps_shifted, shift_one[:, :], start_f[:, 0:NI], start=True, stop=False)
                nc.tensor.matmul(ps_shifted, shift_wrap[:, :], start_f[:, 1:NI + 1], start=False, stop=True).then_inc(starts_shifted, 1)
                for g in range(4):
                    rows = min(P, NBLK - g * P)
                    pe.wait_ge(src_f_made, g + 1)
                    at_least(pe, src_made, g)
                    for j in range(J):
                        mm = nc.tensor.transpose(ps_src[:, j, 0:rows], src_rows_f[0:rows, g, j::J], ident[0:rows, 0:rows])
                    mm.then_inc(src_turned, 1)

            @block.scalar
            def _(act):
                act.dma_start(mids[:, :], dst[MID - 1:MID + 1].partition_broadcast(P)).then_inc(mid_in, 16)
                for h in range(2):
                    act.dma_start(w_ab[h * C:(h + 1) * C, 0:C], W1[0:C, :]).then_inc(w_in, 16)
                    act.dma_start(w_ab[h * C:(h + 1) * C, C:2 * C], W1[C:2 * C, :]).then_inc(w_in, 16)
                act.dma_start(b1_all[:, :], b1.partition_broadcast(P)).then_inc(w_in, 16)
                act.wait_ge(src_padded, 1)
                for g in range(4):
                    rows = min(P, LAST_BLK - g * P)
                    act.dma_start(src_rows[0:rows, g, :],
                                  src[g * P * BLK:(g * P + rows) * BLK].rearrange("(p c) -> p c", c=BLK)).then_inc(src_in, 16)
                act.dma_start(src_rows[LAST_BLK - 3 * P:NBLK - 3 * P, 3, 0:TAIL],
                              src[LAST_BLK * BLK:E].rearrange("(p c) -> p c", p=1)).then_inc(src_in, 16)

                act.wait_ge(firsts_ready, 2)

                def sum_signs(r, s):
                    k = r * SLOTS + s
                    at_least(act, signs_summed, NS * k)
                    for i in range(NS):
                        col = bass.ds(k * NS + i, 1)
                        nc.scalar.activation(signs[:, i, :], first_all[:, :], ACT.Sign, bias=node_m[:, col], scale=-1.0,
                                             accum_out=sign_sum[:, col]).then_inc(signs_summed, 1)

                def deviation(r, s):
                    if s % 2:
                        return
                    at_least(act, var_made, r * 2 + s // 2 + 1)
                    nc.scalar.activation(small[:, 3, :], small[:, 2, :], ACT.Sqrt).then_inc(dev_made, 1)

                def copy_turned(r, s):
                    if s % 2:
                        return
                    k, s = r * 2 + s // 2, s // 2
                    at_least(act, normed_turned, k + 1)
                    at_least(act, ab_made, k - 1)
                    nc.scalar.activation(normed_t[:, s, :, :], ps_t[:, 0:NB // 2, :], ACT.Relu).then_inc(normed_copied, 1)

                def copy_send(r, s):
                    if s % 2:
                        return
                    k = r * 2 + s // 2
                    at_least(act, ab_made, k + 1)
                    nc.scalar.copy(send_sb[:, bass.ds(k * NB, NB), :].rearrange("p (q h) c -> p q h c", h=2),
                                   ps_ab[:, :, 0:NB // 2, C:2 * C].rearrange("p h q c -> p q h c")).then_inc(send_made, 1)

                pipeline(act, SSTEP, SLOTS, [(0, sum_signs), (2, deviation), (3, copy_turned), (4, copy_send)])
                for s in range(2):
                    act.wait_ge(floor_out[s], 16 * (FILLS // 2))
                act.wait_ge(recv_made, NSTEP)
                act.dma_start(recv_table.rearrange("(i p) c -> p i c", p=P), recv_sb[:, :, :]).then_inc(tables_out, 16)
                act.wait_ge(send_made, NSTEP)
                act.dma_start(send_table.rearrange("(i p) c -> p i c", p=P), send_sb[:, :, :]).then_inc(tables_out, 16)
                act.wait_ge(tables_out, 32)

            @block.vector
            def _(dve):
                once = Chain(dve, sem("dve_once"))
                nc.vector.memset(prev_last[:, :], -1).then_inc(dst_padded, 1)
                nc.vector.memset(edge_dst[96:NCO, E - FULL_CO * CO:CO], PAD_DST).then_inc(dst_padded, 1)
                nc.vector.memset(floor_tile[:, :], -BIG).then_inc(floor_made, 1)
                nc.vector.memset(ones_row[:, :], 1.0).then_inc(row_made, 1)
                nc.vector.memset(start_f[:, NI:NI + 1], float(E)).then_inc(last_padded, 1)
                dve.wait_ge(nodes_numbered, 1)
                once.inc(nc.vector.tensor_copy(node_f[:, :], node_i[:, :]))
                nc.vector.tensor_scalar(node_m[:, :], node_i[:, :], 0.5, None, ALU.subtract).then_inc(firsts_ready, 1)
                dve.wait_ge(dst_in, 64)
                nc.vector.tensor_copy(firsts[:, :], edge_dst[:, ::GRP]).then_inc(firsts_made, 1)
                nc.vector.tensor_copy(edge_dst16[:, :], edge_dst[:, :]).then_inc(dst16_made, 1)
                once.link(nc.vector.tensor_copy(prev_last_f[:, :], prev_last[:, :]))
                dve.wait_ge(firsts_turned, 1)
                nc.vector.tensor_copy(first_row[:, :].rearrange("a (h c) -> a h c", h=2), ps_first[0:1, :, 0:NGRP // 2]).then_inc(row_made, 1)
                dve.wait_ge(dst16_made, 1)
                once.link(nc.vector.tensor_tensor(m01[:, 1:CO], edge_dst16[:, 1:CO], edge_dst16[:, 0:CO - 1], ALU.is_equal))
                nc.vector.tensor_tensor(m01[:, 0:1], edge_dst16[:, 0:1], prev_last_f[:, :], ALU.is_equal).then_inc(masks_made, 1)
                dve.wait_ge(firsts_spread, 1)
                nc.vector.tensor_copy(first_all[:, :].rearrange("p (h c) -> p h c", h=2), ps_first[:, :, 0:NGRP // 2]).then_inc(firsts_ready, 1)
                group_chain = Chain(dve, sem("group_chain"), 2)
                entry_chain = Chain(dve, sem("entry_chain"), NS)
                norm_chain = Chain(dve, sem("norm_chain"), NORM_LINKS)

                def find_group(r, s):
                    k = r * SLOTS + s
                    part = bass.ds(k * NS, NS)
                    at_least(dve, signs_summed, NS * (k + 1))
                    group_chain.start(k)
                    group_chain.link(nc.vector.tensor_scalar(clamped[:, :], sign_sum[:, part], 2.0 - NGRP, 0.5, ALU.max, ALU.mult))
                    nc.vector.tensor_scalar(group_idx[:, part], clamped[:, :], NGRP / 2 - 1.0, None, ALU.add).then_inc(group_found, 1)
                    group_chain.link(nc.vector.tensor_scalar(group_f[:, part], clamped[:, :], NGRP / 2 - 1.0, None, ALU.add))
                    group_chain.end()

                def find_start(r, s):
                    k = r * SLOTS + s
                    at_least(dve, entries_in[s], 16 * NS * (r + 1))
                    at_least(dve, start_made, k)
                    entry_chain.start(k)
                    for i in range(NS):
                        entry_chain.inc(nc.vector.tensor_scalar(smaller[:, i, :], entries[:, s, i, :], node_f[:, bass.ds(k * NS + i, 1)], 0.0,
                                                                ALU.is_lt, ALU.add, accum_out=count[:, i:i + 1]))
                    entry_chain.wait()
                    entry_chain.end()
                    nc.vector.scalar_tensor_tensor(out=start_f[:, bass.ds(k * NS, NS)], in0=group_f[:, bass.ds(k * NS, NS)],
                                                   scalar=float(GRP), in1=count[:, :], op0=ALU.mult, op1=ALU.add).then_inc(start_made, 1)

                def norm(r, s):
                    if s % 2:
                        return
                    k, s = r * 2 + s // 2, s // 2
                    if isinstance(k, int) and k == 0:
                        dve.wait_ge(x_in, 48)
                    at_least_apart(dve, normed_turned, k - 1, dve_passed)
                    norm_step(norm_chain, k, stats, small, var_made, dev_made, normed_made, lambda i: normed[:, s, i, :])

                def add_bias(r, s):
                    if s % 2:
                        return
                    k = r * 2 + s // 2
                    at_least(dve, send_made, k + 1)
                    nc.vector.tensor_tensor(recv_sb[:, bass.ds(k * NB, NB), :].rearrange("p (q h) c -> p q h c", h=2),
                                            ps_ab[:, :, 0:NB // 2, 0:C].rearrange("p h q c -> p q h c"),
                                            b1_all[:, :].unsqueeze(1).unsqueeze(1).broadcast_to([P, NB // 2, 2, C]), ALU.add).then_inc(recv_made, 1)

                dve.wait_ge(w_in, 16 * 5)
                nc.vector.tensor_tensor(w_ab[:, 0:C], w_ab[:, 0:C], w_ab[:, C:2 * C], ALU.subtract).then_inc(w_made, 1)
                pipeline(dve, SSTEP, SLOTS, [(0, find_group), (3, find_start), (1, norm), (4, add_bias)])
                dve.wait_ge(masks_made, 1)
                nc.vector.tensor_scalar(mbig[:, :], m01[:, :], 2 * BIG, -BIG, ALU.mult, ALU.add).then_inc(masks_made, 1)

                def to_row(result, edges, add):
                    once.link(nc.vector.tensor_scalar(second[:, :], edges, MID - 0.5, float(1 - 2 * MID), ALU.is_gt, ALU.mult))
                    if add is not None:
                        once.link(nc.vector.tensor_tensor(second[:, :], second[:, :], add[:, :], ALU.add))
                    once.link(nc.vector.scalar_tensor_tensor(out=result[:, :], in0=edges, scalar=2.0, in1=second[:, :],
                                                             op0=ALU.mult, op1=ALU.add))

                dve.wait_ge(start_made, SSTEP)
                dve.wait_ge(last_padded, 1)
                once.link(nc.vector.tensor_scalar(column_end[:, :], start_f[0:1, 1:NI + 1], -1.0, 0.0, ALU.add, ALU.max))
                once.link(nc.vector.tensor_scalar(over_mid[:, :], column_end[:, :], MID - 0.5, None, ALU.is_gt))
                once.link(nc.vector.scalar_tensor_tensor(out=end_piece[:, :], in0=over_mid[:, :], scalar=(1.0 - 2 * MID) / 2,
                                                         in1=column_end[:, :], op0=ALU.mult, op1=ALU.add))
                once.link(nc.vector.tensor_scalar(column_end_i[:, :], end_piece[:, :], 2.0, None, ALU.mult))
                once.link(nc.vector.tensor_scalar(column_end_i[:, :], column_end_i[:, :], PIECE_BITS, None, ALU.logical_shift_right))
                once.link(nc.vector.tensor_scalar(end_piece[:, :], column_end_i[:, :], 1, None, ALU.add))
                once.link(nc.vector.scalar_tensor_tensor(out=over_mid[:, :], in0=start_f[0:1, 0:NI], scalar=MID - 0.5,
                                                         in1=over_mid[:, :], op0=ALU.is_lt, op1=ALU.mult))
                once.link(nc.vector.scalar_tensor_tensor(out=end_piece[:, :], in0=over_mid[:, :], scalar=float(FILLS),
                                                         in1=end_piece[:, :], op0=ALU.mult, op1=ALU.max))
                nc.vector.tensor_tensor(fills_needed[:, :], end_piece[:, 0:NI // 2], end_piece[:, NI // 2:NI], ALU.max).then_inc(fill_known, 1)
                dve.wait_ge(starts_shifted, 1)
                once.link(nc.vector.tensor_copy(next_start[:, :], ps_shifted))
                once.link(nc.vector.tensor_tensor(degree[:, :], next_start[:, :], start_f[:, 0:NI], ALU.subtract))
                once.link(nc.vector.tensor_scalar(has_edge[:, :], degree[:, :], 0.5, None, ALU.is_gt))
                once.link(nc.vector.tensor_scalar(skip[:, :], has_edge[:, :], -OUT_OF_RANGE, OUT_OF_RANGE, ALU.mult, ALU.add))
                to_row(skip, start_f[:, 0:NI], skip)
                nc.vector.tensor_copy(start_idx[:, :], skip[:, :]).then_inc(idx_made, 1)
                nc.vector.tensor_copy(norm_deg[:, 0:NI, C], degree[:, :])
                nc.vector.memset(norm_deg[:, NI:NI_PAD, :], 0.0)
                once.link(nc.vector.tensor_scalar(last_edge[:, :], next_start[:, :], -1.0, 0.0, ALU.add, ALU.max))
                nc.vector.tensor_copy(end_idx[:, :], last_edge[:, :])
                to_row(last_edge, last_edge[:, :], None)
                nc.vector.tensor_copy(end_row[:, :], last_edge[:, :])
                once.link(nc.vector.tensor_copy(column_end_i[:, :], column_end[:, :]))
                once.link(nc.vector.tensor_scalar(column_end_i[:, :], column_end_i[:, :], STEP_BITS, None, ALU.logical_shift_right))
                once.link(nc.vector.tensor_scalar(steps_needed[:, :], column_end_i[:, :], 1, None, ALU.add))
                dve.wait_ge(mid_in, 16)
                once.link(nc.vector.tensor_copy(mids_f[:, :], mids[:, :]))
                once.link(nc.vector.tensor_scalar(spans[:, :], node_f[:, :], mids_f[:, 0:1], None, ALU.is_equal))
                once.link(nc.vector.scalar_tensor_tensor(out=spans[:, :], in0=node_f[:, :], scalar=mids_f[:, 1:2],
                                                         in1=spans[:, :], op0=ALU.is_equal, op1=ALU.mult))
                nc.vector.tensor_scalar(spans_mid[:, :], spans[:, :], BIG, -BIG, ALU.mult, ALU.add)
                dve.wait_ge(src_in, 16 * 5)
                for g in range(4):
                    nc.vector.tensor_copy(src_rows_f[:, g, :], src_rows[:, g, :]).then_inc(src_f_made, 1)
                for g in range(4):
                    rows = min(P, NBLK - g * P)
                    dve.wait_ge(src_turned, g + 1)
                    nc.vector.tensor_copy(src_cols[:, g * P:g * P + rows, :],
                                          ps_src[:, :, 0:rows].rearrange("p j b -> p b j")).then_inc(src_made, 1)

        end_phase()

        with ExitStack() as s2:
            U = 4
            recv_in = tensor(s2, "recv_in", [P, U, J, 2 * C])
            mask_in = tensor(s2, "mask_in", [2, U, BLK], BF16)
            send_in = tensor(s2, "send_in", [P, U, J, 2, C])
            send_idx = tensor(s2, "send_idx", [P, 2, 2, 2 * J], I32)
            mask = tensor(s2, "mask", [P, 2, BLK])
            filled = tensor(s2, "filled", [P, 2, BLK])
            joined = tensor(s2, "joined", [P, 2, BLK])
            hidden = tensor(s2, "hidden", [P, 2, BLK])
            maxima = tensor(s2, "maxima", [P, 2, BLK])
            max_rows = tensor(s2, "max_rows", [P, U, J * 2 * C])
            w2_twice = tensor(s2, "w2_twice", [P, P])
            ps_recv = [banks(s2, f"ps_recv{b}", [P, BLK]) for b in range(2)]
            ps_send = [banks(s2, f"ps_send{b}", [P, BLK]) for b in range(2)]
            ps_mask = banks(s2, "ps_mask", [P, BLK])
            ps_msg = banks(s2, "ps_msg", [P, BLK])
            ps_back = [banks(s2, f"ps_back{b}", [P, J, P]) for b in range(2)]

            loaded = [sem(f"loaded{i}") for i in range(U)]
            gathered = [sem(f"gathered{i}") for i in range(U)]
            stored = [sem(f"stored{i}") for i in range(U)]
            (idx_copied, recv_turned, mask_spread, mask_copied, send_turned, fill_done, join_done, hidden_done, msg_done, max_done,
             back_turned, rows_made, w2_clear, w2_in) = (
                sem(n) for n in ("idx_copied", "recv_turned", "mask_spread", "mask_copied", "send_turned", "fill_done", "join_done",
                                     "hidden_done", "msg_done", "max_done", "back_turned", "rows_made", "w2_clear", "w2_in"))
            fill_start = sem("fill_start")
            pool_passed, dve_passed = sem("pool_passed2"), sem("dve_passed2")
            block = s2.enter_context(nc.Block())

            @block.sync
            def _(sp):
                recv_v = recv_edges.rearrange("(k p j t) c -> p k (j t c)", p=P, j=J, t=2)
                max_v = max_edges.rearrange("(k p j t) c -> p k (j t c)", p=P, j=J, t=2)
                mask_v = same_max.rearrange("(t k c) -> t k c", t=2, k=HB)
                sp.wait_ge(w2_clear, 1)
                for h in range(2):
                    sp.dma_start(w2_twice[h * C:(h + 1) * C, h * C:(h + 1) * C], W2).then_inc(w2_in, 16)

                def load(r, s):
                    k = r * U + s
                    at_least(sp, recv_turned, k - U + 1)
                    sp.dma_start(recv_in[:, s, :, :].rearrange("p j c -> p (j c)"), recv_v[:, bass.ds(k, 1), :].rearrange("p a f -> p (a f)")).then_inc(loaded[s], 16)
                    at_least(sp, mask_spread, k - U + 1)
                    sp.dma_start(mask_in[:, s, :], mask_v[:, bass.ds(k, 1), :].rearrange("t a c -> t (a c)")).then_inc(loaded[s], 16)

                def store(r, s):
                    k = r * U + s
                    at_least(sp, rows_made, k + 1)
                    sp.dma_start(max_v[:, bass.ds(k, 1), :].rearrange("p a f -> p (a f)"), max_rows[:, s, :]).then_inc(stored[s], 16)

                pipeline(sp, HB, U, [(0, load), (3, store)])
                for s in range(U):
                    sp.wait_ge(stored[s], 16 * (HB // U))

            @block.gpsimd
            def _(pool):
                nc.gpsimd.memset(w2_twice[:, :], 0.0).then_inc(w2_clear, 1)

                def gather(r, s):
                    k = r * U + s
                    if s % 2 == 0:
                        at_least(pool, idx_copied, r * (U // 2) + s // 2 + 1)
                    at_least_apart(pool, send_turned, k - U + 1, pool_passed)
                    for t in range(2):
                        for j in range(J):
                            col = (s % 2) * J + j
                            pool.indirect_dma_start(out=send_in[:, s, j, t, :], out_offset=None, in_=send_table,
                                                    in_offset=bass.IndirectOffsetOnAxis(ap=send_idx[:, s // 2, t, col:col + 1], axis=0)
                                                    ).then_inc(gathered[s], 16)

                pipeline(pool, HB, U, [(0, gather)])

            @block.tensor
            def _(pe):
                def message(r, s):
                    k = r * U + s
                    at_least(pe, hidden_done, k + 1)
                    at_least(pe, max_done, k)
                    nc.tensor.matmul(ps_msg[:, :], w2_twice[:, :], hidden[:, s % 2, :], start=True, stop=True).then_inc(msg_done, 1)

                def turn_back(r, s):
                    k = r * U + s
                    at_least(pe, max_done, k + 1)
                    at_least(pe, rows_made, k - 1)
                    for j in range(J):
                        mm = nc.tensor.transpose(ps_back[s % 2][:, j, :], maxima[:, s % 2, j::J], ident[:, :])
                    mm.then_inc(back_turned, 1)

                def turn_in(r, s):
                    k = r * U + s
                    at_least(pe, loaded[s], 32 * (r + 1))
                    at_least(pe, fill_done, k - 1)
                    for j in range(J):
                        mm = nc.tensor.transpose(ps_recv[s % 2][:, j::J], recv_in[:, s, j, :], ident[:, :])
                    mm.then_inc(recv_turned, 1)
                    at_least(pe, mask_copied, k)
                    nc.tensor.matmul(ps_mask[:, :], sel2[:, :], mask_in[:, s, :], start=True, stop=True).then_inc(mask_spread, 1)
                    at_least(pe, gathered[s], 16 * 2 * J * (r + 1))
                    at_least(pe, join_done, k - 1)
                    for j in range(J):
                        mm = nc.tensor.transpose(ps_send[s % 2][:, j::J], send_in[:, s, j, :, :].rearrange("p t c -> p (t c)"), ident[:, :])
                    mm.then_inc(send_turned, 1)

                pe.wait_ge(w2_in, 32)
                pipeline(pe, HB, U, [(1, message), (2, turn_back), (0, turn_in)])

            @block.scalar
            def _(act):
                cols = src_cols[:, :, :].rearrange("p (t k) j -> p t (k j)", t=2)

                def copy_idx(r, s):
                    if s % 2 == 0:
                        nc.scalar.copy(send_idx[:, s // 2, :, :], cols[:, :, bass.ds((r * U + s) * J, 2 * J)]).then_inc(idx_copied, 1)

                def copy_mask(r, s):
                    k = r * U + s
                    at_least(act, mask_spread, k + 1)
                    at_least(act, max_done, k - 1)
                    nc.scalar.copy(mask[:, s % 2, :], ps_mask[:, :]).then_inc(mask_copied, 1)

                def rows_out(r, s):
                    k = r * U + s
                    at_least(act, back_turned, k + 1)
                    at_least(act, stored[s], 16 * r)
                    nc.scalar.copy(max_rows[:, s, :], ps_back[s % 2][:, :, :].rearrange("p j q -> p (j q)")).then_inc(rows_made, 1)

                def relu(r, s):
                    k = r * U + s
                    at_least(act, join_done, k + 1)
                    at_least(act, msg_done, k - 1)
                    nc.scalar.activation(hidden[:, s % 2, :], joined[:, s % 2, :], ACT.Relu).then_inc(hidden_done, 1)

                pipeline(act, HB, U, [(0, copy_idx), (2, copy_mask), (4, rows_out), (2, relu)])

            @block.vector
            def _(dve):
                nc.vector.memset(filled[:, 1, BLK - 1:BLK], -BIG).then_inc(fill_start, 1)
                nc.vector.memset(maxima[:, 1, BLK - 1:BLK], -BIG).then_inc(fill_start, 1)
                dve.wait_ge(fill_start, 2)

                def maximum(r, s):
                    k = r * U + s
                    at_least(dve, msg_done, k + 1)
                    at_least(dve, back_turned, k - 1)
                    at_least(dve, max_done, k)
                    nc.vector.tensor_tensor_scan(maxima[:, s % 2, :], mask[:, s % 2, :], ps_msg[:, :],
                                                 maxima[:, 1 - s % 2, BLK - 1:BLK], ALU.min, ALU.max).then_inc(max_done, 1)

                def fill(r, s):
                    k = r * U + s
                    at_least(dve, recv_turned, k + 1)
                    at_least(dve, mask_copied, k + 1)
                    at_least(dve, fill_done, k)
                    nc.vector.tensor_tensor_scan(filled[:, s % 2, :], mask[:, s % 2, :], ps_recv[s % 2][:, :],
                                                 filled[:, 1 - s % 2, BLK - 1:BLK], ALU.min, ALU.max).then_inc(fill_done, 1)

                def join(r, s):
                    k = r * U + s
                    at_least(dve, send_turned, k + 1)
                    at_least(dve, fill_done, k + 1)
                    at_least(dve, hidden_done, k - 1)
                    nc.vector.tensor_tensor(joined[:, s % 2, :], filled[:, s % 2, :], ps_send[s % 2][:, :], ALU.add).then_inc(join_done, 1)

                pipeline(dve, HB, U, [(1, maximum), (0, fill), (0, join)])

        end_phase()

        with ExitStack() as s3:
            max_in = tensor(s3, "max_in", [P, 2, NB, C])
            node_idx = tensor(s3, "node_idx", [P, 2, NB], I32)
            mid_max = tensor(s3, "mid_max", [P, C])
            b2_all = tensor(s3, "b2_all", [P, C])
            with_mid = tensor(s3, "with_mid", [P, NB, C])
            stats = tensor(s3, "stats3", [P, NB, 6])
            small = tensor(s3, "small3", [P, 8, NB])
            normed = tensor(s3, "normed3", [P, 2, NB, C])
            table_rows = tensor(s3, "table_rows", [P, 2, NB, C])
            max_got = [sem(f"max_got{i}") for i in range(2)]
            table_out = [sem(f"table_out{i}") for i in range(2)]
            idx_copied, mid_in, max_used, var_made, dev_made, normed_made, relu_made, kept = (
                sem(n) for n in ("idx_copied3", "mid_in3", "max_used", "var_made3", "dev_made3", "normed_made3", "relu_made3", "kept"))
            pool_passed, dve_passed = sem("pool_passed3"), sem("dve_passed3")
            block = s3.enter_context(nc.Block())

            @block.sync
            def _(sp):
                table_v = norm_table.rearrange("(i p) c -> p i c", p=P)
                sp.dma_start(mid_max[:, :], max_edges[2 * (MID - 1):2 * MID - 1, :].rearrange("a c -> (a c)").partition_broadcast(P)).then_inc(mid_in, 16)
                sp.dma_start(b2_all[:, :], b2.partition_broadcast(P)).then_inc(mid_in, 16)

                def store(r, s):
                    k = r * 2 + s
                    at_least(sp, relu_made, k + 1)
                    sp.dma_start(table_v[:, bass.ds(k * NB, NB), :], table_rows[:, s, :, :]).then_inc(table_out[s], 16)

                pipeline(sp, NSTEP, 2, [(0, store)])
                for s in range(2):
                    sp.wait_ge(table_out[s], 16 * (NSTEP // 2))

            @block.gpsimd
            def _(pool):
                def gather(r, s):
                    k = r * 2 + s
                    at_least(pool, max_got[s], 16 * NB * r)
                    nc.gpsimd.tensor_copy(node_idx[:, s, :], end_row[:, bass.ds(k * NB, NB)]).then_inc(idx_copied, 1)
                    at_least(pool, idx_copied, k + 1)
                    at_least_apart(pool, max_used, k - 1, pool_passed)
                    for i in range(NB):
                        pool.indirect_dma_start(out=max_in[:, s, i, :], out_offset=None, in_=max_edges,
                                                in_offset=bass.IndirectOffsetOnAxis(ap=node_idx[:, s, i:i + 1], axis=0)).then_inc(max_got[s], 16)

                pipeline(pool, NSTEP, 2, [(0, gather)])

            @block.scalar
            def _(act):
                def step(r, s):
                    k = r * 2 + s
                    at_least(act, var_made, k + 1)
                    nc.scalar.activation(small[:, 3, :], small[:, 2, :], ACT.Sqrt).then_inc(dev_made, 1)
                    at_least(act, normed_made, NB * (k + 1))
                    at_least(act, table_out[s], 16 * r)
                    nc.scalar.activation(table_rows[:, s, :, :], normed[:, s, :, :], ACT.Relu).then_inc(relu_made, 1)
                    nc.scalar.activation(norm_deg[:, bass.ds(k * NB, NB), 0:C], normed[:, s, :, :], ACT.Relu).then_inc(kept, 1)

                pipeline(act, NSTEP, 2, [(0, step)])

            @block.vector
            def _(dve):
                dve.wait_ge(mid_in, 32)
                join_chain = Chain(dve, sem("join_chain"), 4)
                norm_chain = Chain(dve, sem("norm_chain3"), NORM_LINKS)

                def step(r, s):
                    k = r * 2 + s
                    cols = bass.ds(k * NB, NB)
                    at_least(dve, max_got[s], 16 * NB * (r + 1))
                    join_chain.start(k)
                    join_chain.link(nc.vector.tensor_tensor(with_mid[:, :, :], mid_max[:, :].unsqueeze(1).broadcast_to([P, NB, C]),
                                                            spans_mid[:, cols].unsqueeze(2).broadcast_to([P, NB, C]), ALU.add))
                    nc.vector.tensor_tensor(with_mid[:, :, :], max_in[:, s, :, :], with_mid[:, :, :], ALU.max).then_inc(max_used, 1)
                    at_least(dve, max_used, k + 1)
                    join_chain.link(nc.vector.tensor_tensor(with_mid[:, :, :], with_mid[:, :, :],
                                                            b2_all[:, :].unsqueeze(1).broadcast_to([P, NB, C]), ALU.add))
                    join_chain.link(nc.vector.tensor_tensor(with_mid[:, :, :], with_mid[:, :, :],
                                                            has_edge[:, cols].unsqueeze(2).broadcast_to([P, NB, C]), ALU.mult))
                    join_chain.link(nc.vector.tensor_tensor(nodes[:, cols, :], nodes[:, cols, :], with_mid[:, :, :], ALU.add))
                    join_chain.end()
                    at_least_apart(dve, kept, k - 1, dve_passed)
                    norm_step(norm_chain, k, stats, small, var_made, dev_made, normed_made, lambda i: normed[:, s, i, :])

                pipeline(dve, NSTEP, 2, [(0, step)])

        end_phase()

        keep = stack.enter_context(ExitStack())
        gain = tensor(keep, "gain", [P, 2])
        shift = tensor(keep, "shift", [P, 2])
        w_sum = tensor(keep, "w_sum", [P, HID])
        with ExitStack() as s4:
            U = 8
            H = U // 2
            edge_in = tensor(s4, "edge_in", [P, U, J, C])
            pairs = tensor(s4, "pairs", [P, U, J, 2 * C])
            send_idx = tensor(s4, "send_idx4", [P, 2, H * J], I32)
            pairs_t = tensor(s4, "pairs_t", [P, 2, BLK])
            hid = tensor(s4, "hid", [P, U // 2, 2, BLK])
            stats = tensor(s4, "stats4", [P, NBLK, 6])
            w1a = tensor(s4, "w1a", [P, HID])
            vec = tensor(s4, "vec4", [P, 3])
            sums = tensor(s4, "sums4", [P, 6])
            ps_pairs = [banks(s4, f"ps_pairs{b}", [P, BLK]) for b in range(2)]
            ps_hid = [banks(s4, f"ps_hid{b}", [P, BLK]) for b in range(2)]
            w2a = tensor(s4, "w2a", [P, HID])
            w2a_t = tensor(s4, "w2a_t", [P, HID])
            w1b_low = tensor(s4, "w1b_low", [P, HID])
            w1b_top = tensor(s4, "w1b_top", [C + 1, HID])
            b2a_col = tensor(s4, "b2a_col", [P, C + 1])
            w_norm = tensor(s4, "w_norm", [C + 1, HID])
            b1b_col = tensor(s4, "b1b_col", [P, 1])
            node_in = tensor(s4, "node_in", [P, 2, C + 1])
            node_t = tensor(s4, "node_t", [C + 1, 2, P])
            ps_node_t = banks(s4, "ps_node_t", [P, P])
            ps_node_h = banks(s4, "ps_node_h", [P, P])
            cleared, prep_in, w_turned, w_copied, w_multiplied, w_ready, node_taken, node_turned, node_copied, node_multiplied, node_made = (
                sem(n + "4") for n in ("cleared", "prep_in", "w_turned", "w_copied", "w_multiplied", "w_ready", "node_taken", "node_turned", "node_copied",
                                       "node_multiplied", "node_made"))
            loaded = [sem(f"loaded4_{i}") for i in range(U)]
            gathered = [sem(f"gathered4_{i}") for i in range(U)]
            stored = [sem(f"stored4_{i}") for i in range(U // 2)]
            idx_copied, w_in, turned, copied, multiplied, hid_made, stats_made, root_ready, root_made = (
                sem(n + "4") for n in ("idx_copied", "w_in", "turned", "copied", "multiplied", "hid_made", "stats_made", "root_ready", "root_made"))
            edge_copied = sem("edge_copied")
            pool_passed, dve_passed = sem("pool_passed4"), sem("dve_passed4")
            block = s4.enter_context(nc.Block())

            @block.sync
            def _(sp):
                attr_v = edge_attr[0:LAST_BLK * BLK, :].rearrange("(k p j) c -> p k (j c)", p=P, j=J)
                hid_v = hid_edges.rearrange("k p c -> p k c")
                sp.dma_start(w1a[:, :], W1a).then_inc(w_in, 16)
                with nc.allow_non_contiguous_dma(reason="one element per partition"):
                    for n, v in enumerate((b1a, g1a, be1a)):
                        sp.dma_start(vec[:, n:n + 1], v.rearrange("(p a) -> p a", a=1)).then_inc(w_in, 16)

                sp.dma_start(w2a[:, :], W2a).then_inc(prep_in, 16)
                sp.dma_start(w1b_low[:, :], W1b[C:C + HID, :]).then_inc(prep_in, 16)
                sp.wait_ge(cleared, 2)
                sp.dma_start(w1b_top[0:C, :], W1b[0:C, :]).then_inc(prep_in, 16)
                with nc.allow_non_contiguous_dma(reason="one element per partition"):
                    sp.dma_start(b2a_col[:, C:C + 1], b2a.rearrange("(p a) -> p a", a=1)).then_inc(prep_in, 16)
                    sp.dma_start(b1b_col[:, :], b1b.rearrange("(p a) -> p a", a=1)).then_inc(prep_in, 16)

                def load(r, s):
                    k = r * U + s
                    at_least(sp, edge_copied, k - U + 1)
                    if isinstance(k, int) and k == LAST_BLK:
                        sp.dma_start(edge_in[0:TAIL // J, s, :, :].rearrange("p j c -> p (j c)"), edge_attr[LAST_BLK * BLK:E, :].rearrange("(p j) c -> p (j c)", j=J)).then_inc(loaded[s], 16)
                    else:
                        sp.dma_start(edge_in[:, s, :, :].rearrange("p j c -> p (j c)"), attr_v[:, bass.ds(k, 1), :].rearrange("p a f -> p (a f)")).then_inc(loaded[s], 16)

                def store(r, s):
                    if s % 2 == 0:
                        return
                    at_least(sp, hid_made, r * U + s + 1)
                    sp.dma_start(hid_v[:, bass.ds(r * (U // 2) + s // 2, 1), :].rearrange("p a f -> p (a f)"),
                                 hid[:, s // 2, :, :].rearrange("p b q -> p (b q)")).then_inc(stored[s // 2], 16)

                pipeline(sp, NBLK, U, [(0, load), (5, store)])
                for q in range(U // 2):
                    sp.wait_ge(stored[q], 16 * (NBLK // U))

            @block.gpsimd
            def _(pool):
                def gather(r, s):
                    k = r * U + s
                    if s % H == 0:
                        at_least(pool, idx_copied, r * 2 + s // H + 1)
                    at_least_apart(pool, turned, k - U + 1, pool_passed)
                    for j in range(J):
                        col = (s % H) * J + j
                        pool.indirect_dma_start(out=pairs[:, s, j, 0:C], out_offset=None, in_=norm_table,
                                                in_offset=bass.IndirectOffsetOnAxis(ap=send_idx[:, s // H, col:col + 1], axis=0)
                                                ).then_inc(gathered[s], 16)

                pipeline(pool, NBLK, U, [(0, gather)])

            @block.tensor
            def _(pe):
                def turn(r, s):
                    k = r * U + s
                    at_least(pe, edge_copied, k + 1)
                    at_least(pe, gathered[s], 16 * J * (r + 1))
                    at_least(pe, copied, k - 1)
                    for j in range(J):
                        mm = nc.tensor.transpose(ps_pairs[s % 2][:, j::J], pairs[:, s, j, :], ident[:, :])
                    mm.then_inc(turned, 1)

                def product(r, s):
                    k = r * U + s
                    at_least(pe, copied, k + 1)
                    at_least(pe, hid_made, k - 1)
                    nc.tensor.matmul(ps_hid[s % 2][:, :], w1a[:, :], pairs_t[:, s % 2, :], start=True, stop=True).then_inc(multiplied, 1)

                def turn_node(r, s):
                    if s % NODE_EVERY:
                        return
                    i, q = r * (U // NODE_EVERY) + s // NODE_EVERY, s // NODE_EVERY
                    at_least(pe, node_taken, i + 1)
                    at_least(pe, node_copied, i)
                    nc.tensor.transpose(ps_node_t[0:C + 1, :], node_in[:, q, :], ident[:, :]).then_inc(node_turned, 1)

                def product_node(r, s):
                    if s % NODE_EVERY:
                        return
                    i, q = r * (U // NODE_EVERY) + s // NODE_EVERY, s // NODE_EVERY
                    at_least(pe, node_copied, i + 1)
                    if not (isinstance(i, int) and i > NI):
                        at_least(pe, node_made, i)
                    nc.tensor.matmul(ps_node_h[:, :], w_norm[:, :], node_t[:, q, :], start=True, stop=True).then_inc(node_multiplied, 1)

                pe.wait_ge(prep_in, 16 * 5)
                nc.tensor.transpose(ps_node_t[:, :], w2a[:, :], ident[:, :]).then_inc(w_turned, 1)
                pe.wait_ge(w_copied, 1)
                nc.tensor.matmul(ps_node_h[:, :], w2a_t[:, :], w1b_low[:, :], start=True, stop=True).then_inc(w_multiplied, 1)
                nc.tensor.matmul(ps_node_t[0:C + 1, :], b2a_col[:, :], w1b_low[:, :], start=True, stop=True).then_inc(w_multiplied, 1)
                pe.wait_ge(w_ready, 2)
                pe.wait_ge(w_in, 64)
                pipeline(pe, NBLK, U, [(0, turn), (1, product), (0, turn_node), (NODE_EVERY, product_node)])

            @block.scalar
            def _(act):
                def copy(r, s):
                    k = r * U + s
                    at_least(act, turned, k + 1)
                    at_least(act, multiplied, k - 1)
                    nc.scalar.copy(pairs_t[:, s % 2, :], ps_pairs[s % 2][:, :]).then_inc(copied, 1)

                def copy_edge(r, s):
                    k = r * U + s
                    at_least(act, loaded[s], 16 * (r + 1))
                    at_least(act, turned, k - U + 1)
                    nc.scalar.copy(pairs[:, s, :, C:2 * C], edge_in[:, s, :, :]).then_inc(edge_copied, 1)

                cols = src_cols[:, :, :].rearrange("p k j -> p (k j)")

                def copy_idx(r, s):
                    if s % H == 0:
                        nc.scalar.copy(send_idx[:, s // H, :], cols[:, bass.ds((r * U + s) * J, H * J)]).then_inc(idx_copied, 1)

                def take_node(r, s):
                    if s % NODE_EVERY:
                        return
                    i, q = r * (U // NODE_EVERY) + s // NODE_EVERY, s // NODE_EVERY
                    at_least(act, node_turned, i - 1)
                    nc.scalar.copy(node_in[:, q, :], norm_deg[:, bass.ds(i, 1), :].rearrange("p a c -> p (a c)")).then_inc(node_taken, 1)

                def copy_node(r, s):
                    if s % NODE_EVERY:
                        return
                    i, q = r * (U // NODE_EVERY) + s // NODE_EVERY, s // NODE_EVERY
                    at_least(act, node_turned, i + 1)
                    at_least(act, node_multiplied, i - 1)
                    nc.scalar.copy(node_t[:, q, :], ps_node_t[0:C + 1, :]).then_inc(node_copied, 1)

                def bias_node(r, s):
                    if s % NODE_EVERY:
                        return
                    i = r * (U // NODE_EVERY) + s // NODE_EVERY
                    at_least(act, node_multiplied, i + 1)
                    if isinstance(i, int) and i >= NI:
                        return
                    nc.scalar.activation(hid2[:, bass.ds(i * P, P)], ps_node_h[:, :], ACT.Identity, bias=b1b_col[:, 0:1]).then_inc(node_made, 1)

                def prepare():
                    act.wait_ge(w_turned, 1)
                    nc.scalar.copy(w2a_t[:, :], ps_node_t[:, :]).then_inc(w_copied, 1)
                    act.wait_ge(w_multiplied, 2)
                    nc.scalar.copy(w_sum[:, :], ps_node_h[:, :]).then_inc(w_ready, 1)

                def copy_idx_first(r, s):
                    copy_idx(r, s)
                    if isinstance(r, int) and r == 0 and s == H:
                        prepare()

                pipeline(act, NBLK, U, [(0, copy_idx_first), (0, take_node), (H - 1, copy_edge), (H, copy), (H, copy_node), (U, bias_node)])
                act.wait_ge(root_ready, 1)
                nc.scalar.activation(sums[:, 3:4], sums[:, 2:3], ACT.Sqrt).then_inc(root_made, 1)

            @block.vector
            def _(dve):
                def finish(r, s):
                    k = r * U + s
                    at_least(dve, multiplied, k + 1)
                    at_least(dve, stored[s // 2], 16 * r)
                    part = hid[:, s // 2, s % 2, :]
                    nc.vector.tensor_scalar(part, ps_hid[s % 2][:, :], vec[:, 0:1], None, ALU.add).then_inc(hid_made, 1)
                    at_least_apart(dve, hid_made, k + 1, dve_passed)
                    valid = TAIL if isinstance(k, int) and k == LAST_BLK else BLK
                    nc.vector.bn_stats(stats[:, bass.ds(k, 1), :].rearrange("p a q -> p (a q)"), part[:, 0:valid]).then_inc(stats_made, 1)

                nc.vector.memset(w1b_top[:, :], 0.0).then_inc(cleared, 1)
                nc.vector.memset(b2a_col[:, :], 0.0).then_inc(cleared, 1)
                dve.wait_ge(w_multiplied, 2)
                nc.vector.tensor_tensor(w_norm[:, :], ps_node_t[0:C + 1, :], w1b_top[:, :], ALU.add).then_inc(w_ready, 1)
                dve.wait_ge(w_in, 64)
                pipeline(dve, NBLK, U, [(0, finish)])
                dve.wait_ge(stats_made, NBLK)
                affine_of_norm(Chain(dve, sem("affine4")), root_ready, root_made, stats[:, :, :].rearrange("p k q -> p (k q)"),
                               sums, gain[:, 0:1], shift[:, 0:1], vec[:, 1:2], vec[:, 2:3])

        end_phase()

        with ExitStack() as s5:
            U = 8
            R = 4
            JS = STEP // P
            STEPS = EP // STEP
            hid = tensor(s5, "hid5", [P, U, STEP])
            mask_in = tensor(s5, "mask_in5", [1, R, STEP], BF16)
            ones5 = tensor(s5, "ones5", [1, P], BF16)
            act_out = tensor(s5, "act_out", [P, 2, STEP])
            total = tensor(s5, "total", [P, 2, STEP])
            rows = tensor(s5, "rows5", [P, R, JS * HID])
            ps_mask = [banks(s5, f"ps_mask5_{b}", [P, STEP]) for b in range(2)]
            ps_back = [banks(s5, f"ps_back5_{b}", [P, JS * HID]) for b in range(2)]
            loaded = [sem(f"loaded5_{i}") for i in range(U)]
            stored = [sem(f"stored5_{i}") for i in range(R)]
            begun, mask_spread, relu_done, sum_done, back_turned, rows_made = (
                sem(n + "5") for n in ("begun", "mask_spread", "relu_done", "sum_done", "back_turned", "rows_made"))
            steps_out, sums_got, pool_passed = sem("steps_out"), sem("sums_got"), sem("pool_passed5")
            block = s5.enter_context(nc.Block())

            @block.sync
            def _(sp):
                hid_v = hid_edges.rearrange("k p c -> p k c")
                mask_v = same_sum.rearrange("(a k c) -> a k c", a=1, k=STEPS)
                sum_v = sum_edges.rearrange("(k p j) c -> p k (j c)", p=P, j=JS)

                def load(r, s):
                    k = r * U + s
                    at_least(sp, relu_done, k - U + 1)
                    sp.dma_start(hid[:, s, :], hid_v[:, bass.ds(k, 1), :].rearrange("p a f -> p (a f)")).then_inc(loaded[s], 16)
                    at_least(sp, mask_spread, k - R + 1)
                    sp.dma_start(mask_in[:, s % R, :], mask_v[:, bass.ds(k, 1), :].rearrange("t a c -> t (a c)")).then_inc(loaded[s], 16)

                def confirm(r, s):
                    sp.wait_ge(stored[s % R], 16 * (r * (U // R) + s // R + 1))
                    sp.sem_inc(steps_out, 1)

                def store(r, s):
                    k = r * U + s
                    at_least(sp, rows_made, k + 1)
                    sp.dma_start(sum_v[:, bass.ds(k, 1), :].rearrange("p a f -> p (a f)"), rows[:, s % R, :]).then_inc(stored[s % R], 16)

                pipeline(sp, STEPS, U, [(0, load), (5, store), (U, confirm)])

            @block.gpsimd
            def _(pool):
                for i in range(NI):
                    needed = pool.value_load(steps_needed[0:1, i:i + 1], min_val=1, max_val=STEPS)
                    pool.wait_ge(steps_out, needed)
                    pool.sem_inc(pool_passed, 1)
                    pool.indirect_dma_start(out=sum_in[:, i, :], out_offset=None, in_=sum_edges,
                                            in_offset=bass.IndirectOffsetOnAxis(ap=end_idx[:, i:i + 1], axis=0)).then_inc(sums_got, 16)
                pool.wait_ge(sums_got, 16 * NI)

            @block.tensor
            def _(pe):
                def spread(r, s):
                    k = r * U + s
                    at_least(pe, loaded[s], 32 * (r + 1))
                    at_least(pe, sum_done, k - 1)
                    for a in range(0, STEP, BLK):
                        mm = nc.tensor.matmul(ps_mask[s % 2][:, a:a + BLK], ones5[:, :], mask_in[:, s % R, a:a + BLK], start=True, stop=True)
                    mm.then_inc(mask_spread, 1)

                def turn_back(r, s):
                    k = r * U + s
                    at_least(pe, sum_done, k + 1)
                    at_least(pe, rows_made, k - 1)
                    for j in range(JS):
                        mm = nc.tensor.transpose(ps_back[s % 2][:, j * P:(j + 1) * P], total[:, s % 2, j::JS], ident[:, :])
                    mm.then_inc(back_turned, 1)

                pe.wait_ge(begun, 2)
                pipeline(pe, STEPS, U, [(0, spread), (1, turn_back)])

            @block.scalar
            def _(act):
                def relu(r, s):
                    k = r * U + s
                    at_least(act, loaded[s], 32 * (r + 1))
                    at_least(act, sum_done, k - 1)
                    nc.scalar.activation(act_out[:, s % 2, :], hid[:, s, :], ACT.Relu, bias=shift[:, 0:1], scale=gain[:, 0:1]).then_inc(relu_done, 1)

                def rows_out(r, s):
                    k = r * U + s
                    at_least(act, back_turned, k + 1)
                    at_least(act, stored[s % R], 16 * (r * (U // R) + s // R))
                    nc.scalar.copy(rows[:, s % R, :], ps_back[s % 2][:, :]).then_inc(rows_made, 1)

                pipeline(act, STEPS, U, [(0, relu), (1, rows_out)])

            @block.vector
            def _(dve):
                nc.vector.memset(total[:, 1, STEP - 1:STEP], 0.0).then_inc(begun, 1)
                nc.vector.memset(ones5[:, :], 1.0).then_inc(begun, 1)
                dve.wait_ge(begun, 2)

                def running_sum(r, s):
                    k = r * U + s
                    at_least(dve, mask_spread, k + 1)
                    at_least(dve, relu_done, k + 1)
                    at_least(dve, back_turned, k - 1)
                    at_least(dve, sum_done, k)
                    nc.vector.tensor_tensor_scan(total[:, s % 2, :], ps_mask[s % 2][:, :], act_out[:, s % 2, :],
                                                 total[:, 1 - s % 2, STEP - 1:STEP], ALU.mult, ALU.add).then_inc(sum_done, 1)

                pipeline(dve, STEPS, U, [(0, running_sum)])

        end_phase()

        with ExitStack() as s6:
            NC = 5
            STEPS = NI // NC
            assert N // (NC * P) == STEPS - 1 and N - (STEPS - 1) * NC * P > NC * P // 2
            sum_kept = tensor(s6, "sum_kept", [P, 2, NC, HID])
            sum_t = tensor(s6, "sum_t", [P, 2, NC * P])
            stats = tensor(s6, "stats6", [P, 2 * STEPS, 6])
            vec = tensor(s6, "vec6", [P, 2])
            b2b_all = tensor(s6, "b2b_all", [P, C])
            w2b = tensor(s6, "w2b", [P, C])
            sums = tensor(s6, "sums6", [P, 6])
            Q = 4
            active = tensor(s6, "active", [P, Q, NC, P])
            partial = tensor(s6, "partial", [P, Q, NC, C])
            result = tensor(s6, "result", [P, Q, NC, C])
            ps_turned = [banks(s6, f"ps_turned{b}", [P, 8 * P]) for b in range(2)]
            ps_hid = [banks(s6, f"ps_hid6_{b}", [P, 8 * P]) for b in range(2)]
            ps_out = [b[:, h:h + 512].rearrange("p (i c) -> p i c", c=C) for b in ps_turned for h in (0, 512)]
            out_done = [sem(f"out_done{i}") for i in range(Q)]
            (w_in, sum_scaled, sums_turned, sum_copied, multiplied, hid_made, stats_made, root_ready, root_made, affine_ready,
             relu_done, out_multiplied, partial_made, result_made) = (
                sem(n + "6") for n in ("w_in", "sum_scaled", "sums_turned", "sum_copied", "multiplied", "hid_made", "stats_made",
                                       "root_ready", "root_made", "affine_ready", "relu_done", "out_multiplied", "partial_made",
                                       "result_made"))
            pool_passed, dve_passed = sem("pool_passed6"), sem("dve_passed6")
            block = s6.enter_context(nc.Block())

            @block.sync
            def _(sp):
                sp.dma_start(w2b[:, :], W2b).then_inc(w_in, 16)
                sp.dma_start(b2b_all[:, :], b2b.partition_broadcast(P)).then_inc(w_in, 16)
                with nc.allow_non_contiguous_dma(reason="one element per partition"):
                    for n, v in enumerate((g1b, be1b)):
                        sp.dma_start(vec[:, n:n + 1], v.rearrange("(p a) -> p a", a=1)).then_inc(w_in, 16)
                full = N // (NC * P)
                rest = (N - full * NC * P) // P
                out_v = out[0:full * NC * P, :].rearrange("(i p) c -> p i c", p=P)

                def store(r, s):
                    k = r * Q + s
                    at_least(sp, result_made, k + 1)
                    if isinstance(k, int) and k == full:
                        sp.dma_start(out[full * NC * P:FULL_NI * P, :].rearrange("(i p) c -> p i c", p=P), result[:, s, 0:rest, :]).then_inc(out_done[s], 16)
                        sp.dma_start(out[FULL_NI * P:N, :], result[0:REST, s, rest, :]).then_inc(out_done[s], 16)
                    else:
                        sp.dma_start(out_v[:, bass.ds(k * NC, NC), :], result[:, s, :, :]).then_inc(out_done[s], 16)

                pipeline(sp, STEPS, Q, [(0, store)])
                for s in range(Q):
                    sp.wait_ge(out_done[s], 16 * (STEPS // Q + (s == full % Q)))

            @block.gpsimd
            def _(pool):
                def scale(r, s):
                    k = r * 2 + s
                    at_least_apart(pool, sums_turned, k - 1, pool_passed)
                    nc.gpsimd.tensor_tensor(sum_kept[:, s, :, :], sum_in[:, bass.ds(k * NC, NC), :],
                                            has_edge[:, bass.ds(k * NC, NC)].unsqueeze(2).broadcast_to([P, NC, HID]), ALU.mult).then_inc(sum_scaled, 1)

                pipeline(pool, STEPS, 2, [(0, scale)])

            @block.tensor
            def _(pe):
                def turn(r, s):
                    k = r * 2 + s
                    at_least(pe, sum_scaled, k + 1)
                    at_least(pe, sum_copied, k - 1)
                    for i in range(NC):
                        mm = nc.tensor.transpose(ps_turned[s][:, i * P:(i + 1) * P], sum_kept[:, s, i, :], ident[:, :])
                    mm.then_inc(sums_turned, 1)

                def product(r, s):
                    k = r * 2 + s
                    at_least(pe, sum_copied, k + 1)
                    at_least(pe, hid_made, k - 1)
                    for a, b in ((0, 512), (512, NC * P)):
                        mm = nc.tensor.matmul(ps_hid[s][:, a:b], w_sum[:, :], sum_t[:, s, a:b], start=True, stop=True)
                    mm.then_inc(multiplied, 1)

                pipeline(pe, STEPS, 2, [(0, turn), (1, product)])
                pe.wait_ge(w_in, 16 * 4)

                def last_product(r, s):
                    k = r * Q + s
                    at_least(pe, relu_done, k + 1)
                    at_least(pe, partial_made, k - Q + 1)
                    for i in range(NC):
                        mm = nc.tensor.matmul(ps_out[s][:, i, :], active[:, s, i, :], w2b[:, :], start=True, stop=True)
                    mm.then_inc(out_multiplied, 1)

                pipeline(pe, STEPS, Q, [(0, last_product)])

            @block.scalar
            def _(act):
                def copy_sum(r, s):
                    k = r * 2 + s
                    at_least(act, sums_turned, k + 1)
                    at_least(act, multiplied, k - 1)
                    nc.scalar.copy(sum_t[:, s, :], ps_turned[s][:, 0:NC * P]).then_inc(sum_copied, 1)

                pipeline(act, STEPS, 2, [(0, copy_sum)])
                act.wait_ge(root_ready, 1)
                nc.scalar.activation(sums[:, 3:4], sums[:, 2:3], ACT.Sqrt).then_inc(root_made, 1)
                act.wait_ge(affine_ready, 1)

                def relu(r, s):
                    k = r * Q + s
                    at_least(act, out_multiplied, k - Q + 1)
                    nc.scalar.activation(active[:, s, :, :].rearrange("p i q -> p (i q)"), hid2[:, bass.ds(k * NC * P, NC * P)], ACT.Relu,
                                         bias=shift[:, 1:2], scale=gain[:, 1:2]).then_inc(relu_done, 1)

                pipeline(act, STEPS, Q, [(0, relu)])

            @block.vector
            def _(dve):
                def finish(r, s):
                    k = r * 2 + s
                    at_least(dve, multiplied, k + 1)
                    part = hid2[:, bass.ds(k * NC * P, NC * P)]
                    nc.vector.tensor_tensor(part, ps_hid[s][:, 0:NC * P], part, ALU.add).then_inc(hid_made, 1)
                    at_least_apart(dve, hid_made, k + 1, dve_passed)
                    valid = N - (STEPS - 1) * NC * P if isinstance(k, int) and k == STEPS - 1 else NC * P
                    half = NC * P // 2
                    nc.vector.bn_stats(stats[:, bass.ds(2 * k, 1), :].rearrange("p a q -> p (a q)"), part[:, 0:half]).then_inc(stats_made, 1)
                    nc.vector.bn_stats(stats[:, bass.ds(2 * k + 1, 1), :].rearrange("p a q -> p (a q)"), part[:, half:valid]).then_inc(stats_made, 1)

                pipeline(dve, STEPS, 2, [(0, finish)])
                dve.wait_ge(w_in, 16 * 4)
                dve.wait_ge(stats_made, 2 * STEPS)
                affine_of_norm(Chain(dve, sem("affine6")), root_ready, root_made, stats[:, :, :].rearrange("p k q -> p (k q)"),
                               sums, gain[:, 1:2], shift[:, 1:2], vec[:, 0:1], vec[:, 1:2])
                nc.vector.memset(sums[:, 5:6], 0.0).then_inc(affine_ready, 1)

                def partial_step(r, s):
                    k = r * Q + s
                    at_least(dve, out_multiplied, k + 1)
                    at_least(dve, result_made, k - Q + 1)
                    nc.vector.tensor_tensor(partial[:, s, :, :], ps_out[s][:, 0:NC, :], nodes[:, bass.ds(k * NC, NC), :], ALU.add).then_inc(partial_made, 1)

                def result_step(r, s):
                    k = r * Q + s
                    at_least(dve, partial_made, k + 1)
                    at_least(dve, out_done[s], 16 * r)
                    nc.vector.tensor_tensor(result[:, s, :, :], partial[:, s, :, :],
                                            b2b_all[:, :].unsqueeze(1).broadcast_to([P, NC, C]), ALU.add).then_inc(result_made, 1)

                pipeline(dve, STEPS, Q, [(0, partial_step), (1, result_step)])


_INS = ["x", "src", "dst", "edge_attr_64", "L0_gnn_W1", "L0_gnn_b1", "L0_gnn_W2", "L0_gnn_b2", "L1_gnn_W1a", "L1_gnn_b1a",
        "L1_gnn_g1a", "L1_gnn_be1a", "L1_gnn_W2a", "L1_gnn_b2a", "L1_gnn_W1b", "L1_gnn_b1b", "L1_gnn_g1b", "L1_gnn_be1b",
        "L1_gnn_W2b", "L1_gnn_b2b"]


_OUTS = [((12500, 64), "float32")]


def kernel(**inputs):
    import numpy as _np
    import concourse.bacc as _bacc
    from concourse import mybir as _mybir
    from concourse.bass_utils import run_bass_kernel_spmd as _run

    nc = _bacc.Bacc("TRN2", target_bir_lowering=False, num_devices=1)
    arrays, args = {}, []
    for name in _INS:
        a = _np.ascontiguousarray(inputs[name])
        arrays[f"in_{name}_dram"] = a
        args.append(nc.dram_tensor(f"in_{name}_dram", a.shape, _mybir.dt.from_np(a.dtype), kind="ExternalInput").ap())
    for i, (shape, dtype) in enumerate(_OUTS):
        dt = _mybir.dt.from_np(_np.dtype(dtype))
        args.append(nc.dram_tensor(f"out_{i}_dram", shape, dt, kind="ExternalOutput").ap())
    gnn_kernel(nc, *args)
    r = _run(nc, [arrays], core_ids=[0])
    got = tuple(r.results[0][f"out_{i}_dram"] for i in range(len(_OUTS)))
    return got[0]
```
